# Optimizing a Trainium2 kernel written in Bass

```python
import numpy as np
import jax
import jax.numpy as jnp

def _softmax(x, axis=-1):
    return jax.nn.softmax(x, axis=axis)

def _gelu(x):
    return jax.nn.gelu(x, approximate=True)

def _silu(x):
    return jax.nn.silu(x)

def _sigmoid(x):
    return jax.nn.sigmoid(x)

def _layernorm(x, axis=-1, eps=1e-05):
    m = jnp.mean(x, axis=axis, keepdims=True)
    v = jnp.var(x, axis=axis, keepdims=True)
    return (x - m) / jnp.sqrt(v + eps)

def _scatter_add(tgt, idx, src, axis=0):
    return tgt.at[idx].add(src)

def _segment_sum(src, seg, n):
    return jax.ops.segment_sum(src, seg, n)
kernel_name = 'mk_xattn_seq_d2_seqx_r4_645bae'

def setup_inputs(seed: int=0):
    np.random.seed(seed)
    _w = jnp.asarray

    def _rec_inputs():
        import jax
        import jax.numpy as jnp
        _rk = jax.random.key(seed)
        x = -0.000125 + 0.9999 * jax.random.normal(jax.random.fold_in(_rk, 1), (16, 256, 512), jnp.float32)
        _lenS = 256 - jax.random.randint(jax.random.fold_in(_rk, 7), (16,), 0, max(1, 256 // 4) + 1, jnp.int32)
        _lenS2 = 256 - jax.random.randint(jax.random.fold_in(_rk, 8), (16,), 0, max(1, 256 // 4) + 1, jnp.int32)
        _ctx_1024P = jax.random.normal(jax.random.fold_in(_rk, 11), (16, 16, 256), jnp.float32)
        _ctx_1024c = jax.random.dirichlet(jax.random.fold_in(_rk, 511), 0.3 * jnp.ones((16,), jnp.float32), (16, 256))
        _ctx_1024t = jnp.einsum('bsk,bkd->bsd', _ctx_1024c, _ctx_1024P)
        _ctx_1024t = _ctx_1024t * jax.lax.rsqrt(jnp.mean(jnp.square(_ctx_1024t)) + 1e-12) * 0.953939
        ctx_1024 = 4.13588e-05 + 0.999923 * (_ctx_1024t + 0.3 * jax.random.normal(jax.random.fold_in(_rk, 611), (16, 256, 256), jnp.float32))
        pos_1xS = jnp.broadcast_to(jnp.arange(256, dtype=jnp.int32), (1, 256))
        _validS = jnp.arange(256)[None, :] < _lenS[:, None]
        _validS2 = jnp.arange(256)[None, :] < _lenS2[:, None]
        _causal = jnp.tril(jnp.ones((256, 256), dtype=bool))
        mask_BxS_ik0 = jnp.where(jnp.broadcast_to(_validS[:, :], (16, 256)), 0, 1).astype(jnp.int32)
        return (x, ctx_1024, pos_1xS, mask_BxS_ik0)
    x, ctx_1024, pos_1xS, mask_BxS_ik0 = _rec_inputs()

    def _L0_xattn_setup():
        import jax, jax.numpy as jnp
        import numpy as np
        EPS = 1e-06

        def _rmsnorm(x, w):
            var = jnp.mean(jnp.square(x), axis=-1, keepdims=True)
            return x * jax.lax.rsqrt(var + EPS) * w
        key = jax.random.key(seed)
        ks = jax.random.split(key, 6)
        B, N, M = (4, 1024, 512)
        d_model, memory_dim = (512, 256)
        hidden_states = jax.random.normal(ks[0], (B, N, d_model), dtype=jnp.float32)
        memory = jax.random.normal(ks[1], (B, M, memory_dim), dtype=jnp.float32)
        W_mem = jax.random.normal(ks[2], (d_model, memory_dim), dtype=jnp.float32) / np.sqrt(memory_dim)
        W_gate = jax.random.normal(ks[3], (d_model, 2 * d_model), dtype=jnp.float32) / np.sqrt(2 * d_model)
        b_gate = jax.random.normal(ks[4], (d_model,), dtype=jnp.float32) * 0.01
        norm_w = jnp.ones((d_model,), dtype=jnp.float32)
        return {'hidden_states': hidden_states, 'memory': memory, 'W_mem': W_mem, 'W_gate': W_gate, 'b_gate': b_gate, 'norm_w': norm_w}
    _L0_xattn_all = _L0_xattn_setup()
    _L0_xattn_in = {k: v for k, v in _L0_xattn_all.items() if k in ('W_mem', 'W_gate', 'b_gate', 'norm_w')}
    del _L0_xattn_all

    def _L1_xattn_setup():
        import jax, jax.numpy as jnp
        import numpy as np
        H = 512
        NH = 16
        HD = H // NH
        CH = 256
        CC = 256
        CHD = CC // NH
        I = 1376
        B = 2
        L = 512
        LE = 256
        EPS = 1e-06

        def rms_norm(x, w):
            xf = x.astype(jnp.float32)
            var = jnp.mean(xf * xf, axis=-1, keepdims=True)
            return (w * (xf * jax.lax.rsqrt(var + EPS))).astype(x.dtype)

        def expert_mask(tt):
            vm = jnp.zeros(tt.shape, dtype=bool)
            vm = vm.at[:, :-1].set((tt[:, :-1] == 1) & (tt[:, 1:] == 1))
            return vm

        def rotate_half(x):
            d = x.shape[-1] // 2
            return jnp.concatenate([-x[..., d:], x[..., :d]], axis=-1)

        def apply_rotary(q, k, position_ids, seq_len):
            inv = 1.0 / 10000.0 ** (jnp.arange(0, HD, 2, dtype=jnp.float32) / HD)
            t = jnp.arange(seq_len, dtype=jnp.float32)
            freqs = jnp.outer(t, inv)
            emb = jnp.concatenate([freqs, freqs], axis=-1)
            cos = jnp.cos(emb)[position_ids][:, None].astype(q.dtype)
            sin = jnp.sin(emb)[position_ids][:, None].astype(q.dtype)
            return (q * cos + rotate_half(q) * sin, k * cos + rotate_half(k) * sin)

        def sdpa(q, k, v, causal):
            scale = 1.0 / np.sqrt(q.shape[-1])
            scores = jnp.einsum('bhqd,bhkd->bhqk', q * scale, k)
            if causal:
                mask = jnp.tril(jnp.ones((q.shape[-2], k.shape[-2]), dtype=bool))
                scores = jnp.where(mask, scores, jnp.finfo(jnp.float32).min)
            p = jax.nn.softmax(scores.astype(jnp.float32), axis=-1).astype(q.dtype)
            return jnp.einsum('bhqk,bhkd->bhqd', p, v)

        def heads(x, nh, hd):
            b, l, _ = x.shape
            return x.reshape(b, l, nh, hd).transpose(0, 2, 1, 3)
        key = jax.random.key(seed)
        ks = jax.random.split(key, 20)
        s = 0.02
        f32 = jnp.float32
        return {'hidden_states': jax.random.normal(ks[0], (B, L, H), f32), 'encoder_outputs': jax.random.normal(ks[1], (B, LE, CH), f32), 'token_type_ids': jax.random.randint(ks[2], (B, L), 0, 2, jnp.int32), 'position_ids': jnp.arange(L, dtype=jnp.int32)[None, :], 'ln_in_w': jnp.ones((H,), f32), 'ln_post_attn_w': jnp.ones((H,), f32), 'ln_post_cross_w': jnp.ones((H,), f32), 'v_qkv': jax.random.normal(ks[3], (H, 3 * H), f32) * s, 'l_qkv': jax.random.normal(ks[4], (H, 3 * H), f32) * s, 'v_dense': jax.random.normal(ks[5], (H, H), f32) * s, 'l_dense': jax.random.normal(ks[6], (H, H), f32) * s, 'cq_w': jax.random.normal(ks[7], (H, CC), f32) * s, 'ckv_w': jax.random.normal(ks[8], (CH, 2 * CC), f32) * s, 'cdense_w': jax.random.normal(ks[9], (CC, H), f32) * s, 'v_gate': jax.random.normal(ks[10], (H, I), f32) * s, 'v_up': jax.random.normal(ks[11], (H, I), f32) * s, 'v_down': jax.random.normal(ks[12], (I, H), f32) * s, 'l_gate': jax.random.normal(ks[13], (H, I), f32) * s, 'l_up': jax.random.normal(ks[14], (H, I), f32) * s, 'l_down': jax.random.normal(ks[15], (I, H), f32) * s}
    _L1_xattn_all = _L1_xattn_setup()
    _L1_xattn_in = {k: v for k, v in _L1_xattn_all.items() if k in ('ln_in_w', 'ln_post_attn_w', 'ln_post_cross_w', 'v_qkv', 'l_qkv', 'v_dense', 'l_dense', 'cq_w', 'ckv_w', 'cdense_w', 'v_gate', 'v_up', 'v_down', 'l_gate', 'l_up', 'l_down')}
    del _L1_xattn_all
    return {'x': x, 'ctx_1024': ctx_1024, 'pos_1xS': pos_1xS, 'mask_BxS_ik0': mask_BxS_ik0, 'L0_xattn_W_mem': _L0_xattn_in['W_mem'], 'L0_xattn_W_gate': _L0_xattn_in['W_gate'], 'L0_xattn_b_gate': _L0_xattn_in['b_gate'], 'L0_xattn_norm_w': _L0_xattn_in['norm_w'], 'L1_xattn_ln_in_w': _L1_xattn_in['ln_in_w'], 'L1_xattn_ln_post_attn_w': _L1_xattn_in['ln_post_attn_w'], 'L1_xattn_ln_post_cross_w': _L1_xattn_in['ln_post_cross_w'], 'L1_xattn_v_qkv': _L1_xattn_in['v_qkv'], 'L1_xattn_l_qkv': _L1_xattn_in['l_qkv'], 'L1_xattn_v_dense': _L1_xattn_in['v_dense'], 'L1_xattn_l_dense': _L1_xattn_in['l_dense'], 'L1_xattn_cq_w': _L1_xattn_in['cq_w'], 'L1_xattn_ckv_w': _L1_xattn_in['ckv_w'], 'L1_xattn_cdense_w': _L1_xattn_in['cdense_w'], 'L1_xattn_v_gate': _L1_xattn_in['v_gate'], 'L1_xattn_v_up': _L1_xattn_in['v_up'], 'L1_xattn_v_down': _L1_xattn_in['v_down'], 'L1_xattn_l_gate': _L1_xattn_in['l_gate'], 'L1_xattn_l_up': _L1_xattn_in['l_up'], 'L1_xattn_l_down': _L1_xattn_in['l_down']}

def reference(x, ctx_1024, pos_1xS, mask_BxS_ik0, L0_xattn_W_mem, L0_xattn_W_gate, L0_xattn_b_gate, L0_xattn_norm_w, L1_xattn_ln_in_w, L1_xattn_ln_post_attn_w, L1_xattn_ln_post_cross_w, L1_xattn_v_qkv, L1_xattn_l_qkv, L1_xattn_v_dense, L1_xattn_l_dense, L1_xattn_cq_w, L1_xattn_ckv_w, L1_xattn_cdense_w, L1_xattn_v_gate, L1_xattn_v_up, L1_xattn_v_down, L1_xattn_l_gate, L1_xattn_l_up, L1_xattn_l_down):
    import jax
    import jax.numpy as jnp

    def _L0_xattn_ref(hidden_states, memory, W_mem, W_gate, b_gate, norm_w):
        import jax, jax.numpy as jnp
        import numpy as np
        EPS = 1e-06

        def _rmsnorm(x, w):
            var = jnp.mean(jnp.square(x), axis=-1, keepdims=True)
            return x * jax.lax.rsqrt(var + EPS) * w
        D = hidden_states.shape[-1]
        memory_proj = jnp.einsum('bme,de->bmd', memory, W_mem)
        scores = jnp.einsum('bnd,bmd->bnm', hidden_states, memory_proj) / jnp.sqrt(jnp.float32(D))
        attn = jax.nn.softmax(scores, axis=-1)
        memory_context = jnp.einsum('bnm,bmd->bnd', attn, memory_proj)
        gate_input = jnp.concatenate([hidden_states, memory_context], axis=-1)
        gate = jax.nn.sigmoid(jnp.einsum('bnf,df->bnd', gate_input, W_gate) + b_gate)
        fused = hidden_states + gate * memory_context
        return _rmsnorm(fused, norm_w)

    def _L1_xattn_ref(hidden_states, encoder_outputs, token_type_ids, position_ids, ln_in_w, ln_post_attn_w, ln_post_cross_w, v_qkv, l_qkv, v_dense, l_dense, cq_w, ckv_w, cdense_w, v_gate, v_up, v_down, l_gate, l_up, l_down):
        import jax, jax.numpy as jnp
        import numpy as np
        H = 512
        NH = 16
        HD = H // NH
        CH = 256
        CC = 256
        CHD = CC // NH
        I = 1376
        B = 2
        L = 512
        LE = 256
        EPS = 1e-06

        def rms_norm(x, w):
            xf = x.astype(jnp.float32)
            var = jnp.mean(xf * xf, axis=-1, keepdims=True)
            return (w * (xf * jax.lax.rsqrt(var + EPS))).astype(x.dtype)

        def expert_mask(tt):
            vm = jnp.zeros(tt.shape, dtype=bool)
            vm = vm.at[:, :-1].set((tt[:, :-1] == 1) & (tt[:, 1:] == 1))
            return vm

        def rotate_half(x):
            d = x.shape[-1] // 2
            return jnp.concatenate([-x[..., d:], x[..., :d]], axis=-1)

        def apply_rotary(q, k, position_ids, seq_len):
            inv = 1.0 / 10000.0 ** (jnp.arange(0, HD, 2, dtype=jnp.float32) / HD)
            t = jnp.arange(seq_len, dtype=jnp.float32)
            freqs = jnp.outer(t, inv)
            emb = jnp.concatenate([freqs, freqs], axis=-1)
            cos = jnp.cos(emb)[position_ids][:, None].astype(q.dtype)
            sin = jnp.sin(emb)[position_ids][:, None].astype(q.dtype)
            return (q * cos + rotate_half(q) * sin, k * cos + rotate_half(k) * sin)

        def sdpa(q, k, v, causal):
            scale = 1.0 / np.sqrt(q.shape[-1])
            scores = jnp.einsum('bhqd,bhkd->bhqk', q * scale, k)
            if causal:
                mask = jnp.tril(jnp.ones((q.shape[-2], k.shape[-2]), dtype=bool))
                scores = jnp.where(mask, scores, jnp.finfo(jnp.float32).min)
            p = jax.nn.softmax(scores.astype(jnp.float32), axis=-1).astype(q.dtype)
            return jnp.einsum('bhqk,bhkd->bhqd', p, v)

        def heads(x, nh, hd):
            b, l, _ = x.shape
            return x.reshape(b, l, nh, hd).transpose(0, 2, 1, 3)
        b, l, _ = hidden_states.shape
        vm = expert_mask(token_type_ids)[..., None]
        residual = hidden_states
        x = rms_norm(hidden_states, ln_in_w)
        mixed = jnp.where(vm, x @ v_qkv, x @ l_qkv)
        q, k, v = jnp.split(mixed, 3, axis=-1)
        q, k, v = (heads(q, NH, HD), heads(k, NH, HD), heads(v, NH, HD))
        q, k = apply_rotary(q, k, position_ids, l)
        ctx = sdpa(q, k, v, causal=True)
        ctx = ctx.transpose(0, 2, 1, 3).reshape(b, l, H)
        attn_out = jnp.where(vm, ctx @ v_dense, ctx @ l_dense)
        hidden_states = residual + attn_out
        ci = rms_norm(hidden_states, ln_post_cross_w)
        cq = heads(ci @ cq_w, NH, CHD)
        ckv = encoder_outputs @ ckv_w
        ck, cv = jnp.split(ckv, 2, axis=-1)
        ck, cv = (heads(ck, NH, CHD), heads(cv, NH, CHD))
        cctx = sdpa(cq, ck, cv, causal=False)
        cctx = cctx.transpose(0, 2, 1, 3).reshape(b, l, CC)
        hidden_states = hidden_states + cctx @ cdense_w
        mi = rms_norm(hidden_states, ln_post_attn_w)
        v_out = jax.nn.silu(mi @ v_gate) * (mi @ v_up) @ v_down
        l_out = jax.nn.silu(mi @ l_gate) * (mi @ l_up) @ l_down
        hidden_states = hidden_states + jnp.where(vm, v_out, l_out)
        return hidden_states
    x = _L0_xattn_ref(x, ctx_1024, L0_xattn_W_mem, L0_xattn_W_gate, L0_xattn_b_gate, L0_xattn_norm_w)
    x = _L1_xattn_ref(x, ctx_1024, mask_BxS_ik0, pos_1xS, L1_xattn_ln_in_w, L1_xattn_ln_post_attn_w, L1_xattn_ln_post_cross_w, L1_xattn_v_qkv, L1_xattn_l_qkv, L1_xattn_v_dense, L1_xattn_l_dense, L1_xattn_cq_w, L1_xattn_ckv_w, L1_xattn_cdense_w, L1_xattn_v_gate, L1_xattn_v_up, L1_xattn_v_down, L1_xattn_l_gate, L1_xattn_l_up, L1_xattn_l_down)
    return x

_drawn_inputs = setup_inputs


def setup_inputs(seed=0):
    import zlib

    import numpy as np

    out = dict(_drawn_inputs(seed))
    spreads = {'L0_xattn_norm_w': (1.0, 0.2),
     'L1_xattn_ln_in_w': (1.0, 0.6),
     'L1_xattn_ln_post_attn_w': (1.0, 0.6),
     'L1_xattn_ln_post_cross_w': (1.0, 0.6)}
    factors = {'L0_xattn_b_gate': 8.0,
     'L1_xattn_v_qkv': 8.0,
     'L1_xattn_v_dense': 3.559,
     'L1_xattn_cq_w': 35.288,
     'L1_xattn_v_gate': 3.108,
     'L1_xattn_v_up': 3.004,
     'L1_xattn_v_down': 3.009}
    for name, (base, spread) in spreads.items():
        noise = np.random.default_rng([zlib.crc32(name.encode()), seed]).standard_normal(out[name].shape)
        drawn = base * np.exp(spread * noise) if base else spread * noise
        out[name] = jnp.asarray(drawn.astype(out[name].dtype))
    for name, factor in factors.items():
        out[name] = (out[name] * factor).astype(out[name].dtype)
    return out
```

```python
from contextlib import ExitStack

import numpy as np
import concourse.bass as bass
from concourse import mybir

P = 128
F32 = mybir.dt.float32
BF16 = mybir.dt.bfloat16
I32 = mybir.dt.int32
ALU = mybir.AluOpType
ACT = mybir.ActivationFunctionType
AX_X = mybir.AxisListType.X
AX_XY = mybir.AxisListType.XY

EPS = 1e-6
MASKED = -1e30
NH = 16
HD = 32
CHD = 16

BANKS = ["G0", "G1", "S0", "S1", "S2", "T0", "T1", "O"]
N_SELF, N_CROSS = 12, 16

PLAN = (
    [("ctT", "T"), ("xT0", "T"), ("xT1", "T"), ("mp0", "G"), ("mp1", "G"), ("mpT0", "T"), ("mpT1", "T"),
     ("s0", "S"), ("s1", "S"), ("ck", "G"), ("cv", "G"), ("pT0", "T"), ("pT1", "T"), ("mc0", "G"), ("mc1", "G"),
     ("mcT0", "T"), ("mcT1", "T"), ("gate0", "G"), ("gate1", "G"), ("xnT0", "T"), ("xnT1", "T"),
     ("q0", "G"), ("k0", "G"), ("v0", "G"), ("q1", "G"), ("k1", "G"), ("v1", "G"),
     ("qT0", "T"), ("kT0", "T"), ("qT1", "T"), ("kT1", "T")]
    + [(f"s{2 + u}", "S") for u in range(N_SELF)] + [(f"t{2 + u}", "T") for u in range(N_SELF)]
    + [("o0", "O"), ("o1", "O"), ("aoT0", "T"), ("aoT1", "T"), ("dense0", "G"), ("dense1", "G"),
       ("ciT0", "T"), ("ciT1", "T"), ("cq0", "G"), ("cq1", "G")]
    + [(f"s{14 + u}", "S") for u in range(N_CROSS)] + [(f"t{14 + u}", "T") for u in range(N_CROSS)]
    + [("o2", "O"), ("ccT", "T"), ("cd0", "G"), ("cd1", "G")]
)
RING = {"G": 2, "S": 3, "T": 2, "O": 1}


def place_jobs():
    seen, where, uses = dict.fromkeys(RING, 0), {}, dict.fromkeys(BANKS, 0)
    for name, ring in PLAN:
        n = seen[ring]
        bank = "O" if ring == "O" else f"{ring}{n % RING[ring]}"
        where[name] = (bank, n // RING[ring])
        uses[bank] += 1
        seen[ring] += 1
    assert all(seen[r] % RING[r] == 0 for r in RING), seen
    return where, uses


def program(nc, a, out, h_mid, consts):
    B, S, D = a["x"].shape
    E = a["ctx_1024"].shape[2]
    I = a["L1_xattn_v_gate"].shape[1]
    DC, EC = D // P, E // P
    TT = S // P
    FC = -(-I // P)
    FW = [min(P, I - f * P) for f in range(FC)]
    WHERE, USES = place_jobs()
    PRO = {"T0": 5, "T1": 5}
    FREE0 = {"T0": 5, "T1": 5, "G0": 1, "G1": 1, "O": 1}

    with ExitStack() as ctx:
        def sb(name, shape, dt=F32, c=ctx):
            return c.enter_context(nc.sbuf_tensor(name, shape, dt))

        def sem(name):
            return ctx.enter_context(nc.semaphore(name))

        ps = {n: ctx.enter_context(nc.psum_tensor(n, [P, 512], F32)) for n in BANKS}
        bank_ready = {n: sem(f"ready_{n}") for n in BANKS}
        bank_free = {n: sem(f"free_{n}") for n in BANKS}

        ident = sb("ident", [P, P])
        half_neg = sb("half_neg", [P, 1])

        phase_a = ExitStack()

        def sa(name, shape, dt=F32):
            return sb(name, shape, dt, phase_a)

        w_memT = sa("w_memT", [P, EC, D])
        w_gate = sa("w_gate", [P, 2 * DC, D])
        w_qkv = {e: sa(f"w_qkv_{e}", [P, DC, 3 * D]) for e in "lv"}
        w_dense = {e: sa(f"w_dense_{e}", [P, DC, D]) for e in "lv"}
        w_cq = sa("w_cq", [P, DC, E])
        w_ckv = sa("w_ckv", [P, EC, 2 * E])
        w_cd = sa("w_cd", [P, EC, D])
        bias_bc = sa("bias_bc", [P, D])
        nw_bc = {n: sa(f"nw_{n}", [P, D]) for n in ("norm", "ln_in", "cross")}
        cs = sa("cs", [P, TT, 2 * HD])
        pos = sa("pos", [P, TT], I32)
        posf = sa("posf", [P, 3, TT])
        posi = sa("posi", [P, TT], I32)
        identb = sa("identb", [P, P], BF16)
        tri = sa("tri", [P, 2, 512], BF16)
        par = sa("par", [P, 2])

        x_t = sa("x_t", [P, TT, D])
        c_t = sa("c_t", [P, TT, E])
        tok = sa("tok", [P, S], I32)
        eq = sa("eq", [P, S])
        mask = {e: sa(f"mask_{e}", [P, S]) for e in "vl"}
        ctT = sa("ctT", [P, EC, S])
        mp = sa("mp", [P, TT, D])
        bufA = sa("bufA", [P, DC, S])
        bufB = sa("bufB", [P, DC, S])
        qT = sa("qT", [P, DC, S])
        kT = sa("kT", [P, DC, S])
        mc = sa("mc", [P, TT, D])
        gs = sa("gs", [P, TT, D])
        fu = sa("fu", [P, TT, D])
        x1 = sa("x1", [P, TT, D])
        xn = sa("xn", [P, TT, D])
        rotA = sa("rotA", [P, 2, D])
        rotB = sa("rotB", [P, 2, D])
        qk = sa("qk", [P, 2, 2, D])
        p_ring = sa("p_ring", [P, 3, 512])
        pT_ring = sa("pT_ring", [P, 2, 512])
        cqT = sa("cqT", [P, 2, EC, S])
        ckT = sa("ckT", [P, EC, S])
        cvt = sa("cvt", [P, TT, E])
        sq = sa("sq", [P, D])
        mx = sa("mx", [P, 30, 4])
        nm = sa("nm", [P, 30, 4])
        sums = sa("sums", [P, 5, NH])
        rinv = sa("rinv", [P, 5, NH])
        ss = sa("ss", [P, 6])
        ms = sa("ms", [P, 6])
        rs = sa("rs", [P, 6])
        h2 = sa("h2", [P, TT, D])
        vt, ao, ciT = mc, fu, bufA
        gate_in = w_qkv["v"][:].rearrange("p c n -> p (c n)")[:, 0:DC * 2 * D].rearrange("p (c f) -> p c f", c=DC)
        mpT = qT
        cc, ccT = gs, gs

        phase_a.close()
        phase_b = ExitStack()

        def sbb(name, shape, dt=F32):
            return sb(name, shape, dt, phase_b)

        w_up = {e: sbb(f"w_up_{e}", [P, DC, 2, I]) for e in "vl"}
        w_dn = {e: sbb(f"w_dn_{e}", [P, FC, D]) for e in "vl"}
        nw_post = sbb("nw_post", [P, D])
        h_t = sbb("h_t", [P, 2, TT, D])
        mi = sbb("mi", [P, TT, D])
        miT = {e: sbb(f"miT_{e}", [P, DC, S]) for e in "vl"}
        sg = sbb("sg", [P, 2, S])
        hh = sbb("hh", [P, 4, S])
        sqb = sbb("sqb", [P, D])
        ssb = sbb("ssb", [P, 3, TT])
        tokb = sbb("tokb", [P, S], I32)
        eqb = sbb("eqb", [P, S])
        maskb = {e: sbb(f"maskb_{e}", [P, S]) for e in "vl"}
        o_t = sbb("o_t", [P, TT, D])
        phase_b.close()

        s_w = sem("weights_in")
        s_ws = sem("wmem_in")
        s_wg = sem("wgate_in")
        s_small = sem("small_in")
        s_x = sem("x_in")
        s_cs = sem("table_in")
        s_pos = sem("pos_done")
        s_id = sem("consts_done")
        s_par = sem("par_done")
        s_mask = sem("mask_done")
        s_mx = sem("max_done")
        s_nm = sem("negmax_done")
        s_p = sem("probs_done")
        s_pv = sem("pv_done")
        s_ri = sem("rinv_done")
        s_th = sem("tanh_done")
        s_f1 = sem("gated_done")
        s_fu = sem("fused_done")
        s_ss = sem("squares_done")
        s_ms = sem("mean_done")
        s_rs = sem("rsqrt_done")
        s_x1 = sem("x1_done")
        s_xn = sem("xn_done")
        s_rot = sem("rotated_done")
        s_ci = sem("ci_done")
        s_st = sem("h_stored")
        b_w = sem("b_weights_in")
        b_nw = sem("b_norm_weight_in")
        b_h = sem("b_h_in")
        b_ss = sem("b_squares")
        b_ms = sem("b_mean")
        b_rs = sem("b_rsqrt")
        b_mi = sem("b_mi")
        b_mask = sem("b_mask")
        b_sg = sem("b_silu")
        b_hh = sem("b_hidden")
        b_dn = sem("b_down")
        b_out = sem("b_out")
        b_st = sem("b_stored")
        U_B, UP_N = 2 * FC, 4

        def bank(job):
            return ps[WHERE[job][0]]

        def ready(job, b):
            n, k = WHERE[job]
            return bank_ready[n], b * USES[n] + (PRO.get(n, 0) + k + 1)

        def freed(job, b):
            n, k = WHERE[job]
            return bank_free[n], b * USES[n] + (FREE0[n] + k + 1)

        def vacant(job, b):
            n, k = WHERE[job]
            return bank_free[n], b * USES[n] + (FREE0[n] + k)

        def free_sem(job):
            return bank_free[WHERE[job][0]]

        def ready_sem(job):
            return bank_ready[WHERE[job][0]]

        self_units = [(0, [r, r + 4, r + 8, r + 12], P) for r in range(4)]
        self_units += [(1, [8 * cp + r, 8 * cp + 4 + r], S) for r in range(4) for cp in range(2)]
        cross_units = [(t, [2 * g, 2 * g + 1], S) for t in range(TT) for g in range(NH // 2)]
        units = {2 + i: u for i, u in enumerate(self_units)} | {14 + i: u for i, u in enumerate(cross_units)}

        def sum_row(u):
            return (1 if u < 14 else 3) + units[u][0]

        UPB = ["G0", "G1", "S0", "S1"]
        A_USES = {n: PRO.get(n, 0) + B * USES[n] for n in BANKS}

        def up_bank(j, u):
            return UPB[(j * U_B + u) % UP_N]

        def up_count(i, j, u):
            return i * (2 * U_B // UP_N) + (A_USES[up_bank(j, u)] + (j * U_B + u) // UP_N)

        def tb_count(i, j):
            return {n: i * 2 + (A_USES[n] + j) for n in ("T0", "T1")}

        def dn_count(i, j):
            return {n: i * 2 + ((A_USES[n] if n == "S2" else 0) + j) for n in ("S2", "O")}

        block = ctx.enter_context(nc.Block())
        tiled = a["x"].rearrange("b (t p) d -> b p t d", p=P)
        ctiled = a["ctx_1024"].rearrange("b (t p) d -> b p t d", p=P)
        htiled = h_mid.rearrange("b (t p) d -> b p t d", p=P)
        otiled = out.rearrange("b (t p) d -> b p t d", p=P)

        @block.sync
        def _(sp):
            def load_batch(b):
                sp.dma_start(x_t[:], tiled[b]).then_inc(s_x, 16)
                sp.dma_start(c_t[:], ctiled[b]).then_inc(s_x, 16)
                sp.dma_start(tok[:], a["mask_BxS_ik0"][b].partition_broadcast(P)).then_inc(s_x, 16)

            sp.dma_start(pos[:], a["pos_1xS"].rearrange("o (t p) -> p (o t)", p=P), allow_slow_non_contiguous=True).then_inc(s_pos, 16)
            sp.dma_start(bufA[:], a["L0_xattn_W_mem"].rearrange("(c p) e -> p c e", p=P)).then_inc(s_ws, 16)
            sp.dma_start(gate_in, a["L0_xattn_W_gate"].rearrange("(c p) f -> p c f", p=P)).then_inc(s_wg, 16)
            load_batch(0)
            for t, n in ((bias_bc, "L0_xattn_b_gate"), (nw_bc["norm"], "L0_xattn_norm_w"),
                         (nw_bc["ln_in"], "L1_xattn_ln_in_w"), (nw_bc["cross"], "L1_xattn_ln_post_cross_w")):
                sp.dma_start(t[:], a[n].partition_broadcast(P)).then_inc(s_small, 16)
            for t, n in ((w_ckv, "L1_xattn_ckv_w"), (w_qkv["l"], "L1_xattn_l_qkv"), (w_dense["l"], "L1_xattn_l_dense"),
                         (w_dense["v"], "L1_xattn_v_dense"), (w_cq, "L1_xattn_cq_w"), (w_cd, "L1_xattn_cdense_w")):
                sp.dma_start(t[:], a[n].rearrange("(c p) n -> p c n", p=P)).then_inc(s_w, 16)

            sp.wait_ge(bank_ready["T0"], PRO["T0"])
            sp.wait_ge(bank_ready["T1"], PRO["T1"])
            sp.dma_start(w_qkv["v"][:], a["L1_xattn_v_qkv"].rearrange("(c p) n -> p c n", p=P)).then_inc(s_w, 16)

            def store(b):
                sp.wait_ge(*freed("cd0", b))
                sp.wait_ge(*freed("cd1", b))
                sp.dma_start(htiled[b], h2[:]).then_inc(s_st, 16)

            with sp.Fori(0, B - 1) as b:
                sp.wait_ge(s_fu, b * 2 + 2)
                load_batch(b + 1)
                store(b)
            store(B - 1)
            sp.wait_ge(s_st, 16 * B + 16)

            def load_tile(b, buf):
                sp.dma_start(h_t[:, buf], htiled[b]).then_inc(b_h, 16)
                sp.dma_start(tokb[:], a["mask_BxS_ik0"][b].partition_broadcast(P)).then_inc(b_h, 16)

            sp.dma_start(nw_post[:], a["L1_xattn_ln_post_attn_w"].partition_broadcast(P)).then_inc(b_nw, 16)
            load_tile(0, 0)
            for e in "vl":
                for i, n in enumerate((f"L1_xattn_{e}_gate", f"L1_xattn_{e}_up")):
                    sp.dma_start(w_up[e][:, :, i], a[n].rearrange("(c p) n -> p c n", p=P)).then_inc(b_w, 16)
                dn = a[f"L1_xattn_{e}_down"]
                sp.dma_start(w_dn[e][:, 0:FC - 1], dn[0:(FC - 1) * P, :].rearrange("(c p) n -> p c n", p=P)).then_inc(b_w, 16)
                sp.dma_start(w_dn[e][0:FW[-1], FC - 1], dn[(FC - 1) * P:I, :]).then_inc(b_w, 16)

            def store_tile(b):
                sp.wait_ge(b_out, b * 2 + 2)
                sp.dma_start(otiled[b], o_t[:]).then_inc(b_st, 16)

            with sp.Fori(0, B // 2 - 1) as i:
                for j in range(2):
                    b = i * 2 + j
                    sp.wait_ge(b_mi, b * 2 + 2)
                    sp.wait_ge(b_mask, b * 5 + 5)
                    load_tile(b + 1, 1 - j)
                    store_tile(b)
            b = B - 2
            sp.wait_ge(b_mask, b * 5 + 5)
            sp.wait_ge(b_mi, b * 2 + 2)
            load_tile(b + 1, 1)
            store_tile(b)
            store_tile(b + 1)
            sp.wait_ge(b_st, 16 * B + 16)

        @block.gpsimd
        def _(pool):
            nc.gpsimd.memset(ident[:], 0.0).then_inc(s_id, 1)
            nc.gpsimd.memset(half_neg[:], -0.5).then_inc(s_id, 1)
            nc.gpsimd.memset(identb[:], 0.0).then_inc(s_id, 1)
            nc.gpsimd.memset(tri[:], 0.0).then_inc(s_id, 1)
            for first, n in ((bank_free["G0"], 1), (bank_free["G1"], 1), (bank_free["O"], 1), (s_p, 1), (s_ss, 1),
                             (s_st, 16), (b_ss, 1), (b_st, 16)):
                nc.gpsimd.nop().then_inc(first, n)
            pool.wait_ge(s_id, 4)
            for m in (ident, identb):
                nc.gpsimd.affine_select(out=m[:], in_=m[:], compare_op=ALU.not_equal, fill=1.0, base=0,
                                        pattern=[[-1, P]], channel_multiplier=1).then_inc(s_id, 1)
            nc.gpsimd.affine_select(out=tri[:, 0].rearrange("p (h k) -> p h k", k=P),
                                    in_=tri[:, 0].rearrange("p (h k) -> p h k", k=P), compare_op=ALU.is_ge,
                                    fill=MASKED, base=0, pattern=[[0, 4], [-1, P]], channel_multiplier=1).then_inc(s_id, 1)
            nc.gpsimd.affine_select(out=tri[:, 1].rearrange("p (h k) -> p h k", k=S),
                                    in_=tri[:, 1].rearrange("p (h k) -> p h k", k=S), compare_op=ALU.is_ge,
                                    fill=MASKED, base=P, pattern=[[0, 2], [-1, S]], channel_multiplier=1).then_inc(s_id, 1)
            pool.wait_ge(s_pos, 17)
            for t in range(TT):
                nc.gpsimd.indirect_dma_start(cs[:, t], None, consts["rotary"],
                                             bass.IndirectOffsetOnAxis(ap=posi[:, t:t + 1], axis=0)).then_inc(s_cs, 16)

            def rsqrt(b, n):
                pool.wait_ge(s_ms, b * 6 + n + 1)
                nc.gpsimd.tensor_tensor(rs[:, n:n + 1], ms[:, n:n + 1], half_neg[:], ALU.pow).then_inc(s_rs, 1)

            with pool.Fori(0, B) as b:
                for n in range(4):
                    rsqrt(b, n)
                for j, job in enumerate(("q0", "k0", "q1", "k1")):
                    pool.wait_ge(*freed(job, b))
                    nc.gpsimd.tensor_tensor(qk[:, j // 2, j % 2], rotA[:, j % 2], rotB[:, j % 2], ALU.add).then_inc(s_rot, 1)
                for n in range(4, 6):
                    rsqrt(b, n)

            with pool.Fori(0, B) as b:
                for t in range(TT):
                    pool.wait_ge(b_ms, b * 2 + t + 1)
                    nc.gpsimd.tensor_tensor(ssb[:, 2, t:t + 1], ssb[:, 1, t:t + 1], half_neg[:], ALU.pow).then_inc(b_rs, 1)

        @block.scalar
        def _(act):
            def copy(dst, job, b, view=None):
                act.wait_ge(*ready(job, b))
                src = bank(job)[:] if view is None else view(bank(job))
                nc.scalar.activation(dst, src, ACT.Copy).then_inc(free_sem(job), 1)

            def square(src, n, b):
                act.wait_ge(s_ss, b * 6 + (n + 1))
                nc.scalar.activation(sq[:], src, ACT.Square, accum_out=ss[:, n:n + 1]).then_inc(s_ss, 1)

            def exps(u, b):
                act.wait_ge(s_nm, b * 30 + u + 1)
                if u >= 5:
                    act.wait_ge(*ready(f"t{u - 3}", b))
                t, heads, w = units[u]
                scale = (HD if u < 14 else CHD) ** -0.5
                for j, h in enumerate(heads):
                    e = nc.scalar.activation(p_ring[:, u % 3, j * w:(j + 1) * w], bank(f"s{u}")[:, j * w:(j + 1) * w],
                                             ACT.Exp, bias=nm[:, u, j:j + 1], scale=scale,
                                             accum_out=sums[:, sum_row(u), h:h + 1])
                e.then_inc(s_p, 1)

            with act.Fori(0, B) as b:
                copy(ctT[:], "ctT", b, lambda k: k[:].rearrange("p (c m) -> p c m", c=EC))
                copy(bufA[:, :, P:S], "xT1", b, lambda k: k[:].rearrange("p (c m) -> p c m", c=DC))
                copy(mp[:, 0], "mp0", b)
                copy(mp[:, 1], "mp1", b)
                copy(mpT[:, 0:2], "mpT0", b, lambda k: k[:].rearrange("p (c m) -> p c m", c=2))
                copy(mpT[:, 2:4], "mpT1", b, lambda k: k[:].rearrange("p (c m) -> p c m", c=2))
                for t in range(TT):
                    act.wait_ge(s_nm, b * 30 + t + 1)
                    nc.scalar.activation(p_ring[:, t, 0:S], bank(f"s{t}")[:, 0:S], ACT.Exp, bias=nm[:, t, 0:1],
                                         scale=D ** -0.5, accum_out=sums[:, 0, t:t + 1]).then_inc(s_p, 1)
                copy(ckT[:], "ck", b, lambda k: k[:].rearrange("p (c m) -> p c m", c=EC))
                copy(cvt[:], "cv", b, lambda k: k[:].rearrange("p (c m) -> p c m", c=TT))
                copy(bufB[:, :, 0:P], "mcT0", b, lambda k: k[:].rearrange("p (c m) -> p c m", c=DC))
                copy(bufB[:, :, P:S], "mcT1", b, lambda k: k[:].rearrange("p (c m) -> p c m", c=DC))
                for t in range(TT):
                    act.wait_ge(*freed(f"gate{t}", b))
                    nc.scalar.activation(gs[:, t], gs[:, t], ACT.Tanh, scale=0.5).then_inc(s_th, 1)
                for t in range(TT):
                    act.wait_ge(s_fu, b * 2 + t + 1)
                    square(fu[:, t], t, b)
                for t in range(TT):
                    act.wait_ge(s_x1, b * 2 + t + 1)
                    square(x1[:, t], 2 + t, b)
                copy(vt[:, 0], "v0", b)
                copy(vt[:, 1], "v1", b)
                for t in range(TT):
                    for j, x in enumerate((qT, kT)):
                        copy(x[:, :, t * P:(t + 1) * P], f"{'qk'[j]}T{t}", b, lambda k: k[:].rearrange("p (c m) -> p c m", c=DC))
                for u in range(2, 2 + N_SELF):
                    exps(u, b)
                for t in range(TT):
                    act.wait_ge(*freed(f"dense{t}", b))
                    square(x1[:, t], 4 + t, b)
                for u in range(14, 14 + N_CROSS):
                    exps(u, b)
                copy(ccT[:, 1].rearrange("p (c m) -> p c m", c=EC), "ccT", b, lambda k: k[:].rearrange("p (c m) -> p c m", c=EC))

            with act.Fori(0, B // 2) as i:
                for j in range(2):
                    b = i * 2 + j
                    act.wait_ge(b_h, b * 32 + 32)
                    for t in range(TT):
                        act.wait_ge(b_ss, b * 2 + (t + 1))
                        nc.scalar.activation(sqb[:], h_t[:, j, t], ACT.Square, accum_out=ssb[:, 0, t:t + 1]).then_inc(b_ss, 1)
                    for u in range(U_B):
                        n = b * U_B + u
                        act.wait_ge(bank_ready[up_bank(j, u)], up_count(i, j, u) + 1)
                        if u >= 2:
                            act.wait_ge(b_hh, n - 1)
                        w = FW[u % FC]
                        nc.scalar.activation(sg[0:w, u % 2], ps[up_bank(j, u)][0:w, 0:S], ACT.Silu).then_inc(b_sg, 1)

        @block.vector
        def _(dve):
            dve.wait_ge(s_pos, 16)
            nc.vector.tensor_copy(posf[:, 0], pos[:]).then_inc(s_mx, 1)
            dve.wait_ge(s_mx, 1)
            nc.vector.tensor_scalar(posf[:, 1], posf[:, 0], 0.0, float(S), ALU.is_lt, ALU.mult).then_inc(s_mx, 1)
            dve.wait_ge(s_mx, 2)
            nc.vector.tensor_tensor(posf[:, 2], posf[:, 0], posf[:, 1], ALU.add).then_inc(s_mx, 1)
            dve.wait_ge(s_mx, 3)
            nc.vector.tensor_scalar(posi[:], posf[:, 2], 0.0, float(S - 1), ALU.max, ALU.min).then_inc(s_pos, 1)
            for c in range(EC):
                dve.wait_ge(bank_ready[f"T{c}"], 1)
                nc.vector.tensor_copy(w_memT[:, c], ps[f"T{c}"][:]).then_inc(bank_free[f"T{c}"], 1)
            for f in range(2 * DC):
                n = f"T{f % 2}"
                dve.wait_ge(bank_ready[n], 2 + f // 2)
                nc.vector.tensor_copy(w_gate[:, f], ps[n][:]).then_inc(bank_free[n], 1)
            MX0 = 3

            def masks(b, sem_, k, tok_, eq_, mv, ml):
                nc.vector.tensor_scalar(eq_[:], tok_[:], 1.0, None, ALU.is_equal).then_inc(sem_, 1)
                nc.vector.memset(mv[:, S - 1:S], 0.0).then_inc(sem_, 1)
                dve.wait_ge(sem_, b * 5 + 2)
                nc.vector.tensor_tensor(mv[:, 0:S - 1], eq_[:, 0:S - 1], eq_[:, 1:S], ALU.mult).then_inc(sem_, 1)
                dve.wait_ge(sem_, b * 5 + 3)
                nc.vector.tensor_scalar(ml[:], mv[:], -1.0, 1.0, ALU.mult, ALU.add).then_inc(sem_, 2)

            def copy(dst, job, b, view=None):
                dve.wait_ge(*ready(job, b))
                src = bank(job)[:] if view is None else view(bank(job))
                nc.vector.tensor_copy(dst, src).then_inc(free_sem(job), 1)

            def maxima(u, b):
                if u < 2:
                    nh, w, scale = 1, S, D ** -0.5
                else:
                    nh, w = len(units[u][1]), units[u][2]
                    scale = (HD if u < 14 else CHD) ** -0.5
                dve.wait_ge(*ready(f"s{u}", b))
                nc.vector.tensor_reduce(mx[:, u, 0:nh], bank(f"s{u}")[:, 0:nh * w].rearrange("p (h k) -> p h k", k=w),
                                        AX_X, ALU.max).then_inc(s_mx, 1)
                dve.wait_ge(s_mx, b * 30 + (MX0 + u + 1))
                nc.vector.tensor_scalar(nm[:, u, 0:nh], mx[:, u, 0:nh], -scale, None, ALU.mult).then_inc(s_nm, 1)

            def evac_T(u, b):
                dve.wait_ge(*ready(f"t{u}", b))
                if u >= 4:
                    dve.wait_ge(s_pv, b * 28 + (u - 2 - 2 + 1))
                nc.vector.tensor_copy(pT_ring[:, u % 2], bank(f"t{u}")[:]).then_inc(free_sem(f"t{u}"), 1)

            def mean(b, n):
                dve.wait_ge(s_ss, b * 6 + (n + 2))
                nc.vector.tensor_scalar(ms[:, n:n + 1], ss[:, n:n + 1], 1.0 / D, EPS, ALU.mult, ALU.add).then_inc(s_ms, 1)

            def scaled(b, n, dst, src, w, done):
                dve.wait_ge(s_rs, b * 6 + n + 1)
                nc.vector.scalar_tensor_tensor(out=dst, in0=src, scalar=rs[:, n:n + 1], in1=w[:], op0=ALU.mult,
                                               op1=ALU.mult).then_inc(done, 1)

            def split_experts(job, t, b):
                dve.wait_ge(*ready(job, b))
                src = bank(job)[:].rearrange("p (c m) -> p c m", c=DC)
                for buf, e in ((bufA, "v"), (bufB, "l")):
                    m = mask[e][:, t * P:(t + 1) * P].unsqueeze(1).broadcast_to([P, DC, P])
                    o = nc.vector.tensor_tensor(buf[:, :, t * P:(t + 1) * P], src, m, ALU.mult)
                o.then_inc(free_sem(job), 1)

            def rotary(job, j, b):
                t = j // 2
                dve.wait_ge(*ready(job, b))
                if j >= 2:
                    dve.wait_ge(s_rot, b * 4 + (j - 1))
                src = bank(job)[:].rearrange("p (h a d) -> p h a d", h=NH, a=2)
                co = cs[:, t, 0:HD].unsqueeze(1).broadcast_to([P, NH, HD])
                si = cs[:, t, HD:2 * HD].rearrange("p (a d) -> p a d", a=2)
                nc.vector.tensor_tensor(rotA[:, j % 2].rearrange("p (h d) -> p h d", h=NH),
                                        bank(job)[:].rearrange("p (h d) -> p h d", h=NH), co, ALU.mult)
                outB = rotB[:, j % 2].rearrange("p (h a d) -> p h a d", h=NH, a=2)
                for k in range(2):
                    o = nc.vector.tensor_tensor(outB[:, :, k], src[:, :, 1 - k],
                                                si[:, k].unsqueeze(1).broadcast_to([P, NH, HD // 2]), ALU.mult)
                o.then_inc(free_sem(job), 1)

            def reciprocal(b, n, row, cols, p_needed):
                dve.wait_ge(s_p, b * 30 + (p_needed + 1))
                nc.vector.reciprocal(rinv[:, row, cols], sums[:, row, cols]).then_inc(s_ri, 1)

            dve.wait_ge(s_small, 64)
            dve.wait_ge(s_cs, 32)
            dve.wait_ge(s_id, 8)
            nc.vector.tensor_reduce(par[:], ident[:].rearrange("p (g k j) -> p k g j", k=2, j=CHD), AX_XY, ALU.add).then_inc(s_par, 1)
            dve.wait_ge(s_par, 1)
            with dve.Fori(0, B) as b:
                dve.wait_ge(s_x, b * 48 + 48)
                masks(b, s_mask, 0, tok, eq, mask["v"], mask["l"])
                copy(bufA[:, :, 0:P], "xT0", b, lambda k: k[:].rearrange("p (c m) -> p c m", c=DC))
                for t in range(TT):
                    maxima(t, b)
                for t in range(TT):
                    dve.wait_ge(*ready(f"pT{t}", b))
                    nc.vector.tensor_copy(pT_ring[:, t, 0:S], bank(f"pT{t}")[:, 0:S]).then_inc(free_sem(f"pT{t}"), 1)
                reciprocal(b, 0, 0, slice(0, TT), 2)
                dve.wait_ge(s_ri, b * 5 + 1)
                for t in range(TT):
                    dve.wait_ge(*ready(f"mc{t}", b))
                    nc.vector.tensor_scalar(mc[:, t], bank(f"mc{t}")[:], rinv[:, 0, t:t + 1], None, ALU.mult) \
                        .then_inc(free_sem(f"mc{t}"), 1)
                for t in range(TT):
                    dve.wait_ge(*ready(f"gate{t}", b))
                    nc.vector.tensor_tensor(gs[:, t], bank(f"gate{t}")[:], bias_bc[:], ALU.add) \
                        .then_inc(free_sem(f"gate{t}"), 1)
                for t in range(TT):
                    dve.wait_ge(s_th, b * 2 + t + 1)
                    nc.vector.scalar_tensor_tensor(out=gs[:, t], in0=gs[:, t], scalar=1.0, in1=mc[:, t], op0=ALU.add,
                                                   op1=ALU.mult).then_inc(s_f1, 1)
                    dve.wait_ge(s_f1, b * 2 + t + 1)
                    nc.vector.scalar_tensor_tensor(out=fu[:, t], in0=gs[:, t], scalar=0.5, in1=x_t[:, t], op0=ALU.mult,
                                                   op1=ALU.add).then_inc(s_fu, 1)
                for t in range(TT):
                    mean(b, t)
                for t in range(TT):
                    scaled(b, t, x1[:, t], fu[:, t], nw_bc["norm"], s_x1)
                for t in range(TT):
                    mean(b, 2 + t)
                for t in range(TT):
                    scaled(b, 2 + t, xn[:, t], x1[:, t], nw_bc["ln_in"], s_xn)
                for t in range(TT):
                    split_experts(f"xnT{t}", t, b)
                for j, job in enumerate(("q0", "k0", "q1", "k1")):
                    rotary(job, j, b)
                last = 2 + N_SELF
                for i in range(2, last + 3):
                    if i < last:
                        maxima(i, b)
                    if 2 <= i - 2 < last:
                        evac_T(i - 2, b)
                    if i - 3 == 5:
                        reciprocal(b, 1, 1, slice(0, NH), 6)
                        dve.wait_ge(s_ri, b * 5 + 2)
                        dve.wait_ge(s_pv, b * 28 + 4)
                        nc.vector.tensor_tensor(ao[:, 0].rearrange("p (h d) -> p h d", h=NH),
                                                bank("o0")[:].rearrange("p (h d) -> p h d", h=NH),
                                                rinv[:, 1].unsqueeze(2).broadcast_to([P, NH, HD]), ALU.mult) \
                            .then_inc(free_sem("o0"), 1)
                reciprocal(b, 2, 2, slice(0, NH), 14)
                dve.wait_ge(s_ri, b * 5 + 3)
                dve.wait_ge(s_pv, b * 28 + 12)
                nc.vector.tensor_tensor(ao[:, 1].rearrange("p (h d) -> p h d", h=NH),
                                        bank("o1")[:].rearrange("p (h d) -> p h d", h=NH),
                                        rinv[:, 2].unsqueeze(2).broadcast_to([P, NH, HD]), ALU.mult) \
                    .then_inc(free_sem("o1"), 1)
                for t in range(TT):
                    split_experts(f"aoT{t}", t, b)
                for t in range(TT):
                    dve.wait_ge(*ready(f"dense{t}", b))
                    nc.vector.tensor_tensor(x1[:, t], bank(f"dense{t}")[:], x1[:, t], ALU.add) \
                        .then_inc(free_sem(f"dense{t}"), 1)
                for t in range(TT):
                    mean(b, 4 + t)
                for t in range(TT):
                    scaled(b, 4 + t, xn[:, t], x1[:, t], nw_bc["cross"], s_ci)
                for t in range(TT):
                    copy(ciT[:, :, t * P:(t + 1) * P], f"ciT{t}", b, lambda k: k[:].rearrange("p (c m) -> p c m", c=DC))
                for c in range(EC):
                    dve.wait_ge(*ready(f"cq{c}", b))
                    for k in range(2):
                        o = nc.vector.tensor_scalar(cqT[:, k, c], bank(f"cq{c}")[:, 0:S], par[:, k:k + 1], None, ALU.mult)
                    o.then_inc(free_sem(f"cq{c}"), 1)
                last = 14 + N_CROSS
                for i in range(14, last + 2):
                    if i < last:
                        maxima(i, b)
                    if 14 <= i - 2:
                        evac_T(i - 2, b)
                dve.wait_ge(s_p, b * 30 + 31)
                nc.vector.reciprocal(rinv[:, 3:5], sums[:, 3:5]).then_inc(s_ri, 2)
                dve.wait_ge(s_ri, b * 5 + 5)
                dve.wait_ge(s_pv, b * 28 + 28)
                nc.vector.tensor_tensor(cc[:, 0].rearrange("p (h d) -> p h d", d=CHD),
                                        bank("o2")[:].rearrange("p (h d) -> p h d", d=CHD),
                                        rinv[:, 3:5].rearrange("p t h -> p (t h)").unsqueeze(2).broadcast_to([P, 2 * NH, CHD]),
                                        ALU.mult).then_inc(free_sem("o2"), 1)
                dve.wait_ge(s_st, b * 16 + 16)
                for t in range(TT):
                    dve.wait_ge(*ready(f"cd{t}", b))
                    nc.vector.tensor_tensor(h2[:, t], bank(f"cd{t}")[:], x1[:, t], ALU.add).then_inc(free_sem(f"cd{t}"), 1)

            dve.wait_ge(b_nw, 16)
            with dve.Fori(0, B // 2) as i:
                for j in range(2):
                    b = i * 2 + j
                    dve.wait_ge(b_h, b * 32 + 32)
                    masks(b, b_mask, 0, tokb, eqb, maskb["v"], maskb["l"])
                    for t in range(TT):
                        dve.wait_ge(b_ss, b * 2 + (t + 2))
                        nc.vector.tensor_scalar(ssb[:, 1, t:t + 1], ssb[:, 0, t:t + 1], 1.0 / D, EPS, ALU.mult, ALU.add) \
                            .then_inc(b_ms, 1)
                    for t in range(TT):
                        dve.wait_ge(b_rs, b * 2 + t + 1)
                        nc.vector.scalar_tensor_tensor(out=mi[:, t], in0=h_t[:, j, t], scalar=ssb[:, 2, t:t + 1],
                                                       in1=nw_post[:], op0=ALU.mult, op1=ALU.mult).then_inc(b_mi, 1)
                    for t in range(TT):
                        n = f"T{t}"
                        dve.wait_ge(bank_ready[n], tb_count(i, j)[n] + 1)
                        for e in "vl":
                            m = maskb[e][:, t * P:(t + 1) * P].unsqueeze(1).broadcast_to([P, DC, P])
                            o = nc.vector.tensor_tensor(miT[e][:, :, t * P:(t + 1) * P],
                                                        ps[n][:].rearrange("p (c m) -> p c m", c=DC), m, ALU.mult)
                        o.then_inc(bank_free[n], 1)
                    for u in range(U_B):
                        n = b * U_B + u
                        w = FW[u % FC]
                        dve.wait_ge(b_sg, n + 1)
                        if u >= 4:
                            dve.wait_ge(b_dn, b * (U_B - 1) + (u - 3))
                        nc.vector.tensor_tensor(hh[0:w, u % 4], ps[up_bank(j, u)][0:w, S:2 * S], sg[0:w, u % 2], ALU.mult) \
                            .then_inc(b_hh, 1)
                    dve.wait_ge(b_st, b * 16 + 16)
                    for t, n in enumerate(("S2", "O")):
                        dve.wait_ge(bank_ready[n], dn_count(i, j)[n] + 1)
                        nc.vector.tensor_tensor(o_t[:, t], ps[n][:], h_t[:, j, t], ALU.add).then_inc(b_out, 1)

        @block.tensor
        def _(pe):
            pe.wait_ge(s_id, 8)
            pe.wait_ge(s_ws, 16)
            for e in range(EC):
                for d in range(DC):
                    m = nc.tensor.transpose(ps[f"T{e}"][:, d * P:(d + 1) * P], bufA[:, d, e * P:(e + 1) * P], ident[:])
                m.then_inc(bank_ready[f"T{e}"], 1)
            pe.wait_ge(s_wg, 16)
            for f in range(2 * DC):
                n = f"T{f % 2}"
                pe.wait_ge(bank_free[n], 1 + f // 2)
                for d in range(DC):
                    m = nc.tensor.transpose(ps[n][:, d * P:(d + 1) * P], gate_in[:, d, f * P:(f + 1) * P], ident[:])
                m.then_inc(bank_ready[n], 1)

            def transposes(job, b, blocks):
                pe.wait_ge(*vacant(job, b))
                for i, src in enumerate(blocks):
                    m = nc.tensor.transpose(bank(job)[:, i * P:(i + 1) * P], src, ident[:])
                m.then_inc(ready_sem(job), 1)

            def gemm(job, b, dst, pairs, last=True):
                for i, (l, r) in enumerate(pairs):
                    m = nc.tensor.matmul(dst, l, r, start=(i == 0), stop=(i == len(pairs) - 1))
                if last:
                    m.then_inc(ready_sem(job), 1)

            def tiles(x, t, n=DC):
                return [x[:, t, c * P:(c + 1) * P] for c in range(n)]

            def scores(u, b):
                pe.wait_ge(s_p, b * 30 + (u - 1))
                t, heads, w = units[u]
                s = bank(f"s{u}")
                if u < 14:
                    nc.tensor.matmul(s[:], identb[:], tri[:, t], start=True, stop=True, skip_group_check=True)
                for j, h in enumerate(heads):
                    if u < 14:
                        c, r = h // 4, (h % 4) * 32
                        l, k = qT[r:r + 32, c, t * P:(t + 1) * P], kT[r:r + 32, c, 0:w]
                    else:
                        c, r = h // 8, (h % 8) // 2 * 32
                        l, k = cqT[r:r + 32, h % 2, c, t * P:(t + 1) * P], ckT[r:r + 32, c, 0:w]
                    m = nc.tensor.matmul(s[:, j * w:(j + 1) * w], l, k, start=(u >= 14), stop=True,
                                         skip_group_check=True)
                m.then_inc(ready_sem(f"s{u}"), 1)

            def turn(u, b):
                pe.wait_ge(s_p, b * 30 + (u + 2))
                transposes(f"t{u}", b, [p_ring[:, u % 3, i * P:(i + 1) * P] for i in range(4)])

            def values(u, b):
                t, heads, w = units[u]
                cross = u >= 14
                o = "o2" if cross else f"o{t}"
                if u in (2, 6, 14):
                    pe.wait_ge(*vacant(o, b))
                pe.wait_ge(*freed(f"t{u}", b))
                v, d = (cvt, CHD) if cross else (vt, HD)
                for j, h in enumerate(heads):
                    col = h * d + (t * E if cross else 0)
                    for k in range(w // P):
                        i = j * (w // P) + k
                        m = nc.tensor.matmul(bank(o)[:, col:col + d], pT_ring[:, u % 2, i * P:(i + 1) * P],
                                             v[:, k, h * d:(h + 1) * d], start=(k == 0), stop=(k == w // P - 1))
                m.then_inc(s_pv, 1)

            pe.wait_ge(s_w, 112)
            with pe.Fori(0, B) as b:
                pe.wait_ge(s_x, b * 48 + 48)
                transposes("ctT", b, [c_t[:, m, e * P:(e + 1) * P] for e in range(EC) for m in range(TT)])
                for t in range(TT):
                    transposes(f"xT{t}", b, tiles(x_t, t))
                pe.wait_ge(*freed("ctT", b))
                for m in range(TT):
                    pe.wait_ge(*vacant(f"mp{m}", b))
                    gemm(f"mp{m}", b, bank(f"mp{m}")[:], [(ctT[:, e, m * P:(m + 1) * P], w_memT[:, e]) for e in range(EC)])
                pe.wait_ge(*freed("mp0", b))
                pe.wait_ge(*freed("mp1", b))
                for k in range(2):
                    transposes(f"mpT{k}", b, [mp[:, m, (2 * k + c) * P:(2 * k + c + 1) * P] for c in range(2) for m in range(TT)])
                pe.wait_ge(*vacant("ck", b))
                for c in range(EC):
                    gemm("ck", b, bank("ck")[:, c * S:(c + 1) * S],
                         [(w_ckv[:, e, c * P:(c + 1) * P], ctT[:, e]) for e in range(EC)], last=(c == EC - 1))
                pe.wait_ge(*freed("xT0", b))
                pe.wait_ge(*freed("xT1", b))
                pe.wait_ge(*freed("mpT0", b))
                pe.wait_ge(*freed("mpT1", b))
                for t in range(TT):
                    pe.wait_ge(s_p, b * 30 + 1)
                    gemm(f"s{t}", b, bank(f"s{t}")[:, 0:S], [(bufA[:, c, t * P:(t + 1) * P], mpT[:, c]) for c in range(DC)])
                pe.wait_ge(*vacant("cv", b))
                for m in range(TT):
                    gemm("cv", b, bank("cv")[:, m * E:(m + 1) * E],
                         [(ctT[:, e, m * P:(m + 1) * P], w_ckv[:, e, E:2 * E]) for e in range(EC)], last=(m == TT - 1))
                for t in range(TT):
                    pe.wait_ge(s_p, b * 30 + (t + 2))
                    transposes(f"pT{t}", b, [p_ring[:, t, m * P:(m + 1) * P] for m in range(TT)])
                for t in range(TT):
                    pe.wait_ge(*freed(f"pT{t}", b))
                    pe.wait_ge(*vacant(f"mc{t}", b))
                    gemm(f"mc{t}", b, bank(f"mc{t}")[:], [(pT_ring[:, t, m * P:(m + 1) * P], mp[:, m]) for m in range(TT)])
                for t in range(TT):
                    pe.wait_ge(*freed(f"mc{t}", b))
                    transposes(f"mcT{t}", b, tiles(mc, t))
                for t in range(TT):
                    pe.wait_ge(*freed(f"mcT{t}", b))
                    pe.wait_ge(*vacant(f"gate{t}", b))
                    gemm(f"gate{t}", b, bank(f"gate{t}")[:],
                         [((bufA, bufB)[c // DC][:, c % DC, t * P:(t + 1) * P], w_gate[:, c]) for c in range(2 * DC)])
                for t in range(TT):
                    pe.wait_ge(s_xn, b * 2 + t + 1)
                    transposes(f"xnT{t}", b, tiles(xn, t))
                for t in range(TT):
                    pe.wait_ge(*freed(f"xnT{t}", b))
                    for n, job in enumerate("qkv"):
                        job = f"{job}{t}"
                        pe.wait_ge(*vacant(job, b))
                        gemm(job, b, bank(job)[:], [(buf[:, c, t * P:(t + 1) * P], w_qkv[e][:, c, n * D:(n + 1) * D])
                                                   for buf, e in ((bufB, "l"), (bufA, "v")) for c in range(DC)])
                for t in range(TT):
                    for j in range(2):
                        pe.wait_ge(s_rot, b * 4 + (2 * t + j + 1))
                        transposes(f"{'qk'[j]}T{t}", b, [qk[:, t, j, c * P:(c + 1) * P] for c in range(DC)])
                for t in range(TT):
                    for j in "qk":
                        pe.wait_ge(*freed(f"{j}T{t}", b))
                    pe.wait_ge(*freed(f"v{t}", b))
                last = 2 + N_SELF
                for i in range(2, last + 3):
                    if i < last:
                        scores(i, b)
                    if 2 <= i - 2 < last:
                        turn(i - 2, b)
                    if 2 <= i - 3 < last:
                        values(i - 3, b)
                for t in range(TT):
                    pe.wait_ge(*freed(f"o{t}", b))
                    transposes(f"aoT{t}", b, tiles(ao, t))
                for t in range(TT):
                    job = f"dense{t}"
                    pe.wait_ge(*freed(f"aoT{t}", b))
                    pe.wait_ge(*vacant(job, b))
                    gemm(job, b, bank(job)[:], [(buf[:, c, t * P:(t + 1) * P], w_dense[e][:, c])
                                                for buf, e in ((bufB, "l"), (bufA, "v")) for c in range(DC)])
                for t in range(TT):
                    pe.wait_ge(s_ci, b * 2 + t + 1)
                    transposes(f"ciT{t}", b, tiles(xn, t))
                for t in range(TT):
                    pe.wait_ge(*freed(f"ciT{t}", b))
                for c in range(EC):
                    pe.wait_ge(*vacant(f"cq{c}", b))
                    gemm(f"cq{c}", b, bank(f"cq{c}")[:, 0:S], [(w_cq[:, k, c * P:(c + 1) * P], ciT[:, k]) for k in range(DC)])
                for c in range(EC):
                    pe.wait_ge(*freed(f"cq{c}", b))
                pe.wait_ge(*freed("ck", b))
                pe.wait_ge(*freed("cv", b))
                last = 14 + N_CROSS
                for i in range(14, last + 3):
                    if i < last:
                        scores(i, b)
                    if 14 <= i - 2 < last:
                        turn(i - 2, b)
                    if 14 <= i - 3 < last:
                        values(i - 3, b)
                pe.wait_ge(*freed("o2", b))
                transposes("ccT", b, [cc[:, 0, t * E + c * P:t * E + (c + 1) * P] for c in range(EC) for t in range(TT)])
                pe.wait_ge(*freed("ccT", b))
                for t in range(TT):
                    pe.wait_ge(*vacant(f"cd{t}", b))
                    gemm(f"cd{t}", b, bank(f"cd{t}")[:],
                         [(ccT[:, 1, c * S + t * P:c * S + (t + 1) * P], w_cd[:, c]) for c in range(EC)])

            pe.wait_ge(b_w, 128)
            with pe.Fori(0, B // 2) as i:
                for j in range(2):
                    b = i * 2 + j
                    for t in range(TT):
                        n = f"T{t}"
                        pe.wait_ge(b_mi, b * 2 + t + 1)
                        pe.wait_ge(bank_free[n], tb_count(i, j)[n])
                        for c in range(DC):
                            m = nc.tensor.transpose(ps[n][:, c * P:(c + 1) * P], mi[:, t, c * P:(c + 1) * P], ident[:])
                        m.then_inc(bank_ready[n], 1)
                    for t in range(TT):
                        n = f"T{t}"
                        pe.wait_ge(bank_free[n], tb_count(i, j)[n] + 1)

                    def down(u):
                        e, f = "vl"[u // FC], u % FC
                        pe.wait_ge(b_hh, b * U_B + u + 1)
                        for t, n in enumerate(("S2", "O")):
                            m = nc.tensor.matmul(ps[n][:], hh[0:FW[f], u % 4, t * P:(t + 1) * P], w_dn[e][0:FW[f], f],
                                                 start=(u == 0), stop=(u == U_B - 1))
                            if u == U_B - 1:
                                m.then_inc(bank_ready[n], 1)
                        if u < U_B - 1:
                            m.then_inc(b_dn, 1)

                    for u in range(U_B + 2):
                        if u < U_B:
                            e, f = "vl"[u // FC], u % FC
                            if u >= UP_N:
                                pe.wait_ge(b_hh, b * U_B + (u - UP_N + 1))
                            for g in range(2):
                                for c in range(DC):
                                    m = nc.tensor.matmul(ps[up_bank(j, u)][0:FW[f], g * S:(g + 1) * S],
                                                         w_up[e][:, c, g, f * P:f * P + FW[f]], miT[e][:, c],
                                                         start=(c == 0), stop=(c == DC - 1))
                            m.then_inc(bank_ready[up_bank(j, u)], 1)
                        if u >= 2:
                            down(u - 2)


def rotary_table(n):
    inv = (1.0 / 10000.0 ** (np.arange(0, HD, 2, dtype=np.float32) / np.float32(HD))).astype(np.float32)
    f = np.outer(np.arange(n, dtype=np.float32), inv).astype(np.float32)
    return np.concatenate([np.cos(f), np.cos(f), -np.sin(f), np.sin(f)], axis=1).astype(np.float32)


_INS = ["x", "ctx_1024", "pos_1xS", "mask_BxS_ik0", "L0_xattn_W_mem", "L0_xattn_W_gate", "L0_xattn_b_gate",
        "L0_xattn_norm_w", "L1_xattn_ln_in_w", "L1_xattn_ln_post_attn_w", "L1_xattn_ln_post_cross_w",
        "L1_xattn_v_qkv", "L1_xattn_l_qkv", "L1_xattn_v_dense", "L1_xattn_l_dense", "L1_xattn_cq_w",
        "L1_xattn_ckv_w", "L1_xattn_cdense_w", "L1_xattn_v_gate", "L1_xattn_v_up", "L1_xattn_v_down",
        "L1_xattn_l_gate", "L1_xattn_l_up", "L1_xattn_l_down"]


def kernel(**inputs):
    import numpy as _np
    import concourse.bacc as _bacc
    from concourse import mybir as _mybir
    from concourse.bass_utils import run_bass_kernel_spmd as _run

    nc = _bacc.Bacc("TRN2", target_bir_lowering=False, num_devices=1)
    arrays, args = {}, {}
    for name in _INS:
        v = _np.ascontiguousarray(inputs[name])
        arrays[f"in_{name}"] = v
        args[name] = nc.dram_tensor(f"in_{name}", v.shape, _mybir.dt.from_np(v.dtype), kind="ExternalInput").ap()
    table = rotary_table(inputs["x"].shape[1])
    arrays["rotary"] = table
    consts = {"rotary": nc.dram_tensor("rotary", table.shape, _mybir.dt.float32, kind="ExternalInput").ap()}
    shape = inputs["x"].shape
    out = nc.dram_tensor("out_0", shape, _mybir.dt.float32, kind="ExternalOutput").ap()
    h_mid = nc.dram_tensor("h_mid", shape, _mybir.dt.float32, kind="Internal").ap()
    program(nc, args, out, h_mid, consts)
    r = _run(nc, [arrays], core_ids=[0])
    return r.results[0]["out_0"]
```

```python
from contextlib import ExitStack

import numpy as np
import concourse.bass as bass
from concourse import mybir

P = 128
F32 = mybir.dt.float32
BF16 = mybir.dt.bfloat16
F16 = mybir.dt.float16
F32R = mybir.dt.float32r
I32 = mybir.dt.int32
ALU = mybir.AluOpType
ACT = mybir.ActivationFunctionType
AX_X = mybir.AxisListType.X
AX_XY = mybir.AxisListType.XY

EPS = 1e-6
MID = 4
MASKED = -1e30
NH = 16
HD = 32
CHD = 16
P_LIFT = float(np.log(2.0 ** 11))
PARTS = [(0, 0), (0, 1), (0, 2), (1, 0), (1, 1)]

BANKS = ["G0", "G1", "G2", "S0", "S1", "T0", "T1", "O"]
RING = {"G": 3, "S": 2, "T": 2, "O": 1}
N_SELF, N_CROSS = 12, 16
PAIRS = NH // 2
SELF, CROSS, END = 2, 2 + N_SELF, 2 + N_SELF + N_CROSS

PAIR_AHEAD = range(CROSS, CROSS + N_CROSS - 2, 2)

FRONT = {
    0: [("ctT", "T"), ("xT0", "T"), ("xT1", "T")],
    1: [("mp0", "G"), ("mp1", "G")],
    2: [("mpT0", "T"), ("mpT1", "T")],
    3: [("l0s", "G")],
    5: [("pT0", "T"), ("pT1", "T")],
    6: [("mc0", "G"), ("mc1", "G")],
    7: [("mcT0", "T"), ("mcT1", "T")],
    8: [("gate0", "G")],
    9: [("gate1", "G")],
    15: [("xnT0", "T"), ("xnT1", "T")],
    16: [("q0", "G"), ("k0", "G"), ("v0", "G")],
    19: [("q1", "G"), ("k1", "G"), ("v1", "G")],
    20: [("qT0", "T"), ("kT0", "T"), ("qT1", "T"), ("kT1", "T")],
}
SLOTS = N_CROSS + 3


def plan_iteration():
    jobs = []
    for i in range(SELF, CROSS + 3):
        jobs += [(f"s{i}", "S")] * (i < CROSS)
        jobs += [(f"t{i - 2}", "T")] * (SELF <= i - 2 < CROSS)
        jobs += [("o0", "O")] * (i == SELF + 3) + [("o1", "O")] * (i == SELF + 7)
        jobs += {9: [("aoT0", "T")], 10: [("dense0", "G")], 15: [("ciT0", "T")]}.get(i, [])
    jobs += [("aoT1", "T"), ("ck", "G"), ("dense1", "G"), ("cv", "G"), ("ciT1", "T"), ("cq0", "G"), ("cq1", "G"), ("x0", "T")]
    for i in range(CROSS, END + 3):
        jobs += [(f"s{i}", "S")] * (i < END)
        jobs += [(f"t{i - 2}", "T")] * (CROSS <= i - 2 < END)
        jobs += [("o2", "O")] * (i == CROSS + 3)
        jobs += [(f"x{(i - CROSS) // 2 + 1}", "T")] * (i in PAIR_AHEAD)
        jobs += FRONT.get(i - CROSS, [])
    jobs += FRONT[SLOTS] + [("ccT", "T")] + FRONT[SLOTS + 1] + [("cd0", "G"), ("cd1", "G")]
    return jobs


def place_jobs():
    seen, where, uses = dict.fromkeys(RING, 0), {}, dict.fromkeys(BANKS, 0)
    for name, ring in plan_iteration():
        n = seen[ring]
        bank = "O" if ring == "O" else f"{ring}{n % RING[ring]}"
        where[name] = (bank, uses[bank])
        uses[bank] += 1
        seen[ring] += 1
    assert all(seen[r] % RING[r] == 0 for r in RING), seen
    first, first_uses = {}, dict.fromkeys(BANKS, 0)
    for slot in sorted(FRONT):
        for name, _ in FRONT[slot]:
            bank = where[name][0]
            first[name] = (bank, first_uses[bank])
            first_uses[bank] += 1
    last, last_uses = {}, dict.fromkeys(BANKS, 0)
    for name, _ in plan_iteration():
        if name not in first:
            bank = where[name][0]
            last[name] = (bank, last_uses[bank])
            last_uses[bank] += 1
    return where, uses, first, first_uses, last


def program(nc, a, out, h_mid, slots, consts):
    B, S, D = a["x"].shape
    E = a["ctx_1024"].shape[2]
    I = a["L1_xattn_v_gate"].shape[1]
    DC, EC = D // P, E // P
    TT = S // P
    FC = -(-I // P)
    FW = [min(P, I - f * P) for f in range(FC)]
    WHERE, USES, FIRST, FIRST_USES, LAST = place_jobs()
    PRO = {"T0": 5, "T1": 5}
    FREE0 = {"T0": 5, "T1": 5, "G0": 1, "G1": 1, "G2": 1, "O": 1}

    with ExitStack() as ctx:
        def sb(name, shape, dt=F32, c=ctx):
            return c.enter_context(nc.sbuf_tensor(name, shape, dt))

        def sem(name):
            return ctx.enter_context(nc.semaphore(name))

        ps = {n: ctx.enter_context(nc.psum_tensor(n, [P, 512], F32)) for n in BANKS}
        bank_ready = {n: sem(f"ready_{n}") for n in BANKS}
        bank_free = {n: sem(f"free_{n}") for n in BANKS}

        ident = sb("ident", [P, P])
        ident_r = sb("ident_r", [P, P], F32R)
        half_neg = sb("half_neg", [P, 1])
        N = B * S
        CH = N // P
        idx = sb("idx", [P, 2 * CH + TT], I32)
        idx_cur = {e: sb(f"idx_cur_{e}", [P, 2, TT], I32) for e in "vl"}
        counts = sb("counts", [1, 2], I32)

        phase_a = ExitStack()

        def sa(name, shape, dt=F32):
            return sb(name, shape, dt, phase_a)

        w_memT = sa("w_memT", [P, EC, D])
        w_gate = sa("w_gate", [P, 2 * DC, D])
        w_qkv = {e: sa(f"w_qkv_{e}", [P, DC, 3 * D]) for e in "lv"}
        w_dense = {e: sa(f"w_dense_{e}", [P, DC, D]) for e in "lv"}
        w_cq = sa("w_cq", [P, DC, E])
        w_ckv = sa("w_ckv", [P, EC, 2 * E])
        w_cd = sa("w_cd", [P, EC, D])
        bias_bc = sa("bias_bc", [P, D])
        nw_bc = {n: sa(f"nw_{n}", [P, D]) for n in ("norm", "ln_in", "cross")}
        cs = sa("cs", [P, TT, 2 * HD])
        pos = sa("pos", [P, TT], I32)
        posf = sa("posf", [P, 3, TT])
        posi = sa("posi", [P, TT], I32)
        identb = sa("identb", [P, P], BF16)
        tri = sa("tri", [P, 2, 512], BF16)

        off16 = sa("off16", [B, 2])
        below = sa("below", [B, B])
        cnt_f = sa("cnt_f", [1, 2])
        x_t = sa("x_t", [P, TT, D])
        c_t = sa("c_t", [P, TT, E])
        tok = sa("tok", [P, S], I32)
        mask = {e: sa(f"mask_{e}", [P, S]) for e in "vl"}
        ctT = sa("ctT", [P, EC, S])
        mp = sa("mp", [P, TT, D])
        bufA = sa("bufA", [P, DC, S])
        bufB = sa("bufB", [P, DC, S])
        qT = sa("qT", [P, DC, S])
        mc = sa("mc", [P, TT, D])
        gs = sa("gs", [P, TT, D])
        fu = sa("fu", [P, TT, D])
        x1 = sa("x1", [P, TT, D])
        p_ring = sa("p_ring", [P, 3, 512])
        pT_ring = sa("pT_ring", [P, 2, 2, 512], F16)
        q_pair = sa("q_pair", [P, 2, S], F32R)
        k_pair = sa("k_pair", [P, 2, 2, S], F32R)
        v_parts = sa("v_parts", [P, 3, TT, D], BF16)
        cv_parts = sa("cv_parts", [P, 3, TT, E], BF16)
        sq = sa("sq", [P, D], BF16)
        mx = sa("mx", [P, 30, 4])
        nm = sa("nm", [P, 30, 4])
        sums = sa("sums", [P, 5, NH])
        rinv = sa("rinv", [P, 5, NH])
        ss = sa("ss", [P, 6])
        ms = sa("ms", [P, 6])
        rs = sa("rs", [P, 6])
        h2 = sa("h2", [P, TT, D])
        ccs = sa("ccs", [P, 2, D])
        has_v = sa("has_v", [1, TT], I32)
        shared = ExitStack()
        qk = sb("qk", [P, TT, 2, D], F32, shared)
        kT = sb("kT", [P, DC, S], F32, shared)
        xn = sb("xn", [P, TT, D], F32, shared)
        shared.close()
        shared = ExitStack()
        xq_t = sb("xq", [P, TT, NH * 4 * CHD], F32R, shared)
        xk_t = sb("xk", [P, TT, NH * 4 * CHD], F32R, shared)
        xq, xk = [xq_t[:, t] for t in range(TT)], [xk_t[:, t] for t in range(TT)]
        v_rest, ao, ciT, rotA, rotB, h1 = mc, fu, bufA, gs, mp, h2
        cv_rest = mc[:, 0].rearrange("p (t e) -> p t e", t=TT)
        p0, p0T = fu[:, 0].rearrange("p (t m) -> p t m", t=TT), fu[:, 1].rearrange("p (t m) -> p t m", t=TT)
        vm16 = x1[0:B].rearrange("p t (a s) -> p (t a) s", s=S)
        ones16, tok_row = xn[0:B, 0, 0:S], xn[0:B, 0, S:2 * S]
        tok_row_i, tok16 = xn[0:B, 1, 0:S].bitcast(I32), xn[0:B, 1, S:2 * S].bitcast(I32)
        list_i, list_f = rotA[0:2 * CH, 0, 0:P].bitcast(I32), rotA[0:2 * CH, 0, P:2 * P]
        slot_i, tok_id = rotA[:, 1, 0:TT * B].bitcast(I32), rotA[:, 1, P:P + TT * B].bitcast(I32)
        gate_in = w_qkv["v"][:].rearrange("p c n -> p (c n)")[:, 0:DC * 2 * D].rearrange("p (c f) -> p c f", c=DC)
        mpT = qT
        cc, ccT = ccs[:, 0], ccs[:, 1]

        shared.close()
        phase_a.close()
        phase_b = ExitStack()

        def sbb(name, shape, dt=F32):
            return sb(name, shape, dt, phase_b)

        w_up = {e: sbb(f"w_up_{e}", [P, DC, 2, I]) for e in "vl"}
        w_dn = {e: sbb(f"w_dn_{e}", [P, FC, D]) for e in "vl"}
        nw_post = sbb("nw_post", [P, D])
        h_t = {e: sbb(f"h_t_{e}", [P, 2, TT, D]) for e in "vl"}
        mi = sbb("mi", [P, TT, D])
        miT = sbb("miT", [P, 2, DC, S])
        sg = sbb("sg", [P, 2, S])
        hh = sbb("hh", [P, 4, S])
        sqb = sbb("sqb", [P, D])
        ssb = sbb("ssb", [P, 3, TT])
        o_t = {e: sbb(f"o_t_{e}", [P, TT, D]) for e in "vl"}
        phase_b.close()

        s_w = sem("weights_in")
        s_ws = sem("wmem_in")
        s_wg = sem("wgate_in")
        s_small = sem("small_in")
        s_x = sem("x_in")
        s_cs = sem("table_in")
        s_pos = sem("pos_done")
        s_id = sem("consts_done")
        s_mask = sem("mask_done")
        s_has = sem("has_v_done")
        s_mx0 = sem("max_done_layer0")
        s_nm0 = sem("negmax_done_layer0")
        s_ri0 = sem("rinv_done_layer0")
        s_mx = sem("max_done")
        s_nm = sem("negmax_done")
        s_p = sem("probs_done")
        s_pv = sem("pv_done")
        s_hi = sem("probs_high_done")
        s_xh = sem("cross_qk_high_done")
        s_v1, s_v2, s_v3 = (sem(f"values_part{k}_done") for k in (1, 2, 3))
        s_c1, s_c2, s_c3 = (sem(f"cross_values_part{k}_done") for k in (1, 2, 3))
        s_ri = sem("rinv_done")
        s_th = sem("tanh_done")
        s_f1 = sem("gated_done")
        s_fu = sem("fused_done")
        s_ss = sem("squares_done")
        s_ms = sem("mean_done")
        s_rs = sem("rsqrt_done")
        s_x1 = sem("x1_done")
        s_xn = sem("xn_done")
        s_rot = sem("rotated_done")
        s_ci = sem("ci_done")
        s_st = sem("h_stored")
        r_in = sem("route_tokens_in")
        r_const = sem("route_consts")
        r_dve = sem("route_steps")
        r_pe = sem("route_products")
        r_sc = sem("list_scattered")
        r_back = sem("list_back")
        r_done = sem("routing_done")
        b_w = {e: sem(f"b_weights_{e}") for e in "vl"}
        b_nw = sem("b_norm_weight_in")
        b_init = sem("b_init")
        b_go = sem("pool_went_on")
        UP_N = 4

        def per_expert(what):
            return {e: sem(f"{what}_{e}") for e in "vl"}

        b_idx = per_expert("b_idx")
        b_h = per_expert("b_gathered")
        b_ss = per_expert("b_squares")
        b_ms = per_expert("b_mean")
        b_rs = per_expert("b_rsqrt")
        b_mi = per_expert("b_mi")
        b_tr = per_expert("b_turned")
        b_mit = per_expert("b_miT")
        b_up = per_expert("b_up")
        b_sg = per_expert("b_silu")
        b_hh = per_expert("b_hidden")
        b_dn = per_expert("b_down")
        b_out = per_expert("b_out")
        b_st = per_expert("b_scattered")
        N_UNITS, S_P0 = N_SELF + N_CROSS, 2
        R_SCAN, R_POS, R_SLOTS = 5, 16, 17

        def bank(job):
            return ps[WHERE[job][0]]

        def nth(job, r):
            if r is None:
                n, k = FIRST[job]
                return n, k
            n, k = LAST[job] if isinstance(r, int) and r == B - 1 else WHERE[job]
            return n, r * USES[n] + (FIRST_USES[n] + k)

        def ready(job, r):
            n, k = nth(job, r)
            return bank_ready[n], k + (PRO.get(n, 0) + 1)

        def freed(job, r):
            n, k = nth(job, r)
            return bank_free[n], k + (FREE0[n] + 1)

        def vacant(job, r):
            n, k = nth(job, r)
            return bank_free[n], k + FREE0[n]

        def free_sem(job):
            return bank_free[WHERE[job][0]]

        def ready_sem(job):
            return bank_ready[WHERE[job][0]]

        self_units = [(0, [r, r + 4, r + 8, r + 12], P) for r in range(4)]
        self_units += [(1, [8 * cp + r, 8 * cp + 4 + r], S) for r in range(4) for cp in range(2)]
        cross_units = [(t, [2 * g, 2 * g + 1], S) for g in range(PAIRS) for t in range(TT)]
        units = {SELF + i: u for i, u in enumerate(self_units)} | {CROSS + i: u for i, u in enumerate(cross_units)}

        def sum_row(u):
            return (1 if u < CROSS else 3) + units[u][0]

        def probs(u, b):
            return s_p, b * N_UNITS + (u - SELF + 1 + S_P0)

        def unit_done(s_, u, b):
            return s_, b * N_UNITS + (u - SELF + 1)

        def in_parts(x, keys, low):
            v = x.rearrange("p (h a b d) -> p h a b d", h=NH, a=2, b=2)
            return v[:, :, :, low] if keys else v[:, :, low]

        def twice(src):
            return src.rearrange("p (h d) -> p h d", d=CHD).unsqueeze(2).broadcast_to([P, NH, 2, CHD])

        UP = [ps[n] for n in ("G0", "G1", "S0", "S1")]
        DN = [ps[n] for n in ("G2", "O")]
        TB = [ps[n] for n in ("T0", "T1")]
        NT = N // S

        def tiles_of(eng, e):
            n = eng.value_load(counts[0:1, "vl".index(e):"vl".index(e) + 1], min_val=0, max_val=N)
            with eng.Fori(0, NT // 2) as i:
                for j in range(2):
                    with eng.If(n > i * (2 * S) + j * S):
                        yield i * 2 + j, j

        block = ctx.enter_context(nc.Block())
        tiled = a["x"].rearrange("b (t p) d -> b p t d", p=P)
        ctiled = a["ctx_1024"].rearrange("b (t p) d -> b p t d", p=P)
        h_rows = h_mid.rearrange("b s d -> (b s) d")
        out_rows = out.rearrange("b s d -> (b s) d")
        htiled = h_mid.rearrange("b (t p) d -> b p t d", p=P)

        @block.sync
        def _(sp):
            def load_batch(b):
                sp.dma_start(x_t[:], tiled[b]).then_inc(s_x, 16)
                sp.dma_start(c_t[:], ctiled[b]).then_inc(s_x, 16)
                sp.dma_start(tok[:], a["mask_BxS_ik0"][b].partition_broadcast(P)).then_inc(s_x, 16)

            sp.dma_start(pos[:], a["pos_1xS"].rearrange("o (t p) -> p (o t)", p=P), allow_slow_non_contiguous=True).then_inc(s_pos, 16)
            sp.dma_start(tok16, a["mask_BxS_ik0"]).then_inc(r_in, 16)
            sp.dma_start(bufA[:], a["L0_xattn_W_mem"].rearrange("(c p) e -> p c e", p=P)).then_inc(s_ws, 16)
            sp.dma_start(gate_in, a["L0_xattn_W_gate"].rearrange("(c p) f -> p c f", p=P)).then_inc(s_wg, 16)
            load_batch(0)
            for t, n in ((bias_bc, "L0_xattn_b_gate"), (nw_bc["norm"], "L0_xattn_norm_w"),
                         (nw_bc["ln_in"], "L1_xattn_ln_in_w"), (nw_bc["cross"], "L1_xattn_ln_post_cross_w")):
                sp.dma_start(t[:], a[n].partition_broadcast(P)).then_inc(s_small, 16)
            for t, n in ((w_ckv, "L1_xattn_ckv_w"), (w_qkv["l"], "L1_xattn_l_qkv"), (w_dense["l"], "L1_xattn_l_dense"),
                         (w_dense["v"], "L1_xattn_v_dense"), (w_cq, "L1_xattn_cq_w"), (w_cd, "L1_xattn_cdense_w")):
                sp.dma_start(t[:], a[n].rearrange("(c p) n -> p c n", p=P)).then_inc(s_w, 16)

            sp.wait_ge(bank_ready["T0"], PRO["T0"])
            sp.wait_ge(bank_ready["T1"], PRO["T1"])
            sp.dma_start(w_qkv["v"][:], a["L1_xattn_v_qkv"].rearrange("(c p) n -> p c n", p=P)).then_inc(s_w, 16)

            def store(b):
                sp.wait_ge(*freed("cd0", b))
                sp.wait_ge(*freed("cd1", b))
                sp.dma_start(htiled[b], h2[:]).then_inc(s_st, 16)

            with sp.Fori(0, B - 1) as b:
                sp.wait_ge(s_fu, b * 2 + 2)
                load_batch(b + 1)
                store(b)
            store(B - 1)
            sp.wait_ge(s_st, 16 * B + 16)

            sp.dma_start(nw_post[:], a["L1_xattn_ln_post_attn_w"].partition_broadcast(P)).then_inc(b_nw, 16)
            for e in "vl":
                for i, n in enumerate((f"L1_xattn_{e}_gate", f"L1_xattn_{e}_up")):
                    sp.dma_start(w_up[e][:, :, i], a[n].rearrange("(c p) n -> p c n", p=P)).then_inc(b_w[e], 16)
                dn = a[f"L1_xattn_{e}_down"]
                sp.dma_start(w_dn[e][:, 0:FC - 1], dn[0:(FC - 1) * P, :].rearrange("(c p) n -> p c n", p=P)).then_inc(b_w[e], 16)
                sp.dma_start(w_dn[e][0:FW[-1], FC - 1], dn[(FC - 1) * P:I, :]).then_inc(b_w[e], 16)

        @block.gpsimd
        def _(pool):
            nc.gpsimd.memset(ident[:], 0.0).then_inc(s_id, 1)
            nc.gpsimd.memset(half_neg[:], -0.5).then_inc(s_id, 1)
            nc.gpsimd.memset(identb[:], 0.0).then_inc(s_id, 1)
            nc.gpsimd.memset(tri[:], 0.0).then_inc(s_id, 1)
            nc.gpsimd.memset(k_pair[:].bitcast(F32), 0.0).then_inc(s_id, 1)
            for first, n in ((bank_free["G0"], 1), (bank_free["G1"], 1), (bank_free["G2"], 1),
                             (bank_free["O"], 1), (s_p, S_P0), (s_ss, 1),
                             (s_st, 16), (b_ss["v"], 1), (b_ss["l"], 1), (b_out["v"], 1), (b_out["l"], 1)):
                nc.gpsimd.nop().then_inc(first, n)
            nc.gpsimd.memset(ident_r[:].bitcast(F32), 0.0).then_inc(s_id, 1)
            pool.wait_ge(s_id, 6)
            for m in (ident, ident_r, identb):
                nc.gpsimd.affine_select(out=m[:], in_=m[:], compare_op=ALU.not_equal, fill=1.0, base=0,
                                        pattern=[[-1, P]], channel_multiplier=1).then_inc(s_id, 1)
            nc.gpsimd.affine_select(out=tri[:, 0].rearrange("p (h k) -> p h k", k=P),
                                    in_=tri[:, 0].rearrange("p (h k) -> p h k", k=P), compare_op=ALU.is_ge,
                                    fill=MASKED, base=0, pattern=[[0, 4], [-1, P]], channel_multiplier=1).then_inc(s_id, 1)
            nc.gpsimd.affine_select(out=tri[:, 1].rearrange("p (h k) -> p h k", k=S),
                                    in_=tri[:, 1].rearrange("p (h k) -> p h k", k=S), compare_op=ALU.is_ge,
                                    fill=MASKED, base=P, pattern=[[0, 2], [-1, S]], channel_multiplier=1).then_inc(s_id, 1)
            pool.wait_ge(s_pos, 17)
            for t in range(TT):
                nc.gpsimd.indirect_dma_start(cs[:, t], None, consts["rotary"],
                                             bass.IndirectOffsetOnAxis(ap=posi[:, t:t + 1], axis=0)).then_inc(s_cs, 16)

            nc.gpsimd.memset(ones16, 1.0).then_inc(r_const, 1)
            nc.gpsimd.memset(below[:], 1.0).then_inc(r_const, 1)
            nc.gpsimd.memset(idx[:], N).then_inc(r_const, 1)
            nc.gpsimd.iota(tok_row_i, pattern=[[1, S]], base=0, channel_multiplier=S).then_inc(r_const, 1)
            nc.gpsimd.iota(tok_id.rearrange("p (t b) -> p t b", t=TT), pattern=[[P, TT], [S, B]], base=0,
                           channel_multiplier=1).then_inc(r_const, 1)
            pool.wait_ge(r_const, 5)
            nc.gpsimd.affine_select(out=below[:], in_=below[:], compare_op=ALU.is_gt, fill=0.0, base=0,
                                    pattern=[[1, B]], channel_multiplier=-1).then_inc(r_const, 1)
            for k, e in enumerate("vl"):
                pool.dma_start(slots[k * N:(k + 1) * N].rearrange("(p c) o -> p (c o)", p=P), idx[:, 0:CH]) \
                    .then_inc(b_st[e], 16)
            for e in "vl":
                pool.wait_ge(b_st[e], 16)
            pool.wait_ge(r_dve, R_SLOTS)
            for c in range(TT * B):
                nc.gpsimd.indirect_dma_start(slots, bass.IndirectOffsetOnAxis(ap=slot_i[:, c:c + 1], axis=0),
                                             tok_id[:, c:c + 1], None).then_inc(r_sc, 16)
            pool.wait_ge(r_sc, 16 * TT * B)
            pool.dma_start(list_i, slots.rearrange("(c p) o -> c (p o)", p=P)).then_inc(r_back, 16)

            def rsqrt(b, n):
                pool.wait_ge(s_ms, b * 6 + n + 1)
                nc.gpsimd.tensor_tensor(rs[:, n:n + 1], ms[:, n:n + 1], half_neg[:], ALU.pow).then_inc(s_rs, 1)

            def front(c, r):
                for n in range(4):
                    rsqrt(c, n)
                for t in range(TT):
                    for j in range(2):
                        pool.wait_ge(*freed(f"{'qk'[j]}{t}", r))
                        nc.gpsimd.tensor_tensor(qk[:, t, j], rotA[:, j], rotB[:, j], ALU.add).then_inc(s_rot, 1)
                    pool.wait_ge(s_v2, c * 2 + (t + 1))
                    nc.gpsimd.tensor_tensor(v_parts[:, 2, t], v_rest[:, t], v_parts[:, 1, t], ALU.subtract).then_inc(s_v3, 1)

            def back(b):
                for n in range(4, 6):
                    rsqrt(b, n)
                pool.wait_ge(s_c2, b + 1)
                nc.gpsimd.tensor_tensor(cv_parts[:, 2], cv_rest, cv_parts[:, 1], ALU.subtract).then_inc(s_c3, 1)

            front(0, None)
            with pool.Fori(0, B - 1) as b:
                back(b)
                front(b + 1, b)
            back(B - 1)

            def rsqrt_b(e, b):
                for t in range(TT):
                    pool.wait_ge(b_ms[e], b * 2 + (t + 1))
                    nc.gpsimd.tensor_tensor(ssb[:, 2, t:t + 1], ssb[:, 1, t:t + 1], half_neg[:], ALU.pow).then_inc(b_rs[e], 1)

            def gather(e, b, buf):
                pool.wait_ge(b_idx[e], b + 1)
                pool.sem_inc(b_go, 1)
                for t in range(TT):
                    nc.gpsimd.indirect_dma_start(h_t[e][:, buf, t], None, h_rows,
                                                 bass.IndirectOffsetOnAxis(ap=idx_cur[e][:, buf, t:t + 1], axis=0),
                                                 bounds_check=N - 1, oob_is_err=False).then_inc(b_h[e], 16)

            pool.wait_ge(r_done, 1)
            stored = [pool.snap((pool.value_load(counts[0:1, k:k + 1], min_val=0, max_val=N) + (S - 1)) // S * 32 + 16)
                      for k in range(2)]
            pool.wait_ge(b_init, 2)
            for e in "vl":
                gather(e, 0, 0)
                rsqrt_b(e, 0)
                for b, j in tiles_of(pool, e):
                    pool.wait_ge(b_out[e], b * 2 + 1)
                    gather(e, b + 1, 1 - j)
                    rsqrt_b(e, b + 1)
                    pool.wait_ge(b_out[e], b * 2 + 3)
                    pool.sem_inc(b_go, 1)
                    for t in range(TT):
                        nc.gpsimd.indirect_dma_start(out_rows, bass.IndirectOffsetOnAxis(ap=idx_cur[e][:, j, t:t + 1], axis=0),
                                                     o_t[e][:, t], None, bounds_check=N - 1, oob_is_err=False) \
                            .then_inc(b_st[e], 16)
            for e, n in zip("vl", stored):
                pool.wait_ge(b_st[e], n)
            pool.wait_ge(r_done, 1)

        @block.scalar
        def _(act):
            def copy(dst, job, b, view=None):
                act.wait_ge(*ready(job, b))
                src = bank(job)[:] if view is None else view(bank(job))
                nc.scalar.activation(dst, src, ACT.Copy).then_inc(free_sem(job), 1)

            def square(src, n, b):
                act.wait_ge(s_ss, b * 6 + (n + 1))
                nc.scalar.activation(sq[:], src, ACT.Square, accum_out=ss[:, n:n + 1]).then_inc(s_ss, 1)

            def exps(u, b):
                act.wait_ge(*unit_done(s_nm, u, b))
                if u >= SELF + 3:
                    act.wait_ge(*ready(f"t{u - 3}", b))
                t, heads, w = units[u]
                scale = (HD if u < CROSS else CHD) ** -0.5
                for j, h in enumerate(heads):
                    e = nc.scalar.activation(p_ring[:, u % 3, j * w:(j + 1) * w], bank(f"s{u}")[:, j * w:(j + 1) * w],
                                             ACT.Exp, bias=nm[:, u, j:j + 1], scale=scale,
                                             accum_out=sums[:, sum_row(u), h:h + 1])
                e.then_inc(s_p, 1)

            def expand_high(dst, job, part, keys, b):
                act.wait_ge(*ready(job, b))
                nc.scalar.activation(in_parts(dst, keys, 0), twice(bank(job)[:, part * E:(part + 1) * E]), ACT.Copy) \
                    .then_inc(s_xh, 1)

            def high(u, b):
                act.wait_ge(*ready(f"t{u}", b))
                if u >= SELF + 2:
                    act.wait_ge(*unit_done(s_pv, u - 2, b))
                nc.scalar.activation(pT_ring[:, u % 2, 0], bank(f"t{u}")[:], ACT.Copy).then_inc(s_hi, 1)

            def chunks(k, n=DC):
                return k[:].rearrange("p (c m) -> p c m", c=n)

            def front(c, r, slot):
                if slot == 0:
                    copy(ctT[:], "ctT", r, lambda k: chunks(k, EC))
                    copy(bufA[:, :, P:S], "xT1", r, chunks)
                if slot == 1:
                    copy(mp[:, 0], "mp0", r)
                    copy(mp[:, 1], "mp1", r)
                if slot == 2:
                    copy(mpT[:, 0:2], "mpT0", r, lambda k: chunks(k, 2))
                    copy(mpT[:, 2:4], "mpT1", r, lambda k: chunks(k, 2))
                if slot == 4:
                    act.wait_ge(s_nm0, c * 2 + TT)
                    for t in range(TT):
                        e = nc.scalar.activation(p0[:, t], bank("l0s")[:, t * S:(t + 1) * S], ACT.Exp, bias=nm[:, t, 0:1],
                                                 scale=D ** -0.5, accum_out=sums[:, 0, t:t + 1])
                    e.then_inc(free_sem("l0s"), 1)
                if slot == 7:
                    copy(bufB[:, :, 0:P], "mcT0", r, chunks)
                    copy(bufB[:, :, P:S], "mcT1", r, chunks)
                if slot in (8, 9):
                    t = slot - 8
                    act.wait_ge(*freed(f"gate{t}", r))
                    nc.scalar.activation(gs[:, t], gs[:, t], ACT.Tanh, scale=0.5).then_inc(s_th, 1)
                if slot == 11:
                    for t in range(TT):
                        act.wait_ge(s_fu, c * 2 + (t + 1))
                        square(fu[:, t], t, c)
                if slot == 13:
                    for t in range(TT):
                        act.wait_ge(s_x1, c * 2 + (t + 1))
                        square(x1[:, t], 2 + t, c)
                if slot in (16, 19):
                    t = int(slot == 19)
                    act.wait_ge(*ready(f"v{t}", r))
                    nc.scalar.activation(v_parts[:, 0, t], bank(f"v{t}")[:], ACT.Copy).then_inc(s_v1, 1)
                if slot == 20:
                    for t in range(TT):
                        for j, x in enumerate((qT, kT)):
                            copy(x[:, :, t * P:(t + 1) * P], f"{'qk'[j]}T{t}", r, chunks)

            def element(b, has_next):
                for i in range(SELF, CROSS + 3):
                    if SELF <= i - 2 < CROSS:
                        high(i - 2, b)
                    if i < CROSS:
                        exps(i, b)
                    if i == 12:
                        act.wait_ge(*freed("dense0", b))
                        square(h1[:, 0], 4, b)
                expand_high(xk[0], "ck", 0, True, b)
                act.wait_ge(*freed("dense1", b))
                square(h1[:, 1], 5, b)
                act.wait_ge(*ready("cv", b))
                nc.scalar.activation(cv_parts[:, 0], chunks(bank("cv"), TT), ACT.Copy).then_inc(s_c1, 1)
                act.wait_ge(*ready("ciT1", b))
                expand_high(xk[1], "ck", 1, True, b)
                for t in range(TT):
                    expand_high(xq[t], f"cq{t}", 0, False, b)
                for slot in range(SLOTS + 2):
                    if 0 <= slot - 2 < N_CROSS:
                        high(CROSS + slot - 2, b)
                    if slot < N_CROSS:
                        exps(CROSS + slot, b)
                    if has_next:
                        front(b + 1, b, slot)
                    if slot == SLOTS:
                        copy(ccT.rearrange("p (c m) -> p c m", c=EC), "ccT", b, lambda k: chunks(k, EC))

            for slot in range(SLOTS + 2):
                front(0, None, slot)
            with act.Fori(0, B - 1) as b:
                element(b, True)
            element(B - 1, False)

            def square_b(e, b, buf):
                act.wait_ge(b_h[e], b * 32 + 32)
                for t in range(TT):
                    act.wait_ge(b_ss[e], b * 2 + (t + 1))
                    nc.scalar.activation(sqb[:], h_t[e][:, buf, t], ACT.Square, accum_out=ssb[:, 0, t:t + 1]).then_inc(b_ss[e], 1)

            act.wait_ge(r_done, 1)
            for e in "vl":
                square_b(e, 0, 0)
                for b, j in tiles_of(act, e):
                    for u in range(FC):
                        if u == MID:
                            square_b(e, b + 1, 1 - j)
                        act.wait_ge(b_up[e], b * FC + (u + 1))
                        if u >= 2:
                            act.wait_ge(b_hh[e], b * FC + (u - 1))
                        nc.scalar.activation(sg[0:FW[u], u % 2], UP[u % UP_N][0:FW[u], 0:S], ACT.Silu).then_inc(b_sg[e], 1)

        @block.vector
        def _(dve):
            dve.wait_ge(s_pos, 16)
            nc.vector.tensor_copy(posf[:, 0], pos[:]).then_inc(s_mx, 1)
            dve.wait_ge(s_mx, 1)
            nc.vector.tensor_scalar(posf[:, 1], posf[:, 0], 0.0, float(S), ALU.is_lt, ALU.mult).then_inc(s_mx, 1)
            dve.wait_ge(s_mx, 2)
            nc.vector.tensor_tensor(posf[:, 2], posf[:, 0], posf[:, 1], ALU.add).then_inc(s_mx, 1)
            dve.wait_ge(s_mx, 3)
            nc.vector.tensor_scalar(posi[:], posf[:, 2], 0.0, float(S - 1), ALU.max, ALU.min).then_inc(s_pos, 1)
            for c in range(EC):
                dve.wait_ge(bank_ready[f"T{c}"], 1)
                nc.vector.tensor_copy(w_memT[:, c], ps[f"T{c}"][:]).then_inc(bank_free[f"T{c}"], 1)
            for f in range(2 * DC):
                n = f"T{f % 2}"
                dve.wait_ge(bank_ready[n], 2 + f // 2)
                nc.vector.tensor_copy(w_gate[:, f], ps[n][:]).then_inc(bank_free[n], 1)
            MX0 = 3

            steps = [0]

            def step(ins):
                steps[0] += 1
                ins.then_inc(r_dve, 1)
                dve.wait_ge(r_dve, steps[0])

            dve.wait_ge(r_in, 16)
            dve.wait_ge(r_const, 6)
            step(nc.vector.tensor_scalar(vm16[:, 0], tok16, 1.0, None, ALU.is_equal))
            step(nc.vector.memset(vm16[:, 1, S - 1:S], 0.0))
            step(nc.vector.tensor_tensor(vm16[:, 1, 0:S - 1], vm16[:, 0, 0:S - 1], vm16[:, 0, 1:S], ALU.mult))
            step(nc.vector.tensor_tensor_scan(vm16[:, 2], ones16, vm16[:, 1], 0.0, ALU.mult, ALU.add))
            step(nc.vector.tensor_copy(tok_row, tok_row_i))
            assert steps[0] == R_SCAN
            dve.wait_ge(r_pe, 1)
            step(nc.vector.tensor_copy(off16[:, 0:1], ps["O"][0:B, 0:1]))
            step(nc.vector.tensor_copy(cnt_f[:, 0:1], ps["O"][0:1, 1:2]))
            step(nc.vector.tensor_scalar(cnt_f[:, 1:2], cnt_f[:, 0:1], -1.0, float(N), ALU.mult, ALU.add))
            step(nc.vector.tensor_copy(counts[:], cnt_f[:]))
            step(nc.vector.tensor_scalar(vm16[:, 3], vm16[:, 2], off16[:, 0:1], None, ALU.add))
            step(nc.vector.tensor_tensor(tok_row, tok_row, vm16[:, 3], ALU.subtract))
            step(nc.vector.tensor_scalar(tok_row, tok_row, float(N), None, ALU.add))
            step(nc.vector.tensor_scalar(vm16[:, 3], vm16[:, 3], -1.0, None, ALU.add))
            step(nc.vector.tensor_tensor(vm16[:, 3], vm16[:, 3], tok_row, ALU.subtract))
            step(nc.vector.tensor_tensor(vm16[:, 3], vm16[:, 3], vm16[:, 1], ALU.mult))
            step(nc.vector.tensor_tensor(vm16[:, 3], vm16[:, 3], tok_row, ALU.add))
            assert steps[0] == R_POS
            dve.wait_ge(r_pe, 2)
            step(nc.vector.tensor_copy(slot_i, ps["O"][:, 0:TT * B]))
            assert steps[0] == R_SLOTS
            dve.wait_ge(r_back, 16)
            step(nc.vector.tensor_copy(list_f, list_i))
            dve.wait_ge(r_pe, 3)
            nc.vector.tensor_copy(idx[:, 0:2 * CH], ps["O"][:, 0:2 * CH]).then_inc(r_done, 1)

            def masks(b):
                eq, mv, ml = mask["l"], mask["v"], mask["l"]
                nc.vector.tensor_scalar(eq[:], tok[:], 1.0, None, ALU.is_equal).then_inc(s_mask, 1)
                nc.vector.memset(mv[:, S - 1:S], 0.0).then_inc(s_mask, 1)
                dve.wait_ge(s_mask, b * 4 + 2)
                nc.vector.tensor_tensor(mv[:, 0:S - 1], eq[:, 0:S - 1], eq[:, 1:S], ALU.mult).then_inc(s_mask, 1)
                dve.wait_ge(s_mask, b * 4 + 3)
                nc.vector.tensor_scalar(ml[:], mv[:], -1.0, 1.0, ALU.mult, ALU.add).then_inc(s_mask, 1)

            def copy(dst, job, b, view=None):
                dve.wait_ge(*ready(job, b))
                src = bank(job)[:] if view is None else view(bank(job))
                nc.vector.tensor_copy(dst, src).then_inc(free_sem(job), 1)

            def maxima(u, b):
                nh, w = len(units[u][1]), units[u][2]
                scale = (HD if u < CROSS else CHD) ** -0.5
                dve.wait_ge(*ready(f"s{u}", b))
                nc.vector.tensor_reduce(mx[:, u, 0:nh], bank(f"s{u}")[:, 0:nh * w].rearrange("p (h k) -> p h k", k=w),
                                        AX_X, ALU.max).then_inc(s_mx, 1)
                s_, v = unit_done(s_mx, u, b)
                dve.wait_ge(s_, v + MX0)
                nc.vector.tensor_scalar(nm[:, u, 0:nh], mx[:, u, 0:nh], -scale, P_LIFT, ALU.mult, ALU.add).then_inc(s_nm, 1)

            def low(u, b):
                dve.wait_ge(*unit_done(s_hi, u, b))
                nc.vector.tensor_tensor(pT_ring[:, u % 2, 1], bank(f"t{u}")[:], pT_ring[:, u % 2, 0], ALU.subtract) \
                    .then_inc(free_sem(f"t{u}"), 1)

            def mean(b, n):
                dve.wait_ge(s_ss, b * 6 + (n + 2))
                nc.vector.tensor_scalar(ms[:, n:n + 1], ss[:, n:n + 1], 1.0 / D, EPS, ALU.mult, ALU.add).then_inc(s_ms, 1)

            def scaled(b, n, dst, src, w, done):
                dve.wait_ge(s_rs, b * 6 + n + 1)
                nc.vector.scalar_tensor_tensor(out=dst, in0=src, scalar=rs[:, n:n + 1], in1=w[:], op0=ALU.mult,
                                               op1=ALU.mult).then_inc(done, 1)

            def split_experts(job, t, b):
                dve.wait_ge(*ready(job, b))
                src = bank(job)[:].rearrange("p (c m) -> p c m", c=DC)
                for buf, e in ((bufA, "v"), (bufB, "l")):
                    m = mask[e][:, t * P:(t + 1) * P].unsqueeze(1).broadcast_to([P, DC, P])
                    o = nc.vector.tensor_tensor(buf[:, :, t * P:(t + 1) * P], src, m, ALU.mult)
                o.then_inc(free_sem(job), 1)

            def rotary(job, j, c, r):
                t = j // 2
                dve.wait_ge(*ready(job, r))
                if j >= 2:
                    dve.wait_ge(s_rot, c * 4 + (j - 1))
                src = bank(job)[:].rearrange("p (h a d) -> p h a d", h=NH, a=2)
                co = cs[:, t, 0:HD].unsqueeze(1).broadcast_to([P, NH, HD])
                si = cs[:, t, HD:2 * HD].rearrange("p (a d) -> p a d", a=2)
                nc.vector.tensor_tensor(rotA[:, j % 2].rearrange("p (h d) -> p h d", h=NH),
                                        bank(job)[:].rearrange("p (h d) -> p h d", h=NH), co, ALU.mult)
                outB = rotB[:, j % 2].rearrange("p (h a d) -> p h a d", h=NH, a=2)
                for k in range(2):
                    o = nc.vector.tensor_tensor(outB[:, :, k], src[:, :, 1 - k],
                                                si[:, k].unsqueeze(1).broadcast_to([P, NH, HD // 2]), ALU.mult)
                o.then_inc(free_sem(job), 1)

            def chunks(k, n=DC):
                return k[:].rearrange("p (c m) -> p c m", c=n)

            def pair(g, b):
                job = f"x{g}"
                dve.wait_ge(*ready(job, b))
                src = bank(job)[:].bitcast(F32R)
                nc.vector.tensor_copy(q_pair[:, g % 2], src[:, 0:S])
                for k in range(2):
                    rows = slice(k * 64, (k + 1) * 64)
                    o = nc.vector.tensor_copy(k_pair[rows, g % 2, k], src[rows, S:2 * S])
                o.then_inc(free_sem(job), 1)

            def attended(b, t):
                last_unit = SELF + (3, N_SELF - 1)[t]
                dve.wait_ge(*probs(last_unit, b))
                nc.vector.reciprocal(rinv[:, 1 + t], sums[:, 1 + t]).then_inc(s_ri, 1)
                dve.wait_ge(s_ri, b * 4 + (t + 1))
                dve.wait_ge(*unit_done(s_pv, last_unit, b))
                nc.vector.tensor_tensor(ao[:, t].rearrange("p (h d) -> p h d", h=NH),
                                        bank(f"o{t}")[:].rearrange("p (h d) -> p h d", h=NH),
                                        rinv[:, 1 + t].unsqueeze(2).broadcast_to([P, NH, HD]), ALU.mult) \
                    .then_inc(free_sem(f"o{t}"), 1)

            def residual(b, t):
                if t == 0:
                    dve.wait_ge(s_st, b * 16 + 16)
                dve.wait_ge(*ready(f"dense{t}", b))
                nc.vector.tensor_tensor(h1[:, t], bank(f"dense{t}")[:], x1[:, t], ALU.add) \
                    .then_inc(free_sem(f"dense{t}"), 1)

            def front(c, r, slot):
                if slot == 0:
                    dve.wait_ge(s_x, c * 48 + 48)
                    masks(c)
                    copy(bufA[:, :, 0:P], "xT0", r, chunks)
                    nc.vector.tensor_reduce(has_v[:], mask["v"][0:1].rearrange("o (t p) -> o t p", p=P), AX_X, ALU.max) \
                        .then_inc(s_has, 1)
                if slot == 3:
                    dve.wait_ge(*ready("l0s", r))
                    for t in range(TT):
                        nc.vector.tensor_reduce(mx[:, t, 0:1], bank("l0s")[:, t * S:(t + 1) * S], AX_X, ALU.max) \
                            .then_inc(s_mx0, 1)
                        dve.wait_ge(s_mx0, c * 2 + (t + 1))
                        nc.vector.tensor_scalar(nm[:, t, 0:1], mx[:, t, 0:1], -D ** -0.5, None, ALU.mult).then_inc(s_nm0, 1)
                if slot == 5:
                    for t in range(TT):
                        dve.wait_ge(*ready(f"pT{t}", r))
                        nc.vector.tensor_copy(p0T[:, t], bank(f"pT{t}")[:, 0:S]).then_inc(free_sem(f"pT{t}"), 1)
                    nc.vector.reciprocal(rinv[:, 0, 0:TT], sums[:, 0, 0:TT]).then_inc(s_ri0, 1)
                if slot == 6:
                    dve.wait_ge(s_ri0, c + 1)
                    for t in range(TT):
                        dve.wait_ge(*ready(f"mc{t}", r))
                        nc.vector.tensor_scalar(mc[:, t], bank(f"mc{t}")[:], rinv[:, 0, t:t + 1], None, ALU.mult) \
                            .then_inc(free_sem(f"mc{t}"), 1)
                if slot in (8, 9):
                    t = slot - 8
                    dve.wait_ge(*ready(f"gate{t}", r))
                    nc.vector.tensor_tensor(gs[:, t], bank(f"gate{t}")[:], bias_bc[:], ALU.add) \
                        .then_inc(free_sem(f"gate{t}"), 1)
                if slot == 10:
                    for t in range(TT):
                        dve.wait_ge(s_th, c * 2 + (t + 1))
                        nc.vector.scalar_tensor_tensor(out=gs[:, t], in0=gs[:, t], scalar=1.0, in1=mc[:, t], op0=ALU.add,
                                                       op1=ALU.mult).then_inc(s_f1, 1)
                    for t in range(TT):
                        dve.wait_ge(s_f1, c * 2 + (t + 1))
                        nc.vector.scalar_tensor_tensor(out=fu[:, t], in0=gs[:, t], scalar=0.5, in1=x_t[:, t], op0=ALU.mult,
                                                       op1=ALU.add).then_inc(s_fu, 1)
                if slot == 11:
                    for t in range(TT):
                        mean(c, t)
                if slot == 12:
                    for t in range(TT):
                        scaled(c, t, x1[:, t], fu[:, t], nw_bc["norm"], s_x1)
                if slot == 13:
                    for t in range(TT):
                        mean(c, 2 + t)
                if slot == 14:
                    for t in range(TT):
                        scaled(c, 2 + t, xn[:, t], x1[:, t], nw_bc["ln_in"], s_xn)
                if slot == 15:
                    for t in range(TT):
                        split_experts(f"xnT{t}", t, r)
                if slot in (16, 19):
                    for j, job in enumerate(("q0", "k0") if slot == 16 else ("q1", "k1")):
                        rotary(job, j + (slot == 19) * 2, c, r)
                    t = int(slot == 19)
                    dve.wait_ge(s_v1, c * 2 + (t + 1))
                    nc.vector.tensor_tensor(v_rest[:, t], bank(f"v{t}")[:], v_parts[:, 0, t], ALU.subtract) \
                        .then_inc(free_sem(f"v{t}"), 1)
                    dve.wait_ge(*freed(f"v{t}", r))
                    nc.vector.tensor_scalar(v_parts[:, 1, t], v_rest[:, t], 0.0, None, ALU.add).then_inc(s_v2, 1)

            def element(b, has_next):
                for i in range(SELF, CROSS + 3):
                    if i < CROSS:
                        maxima(i, b)
                    if SELF <= i - 2 < CROSS:
                        low(i - 2, b)
                    if i == 8:
                        attended(b, 0)
                    if i == 9:
                        split_experts("aoT0", 0, b)
                    if i == 11:
                        residual(b, 0)
                    if i == 13:
                        mean(b, 4)
                    if i == 14:
                        scaled(b, 4, xn[:, 0], h1[:, 0], nw_bc["cross"], s_ci)
                    if i == 15:
                        copy(ciT[:, :, 0:P], "ciT0", b, chunks)
                attended(b, 1)
                split_experts("aoT1", 1, b)
                residual(b, 1)
                mean(b, 5)
                dve.wait_ge(s_c1, b + 1)
                nc.vector.tensor_tensor(cv_rest, chunks(bank("cv"), TT), cv_parts[:, 0], ALU.subtract).then_inc(free_sem("cv"), 1)
                scaled(b, 5, xn[:, 1], h1[:, 1], nw_bc["cross"], s_ci)
                dve.wait_ge(*freed("cv", b))
                nc.vector.tensor_scalar(cv_parts[:, 1], cv_rest, 0.0, None, ALU.add).then_inc(s_c2, 1)
                copy(ciT[:, :, P:S], "ciT1", b, chunks)
                for n, (dst, job, part) in enumerate(((xk[0], "ck", 0), (xk[1], "ck", 1), (xq[0], "cq0", 0), (xq[1], "cq1", 0))):
                    dve.wait_ge(s_xh, b * 4 + (2 if n < 2 else n + 1))
                    o = nc.vector.tensor_tensor(in_parts(dst, n < 2, 1), twice(bank(job)[:, part * E:(part + 1) * E]),
                                                in_parts(dst, n < 2, 0), ALU.subtract)
                    if n > 0:
                        o.then_inc(free_sem(job), 1)
                pair(0, b)
                for slot in range(SLOTS + 2):
                    if slot < N_CROSS:
                        maxima(CROSS + slot, b)
                    if 0 <= slot - 2 < N_CROSS:
                        low(CROSS + slot - 2, b)
                    if CROSS + slot in PAIR_AHEAD:
                        pair(slot // 2 + 1, b)
                    if slot == SLOTS:
                        dve.wait_ge(*probs(END - 1, b))
                        nc.vector.reciprocal(rinv[:, 3:5], sums[:, 3:5]).then_inc(s_ri, 2)
                        dve.wait_ge(s_ri, b * 4 + 4)
                        dve.wait_ge(*unit_done(s_pv, END - 1, b))
                        nc.vector.tensor_tensor(cc.rearrange("p (h d) -> p h d", d=CHD),
                                                bank("o2")[:].rearrange("p (h d) -> p h d", d=CHD),
                                                rinv[:, 3:5].rearrange("p t h -> p (t h)").unsqueeze(2).broadcast_to([P, 2 * NH, CHD]),
                                                ALU.mult).then_inc(free_sem("o2"), 1)
                    if has_next:
                        front(b + 1, b, slot)
                for t in range(TT):
                    dve.wait_ge(*ready(f"cd{t}", b))
                    nc.vector.tensor_tensor(h2[:, t], bank(f"cd{t}")[:], h1[:, t], ALU.add).then_inc(free_sem(f"cd{t}"), 1)

            dve.wait_ge(s_small, 64)
            dve.wait_ge(s_cs, 32)
            dve.wait_ge(s_id, 11)
            for slot in range(SLOTS + 2):
                front(0, None, slot)
            with dve.Fori(0, B - 1) as b:
                element(b, True)
            element(B - 1, False)

            dve.wait_ge(s_st, 16 * B + 16)
            for e in "vl":
                nc.vector.memset(h_t[e][:], 0.0).then_inc(b_init, 1)
            dve.wait_ge(b_nw, 16)

            def indices(e, b, buf):
                k = b * 2 + CH * "vl".index(e)
                nc.vector.tensor_scalar(idx_cur[e][:, buf], idx[:, bass.ds(k, TT)], 0.0, None, ALU.add).then_inc(b_idx[e], 1)

            def norm_b(e, b, buf):
                for t in range(TT):
                    dve.wait_ge(b_ss[e], b * 2 + (t + 2))
                    nc.vector.tensor_scalar(ssb[:, 1, t:t + 1], ssb[:, 0, t:t + 1], 1.0 / D, EPS, ALU.mult, ALU.add) \
                        .then_inc(b_ms[e], 1)
                for t in range(TT):
                    dve.wait_ge(b_rs[e], b * 2 + (t + 1))
                    nc.vector.scalar_tensor_tensor(out=mi[:, t], in0=h_t[e][:, buf, t], scalar=ssb[:, 2, t:t + 1],
                                                   in1=nw_post[:], op0=ALU.mult, op1=ALU.mult).then_inc(b_mi[e], 1)

            def turned_b(e, b, buf):
                for t in range(TT):
                    dve.wait_ge(b_tr[e], b * 2 + (t + 1))
                    nc.vector.tensor_copy(miT[:, buf, :, t * P:(t + 1) * P], TB[t][:].rearrange("p (c m) -> p c m", c=DC)) \
                        .then_inc(b_mit[e], 1)

            for e in "vl":
                nc.vector.tensor_scalar(idx_cur[e][:, 0], idx[:, CH * "vl".index(e):CH * "vl".index(e) + TT], 0.0, None,
                                        ALU.add).then_inc(b_idx[e], 1)
                norm_b(e, 0, 0)
                turned_b(e, 0, 0)
                for b, j in tiles_of(dve, e):
                    dve.wait_ge(b_st[e], b * 32 + 16)
                    indices(e, b + 1, 1 - j)
                    for u in range(FC):
                        if u == MID:
                            norm_b(e, b + 1, 1 - j)
                        if u == MID + 3:
                            turned_b(e, b + 1, 1 - j)
                        dve.wait_ge(b_sg[e], b * FC + (u + 1))
                        if u >= 4:
                            dve.wait_ge(b_dn[e], b * FC + (u - 3))
                        nc.vector.tensor_tensor(hh[0:FW[u], u % 4], UP[u % UP_N][0:FW[u], S:2 * S], sg[0:FW[u], u % 2], ALU.mult) \
                            .then_inc(b_hh[e], 1)
                    dve.wait_ge(b_dn[e], b * FC + FC)
                    for t in range(TT):
                        nc.vector.tensor_tensor(o_t[e][:, t], DN[t][:], h_t[e][:, j, t], ALU.add).then_inc(b_out[e], 1)

        @block.tensor
        def _(pe):
            pe.wait_ge(s_id, 11)
            pe.wait_ge(s_ws, 16)
            for e in range(EC):
                for d in range(DC):
                    m = nc.tensor.transpose(ps[f"T{e}"][:, d * P:(d + 1) * P], bufA[:, d, e * P:(e + 1) * P], ident[:])
                m.then_inc(bank_ready[f"T{e}"], 1)
            pe.wait_ge(s_wg, 16)
            for f in range(2 * DC):
                n = f"T{f % 2}"
                pe.wait_ge(bank_free[n], 1 + f // 2)
                for d in range(DC):
                    m = nc.tensor.transpose(ps[n][:, d * P:(d + 1) * P], gate_in[:, d, f * P:(f + 1) * P], ident[:])
                m.then_inc(bank_ready[n], 1)

            pe.wait_ge(r_dve, R_SCAN)
            nc.tensor.matmul(ps["O"][0:B, 0:1], below[:], vm16[:, 2, S - 1:S], start=True, stop=True)
            nc.tensor.matmul(ps["O"][0:1, 1:2], vm16[:, 2, S - 1:S], ones16[:, 0:1], start=True, stop=True).then_inc(r_pe, 1)
            pe.wait_ge(r_dve, R_POS)
            for t in range(TT):
                m = nc.tensor.transpose(ps["O"][:, t * B:(t + 1) * B], vm16[:, 3, t * P:(t + 1) * P], ident[0:B, 0:B])
            m.then_inc(r_pe, 1)
            pe.wait_ge(r_dve, R_SLOTS + 1)
            nc.tensor.transpose(ps["O"][:, 0:2 * CH], list_f, ident[0:2 * CH, 0:2 * CH]).then_inc(r_pe, 1)

            def transposes(job, b, blocks):
                pe.wait_ge(*vacant(job, b))
                for i, src in enumerate(blocks):
                    m = nc.tensor.transpose(bank(job)[:, i * P:(i + 1) * P], src, ident[:])
                m.then_inc(ready_sem(job), 1)

            def gemm(job, b, dst, pairs, last=True):
                for i, (l, r) in enumerate(pairs):
                    m = nc.tensor.matmul(dst, l, r, start=(i == 0), stop=(i == len(pairs) - 1))
                if last:
                    m.then_inc(ready_sem(job), 1)

            def tiles(x, t, n=DC):
                return [x[:, t, c * P:(c + 1) * P] for c in range(n)]

            def scores(u, b):
                s_, v = probs(u, b)
                pe.wait_ge(s_, v - 2)
                t, heads, w = units[u]
                s = bank(f"s{u}")
                if u >= CROSS and t == 0:
                    pe.wait_ge(*freed(f"x{heads[0] // 2}", b))
                if u < CROSS:
                    nc.tensor.matmul(s[:], identb[:], tri[:, t], start=True, stop=True, skip_group_check=True)
                for j, h in enumerate(heads):
                    if u < CROSS:
                        c, r = h // 4, (h % 4) * 32
                        l, k = qT[r:r + 32, c, t * P:(t + 1) * P], kT[r:r + 32, c, 0:w]
                    else:
                        g = h // 2 % 2
                        l, k = q_pair[:, g, t * P:(t + 1) * P], k_pair[:, g, h % 2]
                    m = nc.tensor.matmul(s[:, j * w:(j + 1) * w], l, k, start=(u >= CROSS), stop=True,
                                         skip_group_check=True)
                m.then_inc(ready_sem(f"s{u}"), 1)

            def turn_pair(g, b):
                job = f"x{g}"
                pe.wait_ge(*vacant(job, b))
                for i, src in enumerate(xq + xk):
                    m = nc.tensor.transpose(bank(job)[:, i * P:(i + 1) * P].bitcast(F32R), src[:, g * P:(g + 1) * P],
                                            ident_r[:])
                m.then_inc(ready_sem(job), 1)

            def turn(u, b):
                pe.wait_ge(*probs(u, b))
                transposes(f"t{u}", b, [p_ring[:, u % 3, i * P:(i + 1) * P] for i in range(4)])

            def values(u, b):
                t, heads, w = units[u]
                cross = u >= CROSS
                o = "o2" if cross else f"o{t}"
                if u in (SELF, SELF + 4, CROSS):
                    pe.wait_ge(*vacant(o, b))
                pe.wait_ge(*freed(f"t{u}", b))
                v, d = (cv_parts, CHD) if cross else (v_parts, HD)
                for j, h in enumerate(heads):
                    col = h * d + (t * E if cross else 0)
                    terms = [(k, *parts) for k in range(w // P) for parts in PARTS]
                    for n, (k, pp, vp) in enumerate(terms):
                        i = j * (w // P) + k
                        m = nc.tensor.matmul(bank(o)[:, col:col + d], pT_ring[:, u % 2, pp, i * P:(i + 1) * P],
                                             v[:, vp, k, h * d:(h + 1) * d], start=(n == 0), stop=(n == len(terms) - 1))
                m.then_inc(s_pv, 1)

            def expert_gemms(t, r, inputs, jobs):
                def products(experts):
                    pe.wait_ge(*freed(inputs, r))
                    for job, w, cols in jobs:
                        pe.wait_ge(*vacant(job, r))
                        gemm(job, r, bank(job)[:], [(buf[:, c, t * P:(t + 1) * P], w[e][:, c, cols])
                                                    for buf, e in ((bufB, "l"), (bufA, "v"))[:experts] for c in range(DC)])

                n = pe.value_load(has_v[0:1, t:t + 1], min_val=0, max_val=1)
                with pe.If(n > 0):
                    products(2)
                with pe.Else():
                    products(1)

            def dense(t, b):
                expert_gemms(t, b, f"aoT{t}", [(f"dense{t}", w_dense, slice(0, D))])

            def turn_inputs(t, b):
                pe.wait_ge(s_ci, b * 2 + (t + 1))
                transposes(f"ciT{t}", b, tiles(xn, t))

            def front(c, r, slot):
                if slot == 0:
                    pe.wait_ge(s_x, c * 48 + 48)
                    transposes("ctT", r, [c_t[:, m, e * P:(e + 1) * P] for e in range(EC) for m in range(TT)])
                    for t in range(TT):
                        transposes(f"xT{t}", r, tiles(x_t, t))
                if slot == 1:
                    pe.wait_ge(*freed("ctT", r))
                    for m in range(TT):
                        pe.wait_ge(*vacant(f"mp{m}", r))
                        gemm(f"mp{m}", r, bank(f"mp{m}")[:], [(ctT[:, e, m * P:(m + 1) * P], w_memT[:, e]) for e in range(EC)])
                if slot == 2:
                    pe.wait_ge(*freed("mp0", r))
                    pe.wait_ge(*freed("mp1", r))
                    for k in range(2):
                        transposes(f"mpT{k}", r, [mp[:, m, (2 * k + d) * P:(2 * k + d + 1) * P] for d in range(2) for m in range(TT)])
                if slot == 3:
                    for job in ("xT0", "xT1", "mpT0", "mpT1"):
                        pe.wait_ge(*freed(job, r))
                    pe.wait_ge(*vacant("l0s", r))
                    for t in range(TT):
                        gemm("l0s", r, bank("l0s")[:, t * S:(t + 1) * S],
                             [(bufA[:, d, t * P:(t + 1) * P], mpT[:, d]) for d in range(DC)], last=(t == TT - 1))
                if slot == 5:
                    pe.wait_ge(*freed("l0s", r))
                    for t in range(TT):
                        transposes(f"pT{t}", r, [p0[:, t, m * P:(m + 1) * P] for m in range(TT)])
                if slot == 6:
                    for t in range(TT):
                        pe.wait_ge(*freed(f"pT{t}", r))
                        pe.wait_ge(*vacant(f"mc{t}", r))
                        gemm(f"mc{t}", r, bank(f"mc{t}")[:], [(p0T[:, t, m * P:(m + 1) * P], mp[:, m]) for m in range(TT)])
                if slot == 7:
                    for t in range(TT):
                        pe.wait_ge(*freed(f"mc{t}", r))
                        transposes(f"mcT{t}", r, tiles(mc, t))
                if slot in (8, 9):
                    t = slot - 8
                    pe.wait_ge(*freed(f"mcT{t}", r))
                    pe.wait_ge(*vacant(f"gate{t}", r))
                    gemm(f"gate{t}", r, bank(f"gate{t}")[:],
                         [((bufA, bufB)[d // DC][:, d % DC, t * P:(t + 1) * P], w_gate[:, d]) for d in range(2 * DC)])
                if slot == 15:
                    pe.wait_ge(s_has, c + 1)
                    for t in range(TT):
                        pe.wait_ge(s_xn, c * 2 + (t + 1))
                        transposes(f"xnT{t}", r, tiles(xn, t))
                if slot in (16, 19):
                    t = int(slot == 19)
                    expert_gemms(t, r, f"xnT{t}", [(f"{j}{t}", w_qkv, slice(n * D, (n + 1) * D)) for n, j in enumerate("qkv")])
                if slot == 20:
                    for t in range(TT):
                        for j in range(2):
                            pe.wait_ge(s_rot, c * 4 + (2 * t + j + 1))
                            transposes(f"{'qk'[j]}T{t}", r, [qk[:, t, j, d * P:(d + 1) * P] for d in range(DC)])

            def front_done(c, r):
                for t in range(TT):
                    for j in ("qT", "kT"):
                        pe.wait_ge(*freed(f"{j}{t}", r))
                pe.wait_ge(s_v3, c * 2 + 2)

            def element(b, has_next):
                for i in range(SELF, CROSS + 3):
                    if i < CROSS:
                        scores(i, b)
                    if SELF <= i - 2 < CROSS:
                        turn(i - 2, b)
                    if SELF <= i - 3 < CROSS:
                        values(i - 3, b)
                    if i == 9:
                        pe.wait_ge(*freed("o0", b))
                        transposes("aoT0", b, tiles(ao, 0))
                    if i == 10:
                        dense(0, b)
                    if i == 15:
                        turn_inputs(0, b)
                pe.wait_ge(*freed("o1", b))
                transposes("aoT1", b, tiles(ao, 1))
                pe.wait_ge(*vacant("ck", b))
                for m in range(TT):
                    gemm("ck", b, bank("ck")[:, m * E:(m + 1) * E],
                         [(ctT[:, e, m * P:(m + 1) * P], w_ckv[:, e, 0:E]) for e in range(EC)], last=(m == TT - 1))
                dense(1, b)
                pe.wait_ge(*vacant("cv", b))
                for m in range(TT):
                    gemm("cv", b, bank("cv")[:, m * E:(m + 1) * E],
                         [(ctT[:, e, m * P:(m + 1) * P], w_ckv[:, e, E:2 * E]) for e in range(EC)], last=(m == TT - 1))
                turn_inputs(1, b)
                for t in range(TT):
                    pe.wait_ge(*freed(f"ciT{t}", b))
                for t in range(TT):
                    pe.wait_ge(*vacant(f"cq{t}", b))
                    gemm(f"cq{t}", b, bank(f"cq{t}")[:, 0:E], [(ciT[:, k, t * P:(t + 1) * P], w_cq[:, k]) for k in range(DC)])
                for job in ("cq0", "cq1", "ck"):
                    pe.wait_ge(*freed(job, b))
                turn_pair(0, b)
                pe.wait_ge(s_c3, b + 1)
                for slot in range(SLOTS + 2):
                    i = CROSS + slot
                    if slot < N_CROSS:
                        scores(i, b)
                    if 0 <= slot - 2 < N_CROSS:
                        turn(i - 2, b)
                    if 0 <= slot - 3 < N_CROSS:
                        values(i - 3, b)
                    if i in PAIR_AHEAD:
                        turn_pair(slot // 2 + 1, b)
                    if has_next:
                        front(b + 1, b, slot)
                    if slot == SLOTS:
                        pe.wait_ge(*freed("o2", b))
                        transposes("ccT", b, [cc[:, t * E + c * P:t * E + (c + 1) * P] for c in range(EC) for t in range(TT)])
                pe.wait_ge(*freed("ccT", b))
                for t in range(TT):
                    pe.wait_ge(*vacant(f"cd{t}", b))
                    gemm(f"cd{t}", b, bank(f"cd{t}")[:],
                         [(ccT[:, c * S + t * P:c * S + (t + 1) * P], w_cd[:, c]) for c in range(EC)])

                if has_next:
                    front_done(b + 1, b)

            for slot in range(SLOTS + 2):
                if slot == 16:
                    pe.wait_ge(s_w, 112)
                front(0, None, slot)
            front_done(0, None)
            with pe.Fori(0, B - 1) as b:
                element(b, True)
            element(B - 1, False)

            def turn_b(e, b, buf):
                for t in range(TT):
                    pe.wait_ge(b_mi[e], b * 2 + (t + 1))
                    for c in range(DC):
                        m = nc.tensor.transpose(TB[t][:, c * P:(c + 1) * P], mi[:, t, c * P:(c + 1) * P], ident[:])
                    m.then_inc(b_tr[e], 1)

            def down(e, b, u):
                pe.wait_ge(b_hh[e], b * FC + (u + 1))
                for t in range(TT):
                    m = nc.tensor.matmul(DN[t][:], hh[0:FW[u], u % 4, t * P:(t + 1) * P], w_dn[e][0:FW[u], u],
                                         start=(u == 0), stop=(u == FC - 1))
                m.then_inc(b_dn[e], 1)

            for e in "vl":
                turn_b(e, 0, 0)
                pe.wait_ge(b_w[e], 64)
                for b, j in tiles_of(pe, e):
                    pe.wait_ge(b_mit[e], b * 2 + 2)
                    for u in range(FC + 2):
                        if u == MID + 3:
                            turn_b(e, b + 1, 1 - j)
                        if u < FC:
                            if u >= UP_N:
                                pe.wait_ge(b_hh[e], b * FC + (u - UP_N + 1))
                            for g in range(2):
                                for c in range(DC):
                                    m = nc.tensor.matmul(UP[u % UP_N][0:FW[u], g * S:(g + 1) * S],
                                                         w_up[e][:, c, g, u * P:u * P + FW[u]], miT[:, j, c],
                                                         start=(c == 0), stop=(c == DC - 1))
                            m.then_inc(b_up[e], 1)
                        if u == 2:
                            pe.wait_ge(b_out[e], b * 2 + 1)
                        if u >= 2:
                            down(e, b, u - 2)


def rotary_table(n):
    inv = (1.0 / 10000.0 ** (np.arange(0, HD, 2, dtype=np.float32) / np.float32(HD))).astype(np.float32)
    f = np.outer(np.arange(n, dtype=np.float32), inv).astype(np.float32)
    return np.concatenate([np.cos(f), np.cos(f), -np.sin(f), np.sin(f)], axis=1).astype(np.float32)


_INS = ["x", "ctx_1024", "pos_1xS", "mask_BxS_ik0", "L0_xattn_W_mem", "L0_xattn_W_gate", "L0_xattn_b_gate",
        "L0_xattn_norm_w", "L1_xattn_ln_in_w", "L1_xattn_ln_post_attn_w", "L1_xattn_ln_post_cross_w",
        "L1_xattn_v_qkv", "L1_xattn_l_qkv", "L1_xattn_v_dense", "L1_xattn_l_dense", "L1_xattn_cq_w",
        "L1_xattn_ckv_w", "L1_xattn_cdense_w", "L1_xattn_v_gate", "L1_xattn_v_up", "L1_xattn_v_down",
        "L1_xattn_l_gate", "L1_xattn_l_up", "L1_xattn_l_down"]


def kernel(**inputs):
    import numpy as _np
    import concourse.bacc as _bacc
    from concourse import mybir as _mybir
    from concourse.bass_utils import run_bass_kernel_spmd as _run

    nc = _bacc.Bacc("TRN2", target_bir_lowering=False, num_devices=1)
    arrays, args = {}, {}
    for name in _INS:
        v = _np.ascontiguousarray(inputs[name])
        arrays[f"in_{name}"] = v
        args[name] = nc.dram_tensor(f"in_{name}", v.shape, _mybir.dt.from_np(v.dtype), kind="ExternalInput").ap()
    table = rotary_table(inputs["x"].shape[1])
    arrays["rotary"] = table
    consts = {"rotary": nc.dram_tensor("rotary", table.shape, _mybir.dt.float32, kind="ExternalInput").ap()}
    shape = inputs["x"].shape
    out = nc.dram_tensor("out_0", shape, _mybir.dt.float32, kind="ExternalOutput").ap()
    h_mid = nc.dram_tensor("h_mid", shape, _mybir.dt.float32, kind="Internal").ap()
    slots = nc.dram_tensor("slots", (2 * shape[0] * shape[1], 1), _mybir.dt.int32, kind="Internal").ap()
    program(nc, args, out, h_mid, slots, consts)
    r = _run(nc, [arrays], core_ids=[0])
    return r.results[0]["out_0"]
```

```python
from contextlib import ExitStack

import numpy as np
import concourse.bass as bass
from concourse import mybir

P = 128
F32 = mybir.dt.float32
BF16 = mybir.dt.bfloat16
F16 = mybir.dt.float16
F32R = mybir.dt.float32r
I32 = mybir.dt.int32
ALU = mybir.AluOpType
ACT = mybir.ActivationFunctionType
AX_X = mybir.AxisListType.X

EPS = 1e-6
MID = 4
MASKED = -1e30
NH = 16
HD = 32
CHD = 16
P_LIFT = float(np.log(2.0 ** 11))
PARTS = [(0, 0), (0, 1), (0, 2), (1, 0), (1, 1)]

BANKS = ["G0", "G1", "S0", "S1", "S2", "T0", "T1", "O"]
RING = {"G": 2, "S": 3, "T": 2, "O": 1}
N_SELF, N_CROSS = 12, 16
PAIRS = NH // 2
TURN, VALUES = 2, 3
SELF, CROSS, END = 2, 2 + N_SELF, 2 + N_SELF + N_CROSS

PAIR_AHEAD = range(CROSS, CROSS + N_CROSS - 2, 2)

FRONT = {
    -3: [("ctT", "T")],
    -2: [("mp0", "G"), ("mp1", "G")],
    -1: [("mpT0", "T"), ("mpT1", "T")],
    0: [("xT0", "T"), ("xT1", "T")],
    1: [("l0s", "G")],
    3: [("pT0", "T"), ("pT1", "T")],
    4: [("mc0", "G"), ("mc1", "G")],
    5: [("mcT0", "T"), ("mcT1", "T")],
    6: [("gate0", "G")],
    8: [("gate1", "G")],
    12: [("xnT0", "T")],
    13: [("q0", "G")],
    14: [("k0", "G"), ("xnT1", "T")],
    15: [("v0", "G")],
    17: [("q1", "G")],
    19: [("k1", "G"), ("v1", "G")],
    20: [("qT0", "T"), ("kT0", "T"), ("qT1", "T"), ("kT1", "T")],
}
Q_SLOTS, K_SLOTS, V_SLOTS = ([min(s for s in FRONT if (f"{j}{t}", "G") in FRONT[s]) for t in range(2)] for j in "qkv")
SLOTS = N_CROSS + VALUES


def plan_iteration():
    jobs = []
    for i in range(SELF, CROSS + VALUES):
        jobs += [(f"s{i}", "S")] * (i < CROSS)
        jobs += [(f"t{i - TURN}", "T")] * (SELF <= i - TURN < CROSS)
        jobs += [("o0", "O")] * (i == SELF + VALUES) + [("o1", "O")] * (i == SELF + VALUES + 4)
        jobs += {9: [("aoT0", "T")], 10: [("dense0", "G")], 15: [("ciT0", "T")]}.get(i, [])
    jobs += [("aoT1", "T"), ("ck", "O"), ("dense1", "G"), ("cv", "G")] + FRONT[-3] + FRONT[-2]
    jobs += [("ciT1", "T")] + FRONT[-1] + [("cq0", "G"), ("cq1", "G")] + FRONT[0] + [("x0", "T")]
    for i in range(CROSS, END + VALUES):
        jobs += [(f"s{i}", "S")] * (i < END)
        jobs += [(f"t{i - TURN}", "T")] * (CROSS <= i - TURN < END)
        jobs += [("o2", "O")] * (i == CROSS + VALUES)
        jobs += [(f"x{(i - CROSS) // 2 + 1}", "T")] * (i in PAIR_AHEAD)
        jobs += (FRONT.get(i - CROSS, []) if i > CROSS else [])
    jobs += FRONT[SLOTS] + [("ccT", "T")] + FRONT[SLOTS + 1] + [("cd0", "G"), ("cd1", "G")]
    return jobs


def place_jobs():
    seen, where, uses = dict.fromkeys(RING, 0), {}, dict.fromkeys(BANKS, 0)
    for name, ring in plan_iteration():
        n = seen[ring]
        bank = "O" if ring == "O" else f"{ring}{n % RING[ring]}"
        where[name] = (bank, uses[bank])
        uses[bank] += 1
        seen[ring] += 1
    first, first_uses = {}, dict.fromkeys(BANKS, 0)
    for slot in sorted(FRONT):
        for name, _ in FRONT[slot]:
            bank = where[name][0]
            first[name] = (bank, first_uses[bank])
            first_uses[bank] += 1
    last, last_uses = {}, dict.fromkeys(BANKS, 0)
    for name, _ in plan_iteration():
        if name not in first:
            bank = where[name][0]
            last[name] = (bank, last_uses[bank])
            last_uses[bank] += 1
    return where, uses, first, first_uses, last


def program(nc, a, out, h_mid, slots, consts):
    B, S, D = a["x"].shape
    E = a["ctx_1024"].shape[2]
    I = a["L1_xattn_v_gate"].shape[1]
    DC, EC = D // P, E // P
    TT = S // P
    FC = -(-I // P)
    FW = [min(P, I - f * P) for f in range(FC)]
    WHERE, USES, FIRST, FIRST_USES, LAST = place_jobs()
    PRO = {"T0": 5, "T1": 5}
    FREE0 = {"T0": 5, "T1": 5, "G0": 1, "G1": 1, "O": 1}

    with ExitStack() as ctx:
        def sb(name, shape, dt=F32, c=ctx):
            return c.enter_context(nc.sbuf_tensor(name, shape, dt))

        def sem(name):
            return ctx.enter_context(nc.semaphore(name))

        ps = {n: ctx.enter_context(nc.psum_tensor(n, [P, 512], F32)) for n in BANKS}
        bank_ready = {n: sem(f"ready_{n}") for n in BANKS}
        bank_free = {n: sem(f"free_{n}") for n in BANKS}

        ident = sb("ident", [P, P])
        ident_r = sb("ident_r", [P, P], F32R)
        half_neg = sb("half_neg", [P, 1])
        N = B * S
        CH = N // P
        idx = sb("idx", [P, 2 * CH + TT], I32)
        idx_cur = {e: sb(f"idx_cur_{e}", [P, 2, TT], I32) for e in "vl"}
        counts = sb("counts", [1, 2], I32)
        slot_i, tok_id = (sb(n, [P, TT * B], I32)[:] for n in ("slot_i", "tok_id"))

        phase_a = ExitStack()

        def sa(name, shape, dt=F32):
            return sb(name, shape, dt, phase_a)

        w_memT = sa("w_memT", [P, EC, D])
        w_gate = sa("w_gate", [P, 2 * DC, D])
        w_qkv = {e: sa(f"w_qkv_{e}", [P, DC, 3 * D]) for e in "lv"}
        assert DC * 2 * I + FC * D <= EC * D + 2 * DC * D + 2 * DC * 3 * D
        w_dense = {e: sa(f"w_dense_{e}", [P, DC, D]) for e in "lv"}
        w_cq = sa("w_cq", [P, DC, E])
        w_ckv = sa("w_ckv", [P, EC, 2 * E])
        w_cd = sa("w_cd", [P, EC, D])
        bias_bc = sa("bias_bc", [P, D])
        nw_bc = {n: sa(f"nw_{n}", [P, D]) for n in ("norm", "ln_in", "cross")}
        cs = sa("cs", [P, TT, 2 * HD])
        pos = sa("pos", [P, TT], I32)
        posf = sa("posf", [P, 3, TT])
        posi = sa("posi", [P, TT], I32)
        identb = sa("identb", [P, P], BF16)
        tri = sa("tri", [P, 2, 512], BF16)

        off16 = sa("off16", [B, 2])
        below = sa("below", [B, B])
        cnt_f = sa("cnt_f", [1, 2])
        x_t = sa("x_t", [P, TT, D])
        c_t = sa("c_t", [P, TT, E])
        tok = sa("tok", [P, S], I32)
        mask = {e: sa(f"mask_{e}", [P, S]) for e in "vl"}
        ctT = sa("ctT", [P, EC, S])
        mp = sa("mp", [P, TT, D])
        bufA = sa("bufA", [P, DC, S])
        bufB = sa("bufB", [P, DC, S])
        qT = sa("qT", [P, DC, S])
        mc = sa("mc", [P, TT, D])
        gs = sa("gs", [P, TT, D])
        fu = sa("fu", [P, TT, D])
        x1 = sa("x1", [P, TT, D])
        p_ring = sa("p_ring", [P, 3, 512])
        pT_ring = sa("pT_ring", [P, 2, 2, 512], F16)
        q_pair = sa("q_pair", [P, 2, S], F32R)
        k_pair = sa("k_pair", [P, 2, 2, S], F32R)
        v_parts = sa("v_parts", [P, 3, TT, D], BF16)
        cv_parts = sa("cv_parts", [P, 3, TT, E], BF16)
        sq = sa("sq", [P, D], BF16)
        mx = sa("mx", [P, 30, 4])
        nm = sa("nm", [P, 30, 4])
        sums = sa("sums", [P, 5, NH])
        rinv = sa("rinv", [P, 5, NH])
        ss = sa("ss", [P, 6])
        ms = sa("ms", [P, 6])
        rs = sa("rs", [P, 6])
        h2 = sa("h2", [P, TT, D])
        ccs = sa("ccs", [P, 2, D])
        has_v = sa("has_v", [1, TT], I32)
        shared = ExitStack()
        qk = sb("qk", [P, TT, 2, D], F32, shared)
        kT = sb("kT", [P, DC, S], F32, shared)
        xn = sb("xn", [P, TT, D], F32, shared)
        shared.close()
        shared = ExitStack()
        xq_t = sb("xq", [P, TT, NH * 4 * CHD], F32R, shared)
        xk_t = sb("xk", [P, TT, NH * 4 * CHD], F32R, shared)
        xq, xk = [xq_t[:, t] for t in range(TT)], [xk_t[:, t] for t in range(TT)]
        xf = fu
        v_rest, ao, ciT, rotA, rotB, h1 = mc, fu, bufA, gs, mp, h2
        cv_rest = mc[:, 0].rearrange("p (t e) -> p t e", t=TT)
        p0, p0T = fu[:, 0].rearrange("p (t m) -> p t m", t=TT), fu[:, 1].rearrange("p (t m) -> p t m", t=TT)
        vm16 = x1[0:B].rearrange("p t (a s) -> p (t a) s", s=S)
        ones16, tok_row = xn[0:B, 0, 0:S], xn[0:B, 0, S:2 * S]
        tok_row_i, tok16 = xn[0:B, 1, 0:S].bitcast(I32), xn[0:B, 1, S:2 * S].bitcast(I32)
        gate_in = w_qkv["v"][:].rearrange("p c n -> p (c n)")[:, 0:DC * 2 * D].rearrange("p (c f) -> p c f", c=DC)
        mpT = qT
        cc, ccT = ccs[:, 0], ccs[:, 1]

        shared.close()
        phase_a.close()
        phase_b = ExitStack()

        def sbb(name, shape, dt=F32):
            return sb(name, shape, dt, phase_b)

        w_up, w_dn = {}, {}
        parts = ExitStack()
        up_hi = sb("w_up_l_high", [P, DC, 2, I], F32R, parts)
        dn_hi = sb("w_dn_l_high", [P, FC, D], F32R, parts)
        up_lo = sb("w_up_l_low", [P, DC, 2, I], F32R, parts)
        dn_lo = sb("w_dn_l_low", [P, FC, D], F32R, parts)
        parts.close()
        for e in "vl":
            w_up[e] = sbb(f"w_up_{e}", [P, DC, 2, I])
            w_dn[e] = sbb(f"w_dn_{e}", [P, FC, D])
        up_parts, dn_parts = (up_hi, up_lo), (dn_hi, dn_lo)
        miT_parts = [sbb(f"miT_{n}", [P, 2, DC, S], F32R) for n in ("high", "low")]
        hh_parts = [sbb(f"hh_{n}", [P, 4, S], F32R) for n in ("high", "low")]
        hh_sum = sbb("hh_sum", [P, 2, S])
        nw_post = sbb("nw_post", [P, D])
        h_t = {e: sbb(f"h_t_{e}", [P, 2, TT, D]) for e in "vl"}
        mi = sbb("mi", [P, TT, D])
        miT = sbb("miT", [P, 2, DC, S])
        sg = sbb("sg", [P, 2, S])
        hh = sbb("hh", [P, 4, S])
        sqb = sbb("sqb", [P, D])
        ssb = sbb("ssb", [P, 3, TT])
        o_t = {e: sbb(f"o_t_{e}", [P, TT, D]) for e in "vl"}
        list_i = sbb("list_i", [2 * CH, P], I32)[:]
        list_f = sbb("list_f", [2 * CH, P])[:]
        phase_b.close()

        s_w = sem("weights_in")
        s_ws = sem("wmem_in")
        s_wg = sem("wgate_in")
        s_small = sem("small_in")
        s_x = sem("x_in")
        s_cs = sem("table_in")
        s_pos = sem("pos_done")
        s_id = sem("consts_done")
        s_mask = sem("mask_done")
        s_has = sem("has_v_done")
        s_mx0 = sem("max_done_layer0")
        s_nm0 = sem("negmax_done_layer0")
        s_ri0 = sem("rinv_done_layer0")
        s_mx = sem("max_done")
        s_nm = sem("negmax_done")
        s_p = sem("probs_done")
        s_pv = sem("pv_done")
        s_hi = sem("probs_high_done")
        s_xh = sem("cross_qk_high_done")
        s_v1, s_v2, s_v3 = (sem(f"values_part{k}_done") for k in (1, 2, 3))
        s_c1, s_c2, s_c3 = (sem(f"cross_values_part{k}_done") for k in (1, 2, 3))
        s_ri = sem("rinv_done")
        s_th = sem("tanh_done")
        s_f1 = sem("gated_done")
        s_fu = sem("fused_done")
        s_ss = sem("squares_done")
        s_ms = sem("mean_done")
        s_rs = sem("rsqrt_done")
        s_x1 = sem("x1_done")
        s_xn = sem("xn_done")
        s_rot = sem("rotated_done")
        s_ci = sem("ci_done")
        s_st = sem("h_stored")
        r_in = sem("route_tokens_in")
        r_const = sem("route_consts")
        r_dve = sem("route_steps")
        r_pe = sem("route_products")
        r_sc = sem("list_scattered")
        r_back = sem("list_back")
        r_done = sem("routing_done")
        b_w = {e: sem(f"b_weights_{e}") for e in "vl"}
        b_nw = sem("b_norm_weight_in")
        b_init = sem("b_init")
        b_go = sem("pool_went_on")
        UP_N = 4

        def per_expert(what):
            return {e: sem(f"{what}_{e}") for e in "vl"}

        b_idx = per_expert("b_idx")
        b_h = per_expert("b_gathered")
        b_ss = per_expert("b_squares")
        b_ms = per_expert("b_mean")
        b_rs = per_expert("b_rsqrt")
        b_mi = per_expert("b_mi")
        b_tr = per_expert("b_turned")
        b_mit = per_expert("b_miT")
        b_up = per_expert("b_up")
        b_sg = per_expert("b_silu")
        b_hh = per_expert("b_hidden")
        b_dn = per_expert("b_down")
        b_wh = sem("b_weights_high")
        b_wl = sem("b_weights_low")
        b_mih = sem("b_miT_high")
        b_sum = sem("b_hidden_sum")
        b_hhh = sem("b_hidden_high")
        b_out = per_expert("b_out")
        b_st = per_expert("b_scattered")
        N_UNITS, S_P0 = N_SELF + N_CROSS, 2
        R_SCAN, R_POS, R_SLOTS = 5, 16, 17

        def bank(job):
            return ps[WHERE[job][0]]

        def nth(job, r):
            if r is None:
                n, k = FIRST[job]
                return n, k
            n, k = LAST[job] if isinstance(r, int) and r == B - 1 else WHERE[job]
            return n, r * USES[n] + (FIRST_USES[n] + k)

        def ready(job, r):
            if job == "ck":
                return bank_ready["O"], r + 1
            n, k = nth(job, r)
            return bank_ready[n], k + (PRO.get(n, 0) + 1)

        def freed(job, r):
            n, k = nth(job, r)
            return bank_free[n], k + (FREE0[n] + 1)

        def vacant(job, r):
            n, k = nth(job, r)
            return bank_free[n], k + FREE0[n]

        def free_sem(job):
            return bank_free[WHERE[job][0]]

        def ready_sem(job):
            return bank_ready[WHERE[job][0]]

        self_units = [(0, [r, r + 4, r + 8, r + 12], P) for r in range(4)]
        self_units += [(1, [8 * cp + r, 8 * cp + 4 + r], S) for r in range(4) for cp in range(2)]
        cross_units = [(t, [2 * g, 2 * g + 1], S) for g in range(PAIRS) for t in range(TT)]
        units = {SELF + i: u for i, u in enumerate(self_units)} | {CROSS + i: u for i, u in enumerate(cross_units)}

        def sum_row(u):
            return (1 if u < CROSS else 3) + units[u][0]

        def probs(u, b):
            return s_p, b * N_UNITS + (u - SELF + 1 + S_P0)

        def unit_done(s_, u, b):
            return s_, b * N_UNITS + (u - SELF + 1)

        def in_parts(x, keys, low):
            v = x.rearrange("p (h a b d) -> p h a b d", h=NH, a=2, b=2)
            return v[:, :, :, low] if keys else v[:, :, low]

        def twice(src):
            return src.rearrange("p (h d) -> p h d", d=CHD).unsqueeze(2).broadcast_to([P, NH, 2, CHD])

        UP = [ps[n] for n in ("G0", "G1", "S0", "S1")]
        DN = [ps[n] for n in ("S2", "O")]
        TB = [ps[n] for n in ("T0", "T1")]
        NT = N // S

        def tiles_of(eng, e):
            n = eng.value_load(counts[0:1, "vl".index(e):"vl".index(e) + 1], min_val=0, max_val=N)
            with eng.Fori(0, NT // 2) as i:
                for j in range(2):
                    with eng.If(n > i * (2 * S) + j * S):
                        yield i * 2 + j, j

        block = ctx.enter_context(nc.Block())
        tiled = a["x"].rearrange("b (t p) d -> b p t d", p=P)
        ctiled = a["ctx_1024"].rearrange("b (t p) d -> b p t d", p=P)
        h_rows = h_mid.rearrange("b s d -> (b s) d")
        out_rows = out.rearrange("b s d -> (b s) d")
        htiled = h_mid.rearrange("b (t p) d -> b p t d", p=P)

        @block.sync
        def _(sp):
            def load_batch(b):
                sp.dma_start(x_t[:], tiled[b]).then_inc(s_x, 16)
                sp.dma_start(c_t[:], ctiled[b]).then_inc(s_x, 16)
                sp.dma_start(tok[:], a["mask_BxS_ik0"][b].partition_broadcast(P)).then_inc(s_x, 16)

            sp.dma_start(pos[:], a["pos_1xS"].rearrange("o (t p) -> p (o t)", p=P), allow_slow_non_contiguous=True).then_inc(s_pos, 16)
            sp.dma_start(tok16, a["mask_BxS_ik0"]).then_inc(r_in, 16)
            sp.dma_start(bufA[:], a["L0_xattn_W_mem"].rearrange("(c p) e -> p c e", p=P)).then_inc(s_ws, 16)
            sp.dma_start(gate_in, a["L0_xattn_W_gate"].rearrange("(c p) f -> p c f", p=P)).then_inc(s_wg, 16)
            load_batch(0)
            for t, n in ((bias_bc, "L0_xattn_b_gate"), (nw_bc["norm"], "L0_xattn_norm_w"),
                         (nw_bc["ln_in"], "L1_xattn_ln_in_w"), (nw_bc["cross"], "L1_xattn_ln_post_cross_w")):
                sp.dma_start(t[:], a[n].partition_broadcast(P)).then_inc(s_small, 16)
            for t, n in ((w_ckv, "L1_xattn_ckv_w"), (w_qkv["l"], "L1_xattn_l_qkv"), (w_dense["l"], "L1_xattn_l_dense"),
                         (w_dense["v"], "L1_xattn_v_dense"), (w_cq, "L1_xattn_cq_w"), (w_cd, "L1_xattn_cdense_w")):
                sp.dma_start(t[:], a[n].rearrange("(c p) n -> p c n", p=P)).then_inc(s_w, 16)

            sp.wait_ge(bank_ready["T0"], PRO["T0"])
            sp.wait_ge(bank_ready["T1"], PRO["T1"])
            sp.dma_start(w_qkv["v"][:], a["L1_xattn_v_qkv"].rearrange("(c p) n -> p c n", p=P)).then_inc(s_w, 16)

            def store(b):
                sp.wait_ge(*freed("cd1", b))
                sp.dma_start(htiled[b], h2[:]).then_inc(s_st, 16)

            with sp.Fori(0, B - 1) as b:
                sp.wait_ge(s_fu, b * 2 + 2)
                load_batch(b + 1)
                store(b)

            def load_experts(e):
                for i, n in enumerate((f"L1_xattn_{e}_gate", f"L1_xattn_{e}_up")):
                    sp.dma_start(w_up[e][:, :, i], a[n].rearrange("(c p) n -> p c n", p=P)).then_inc(b_w[e], 16)
                dn = a[f"L1_xattn_{e}_down"]
                sp.dma_start(w_dn[e][:, 0:FC - 1], dn[0:(FC - 1) * P, :].rearrange("(c p) n -> p c n", p=P)).then_inc(b_w[e], 16)
                sp.dma_start(w_dn[e][0:FW[-1], FC - 1], dn[(FC - 1) * P:I, :]).then_inc(b_w[e], 16)

            for job in ("q1", "k1", "v1"):
                sp.wait_ge(*ready(job, B - 2))
            load_experts("v")
            store(B - 1)
            sp.wait_ge(s_st, 16 * B + 16)
            sp.dma_start(nw_post[:], a["L1_xattn_ln_post_attn_w"].partition_broadcast(P)).then_inc(b_nw, 16)
            load_experts("l")

        @block.gpsimd
        def _(pool):
            nc.gpsimd.memset(ident[:], 0.0).then_inc(s_id, 1)
            nc.gpsimd.memset(half_neg[:], -0.5).then_inc(s_id, 1)
            nc.gpsimd.memset(identb[:], 0.0).then_inc(s_id, 1)
            nc.gpsimd.memset(tri[:], 0.0).then_inc(s_id, 1)
            nc.gpsimd.memset(k_pair[:].bitcast(F32), 0.0).then_inc(s_id, 1)
            for first, n in ((bank_free["G0"], 1), (bank_free["G1"], 1),
                             (bank_free["O"], 1), (s_p, S_P0), (s_ss, 1),
                             (s_st, 16), (b_ss["v"], 1), (b_ss["l"], 1), (b_out["v"], 1), (b_out["l"], 1)):
                nc.gpsimd.nop().then_inc(first, n)
            nc.gpsimd.memset(ident_r[:].bitcast(F32), 0.0).then_inc(s_id, 1)
            pool.wait_ge(s_id, 6)
            for m in (ident, ident_r, identb):
                nc.gpsimd.affine_select(out=m[:], in_=m[:], compare_op=ALU.not_equal, fill=1.0, base=0,
                                        pattern=[[-1, P]], channel_multiplier=1).then_inc(s_id, 1)
            nc.gpsimd.affine_select(out=tri[:, 0].rearrange("p (h k) -> p h k", k=P),
                                    in_=tri[:, 0].rearrange("p (h k) -> p h k", k=P), compare_op=ALU.is_ge,
                                    fill=MASKED, base=0, pattern=[[0, 4], [-1, P]], channel_multiplier=1).then_inc(s_id, 1)
            nc.gpsimd.affine_select(out=tri[:, 1].rearrange("p (h k) -> p h k", k=S),
                                    in_=tri[:, 1].rearrange("p (h k) -> p h k", k=S), compare_op=ALU.is_ge,
                                    fill=MASKED, base=P, pattern=[[0, 2], [-1, S]], channel_multiplier=1).then_inc(s_id, 1)
            pool.wait_ge(s_pos, 17)
            for t in range(TT):
                nc.gpsimd.indirect_dma_start(cs[:, t], None, consts["rotary"],
                                             bass.IndirectOffsetOnAxis(ap=posi[:, t:t + 1], axis=0)).then_inc(s_cs, 16)

            nc.gpsimd.memset(ones16, 1.0).then_inc(r_const, 1)
            nc.gpsimd.memset(below[:], 1.0).then_inc(r_const, 1)
            nc.gpsimd.memset(idx[:], N).then_inc(r_const, 1)
            nc.gpsimd.iota(tok_row_i, pattern=[[1, S]], base=0, channel_multiplier=S).then_inc(r_const, 1)
            nc.gpsimd.iota(tok_id.rearrange("p (t b) -> p t b", t=TT), pattern=[[P, TT], [S, B]], base=0,
                           channel_multiplier=1).then_inc(r_const, 1)
            pool.wait_ge(r_const, 5)
            nc.gpsimd.affine_select(out=below[:], in_=below[:], compare_op=ALU.is_gt, fill=0.0, base=0,
                                    pattern=[[1, B]], channel_multiplier=-1).then_inc(r_const, 1)
            for k, e in enumerate("vl"):
                pool.dma_start(slots[k * N:(k + 1) * N].rearrange("(p c) o -> p (c o)", p=P), idx[:, 0:CH]) \
                    .then_inc(b_st[e], 16)
            for e in "vl":
                pool.wait_ge(b_st[e], 16)
            pool.wait_ge(r_dve, R_SLOTS)
            for c in range(TT * B):
                nc.gpsimd.indirect_dma_start(slots, bass.IndirectOffsetOnAxis(ap=slot_i[:, c:c + 1], axis=0),
                                             tok_id[:, c:c + 1], None).then_inc(r_sc, 16)
            def rsqrt(b, n):
                pool.wait_ge(s_ms, b * 6 + n + 1)
                nc.gpsimd.tensor_tensor(rs[:, n:n + 1], ms[:, n:n + 1], half_neg[:], ALU.pow).then_inc(s_rs, 1)

            def front(c, r):
                for n in range(4):
                    rsqrt(c, n)
                for t in range(TT):
                    for j in range(2):
                        pool.wait_ge(*freed(f"{'qk'[j]}{t}", r))
                        nc.gpsimd.tensor_tensor(qk[:, t, j], rotA[:, j], rotB[:, j], ALU.add).then_inc(s_rot, 1)
                    pool.wait_ge(s_v2, c * 2 + (t + 1))
                    nc.gpsimd.tensor_tensor(v_parts[:, 2, t], v_rest[:, t], v_parts[:, 1, t], ALU.subtract).then_inc(s_v3, 1)

            def back(b):
                for n in range(4, 6):
                    rsqrt(b, n)
                pool.wait_ge(s_c2, b + 1)
                nc.gpsimd.tensor_tensor(cv_parts[:, 2], cv_rest, cv_parts[:, 1], ALU.subtract).then_inc(s_c3, 1)

            front(0, None)
            with pool.Fori(0, B - 1) as b:
                back(b)
                front(b + 1, b)
            back(B - 1)

            def rsqrt_b(e, b):
                for t in range(TT):
                    pool.wait_ge(b_ms[e], b * 2 + (t + 1))
                    nc.gpsimd.tensor_tensor(ssb[:, 2, t:t + 1], ssb[:, 1, t:t + 1], half_neg[:], ALU.pow).then_inc(b_rs[e], 1)

            def gather(e, b, buf):
                pool.wait_ge(b_idx[e], b + 1)
                pool.sem_inc(b_go, 1)
                for t in range(TT):
                    nc.gpsimd.indirect_dma_start(h_t[e][:, buf, t], None, h_rows,
                                                 bass.IndirectOffsetOnAxis(ap=idx_cur[e][:, buf, t:t + 1], axis=0),
                                                 bounds_check=N - 1, oob_is_err=False).then_inc(b_h[e], 16)

            pool.wait_ge(s_st, 16 * B + 16)
            pool.wait_ge(r_sc, 16 * TT * B)
            pool.dma_start(list_i, slots.rearrange("(c p) o -> c (p o)", p=P)).then_inc(r_back, 16)
            pool.wait_ge(r_done, 1)
            stored = [pool.snap((pool.value_load(counts[0:1, k:k + 1], min_val=0, max_val=N) + (S - 1)) // S * 32 + 16)
                      for k in range(2)]
            pool.wait_ge(b_init, 2)
            for e in "vl":
                gather(e, 0, 0)
                rsqrt_b(e, 0)
                for b, j in tiles_of(pool, e):
                    pool.wait_ge(b_out[e], b * 2 + 1)
                    gather(e, b + 1, 1 - j)
                    rsqrt_b(e, b + 1)
                    pool.wait_ge(b_out[e], b * 2 + 3)
                    pool.sem_inc(b_go, 1)
                    for t in range(TT):
                        nc.gpsimd.indirect_dma_start(out_rows, bass.IndirectOffsetOnAxis(ap=idx_cur[e][:, j, t:t + 1], axis=0),
                                                     o_t[e][:, t], None, bounds_check=N - 1, oob_is_err=False) \
                            .then_inc(b_st[e], 16)
            for e, n in zip("vl", stored):
                pool.wait_ge(b_st[e], n)
            pool.wait_ge(r_done, 1)

        @block.scalar
        def _(act):
            def copy(dst, job, b, view=None):
                act.wait_ge(*ready(job, b))
                src = bank(job)[:] if view is None else view(bank(job))
                nc.scalar.activation(dst, src, ACT.Copy).then_inc(free_sem(job), 1)

            def square(src, n, b):
                act.wait_ge(s_ss, b * 6 + (n + 1))
                nc.scalar.activation(sq[:], src, ACT.Square, accum_out=ss[:, n:n + 1]).then_inc(s_ss, 1)

            def exps(u, b):
                act.wait_ge(*unit_done(s_nm, u, b))
                if u >= SELF + 3:
                    act.wait_ge(*ready(f"t{u - 3}", b))
                t, heads, w = units[u]
                scale = (HD if u < CROSS else CHD) ** -0.5
                for j, h in enumerate(heads):
                    e = nc.scalar.activation(p_ring[:, u % 3, j * w:(j + 1) * w], bank(f"s{u}")[:, j * w:(j + 1) * w],
                                             ACT.Exp, bias=nm[:, u, j:j + 1], scale=scale,
                                             accum_out=sums[:, sum_row(u), h:h + 1])
                e.then_inc(s_p, 1)

            def expand_high(dst, job, part, keys, b):
                act.wait_ge(*ready(job, b))
                nc.scalar.activation(in_parts(dst, keys, 0), twice(bank(job)[:, part * E:(part + 1) * E]), ACT.Copy) \
                    .then_inc(s_xh, 1)

            def high(u, b):
                act.wait_ge(*ready(f"t{u}", b))
                if u >= SELF + 2:
                    act.wait_ge(*unit_done(s_pv, u - 2, b))
                nc.scalar.activation(pT_ring[:, u % 2, 0], bank(f"t{u}")[:], ACT.Copy).then_inc(s_hi, 1)

            def chunks(k, n=DC):
                return k[:].rearrange("p (c m) -> p c m", c=n)

            def front(c, r, slot):
                if slot == -3:
                    copy(ctT[:], "ctT", r, lambda k: chunks(k, EC))
                if slot == 0:
                    copy(bufA[:, :, P:S], "xT1", r, chunks)
                if slot == -2:
                    copy(mp[:, 0], "mp0", r)
                    copy(mp[:, 1], "mp1", r)
                if slot == -1:
                    copy(mpT[:, 0:2], "mpT0", r, lambda k: chunks(k, 2))
                    copy(mpT[:, 2:4], "mpT1", r, lambda k: chunks(k, 2))
                if slot == 2:
                    act.wait_ge(s_nm0, c * 2 + TT)
                    for t in range(TT):
                        e = nc.scalar.activation(p0[:, t], bank("l0s")[:, t * S:(t + 1) * S], ACT.Exp, bias=nm[:, t, 0:1],
                                                 scale=D ** -0.5, accum_out=sums[:, 0, t:t + 1])
                    e.then_inc(free_sem("l0s"), 1)
                if slot == 5:
                    copy(bufB[:, :, 0:P], "mcT0", r, chunks)
                    copy(bufB[:, :, P:S], "mcT1", r, chunks)
                if slot in (6, 8):
                    t = slot // 8
                    act.wait_ge(*freed(f"gate{t}", r))
                    nc.scalar.activation(gs[:, t], gs[:, t], ACT.Tanh, scale=0.5).then_inc(s_th, 1)
                for t in range(TT):
                    if slot == 9 + 2 * t:
                        act.wait_ge(s_x1, c * 2 + (t + 1))
                        square(x1[:, t], 2 * t + 1, c)
                for t in range(TT):
                    if slot == 7 + 2 * t:
                        act.wait_ge(s_fu, c * 2 + (t + 1))
                        square(fu[:, t], 2 * t, c)
                if slot in V_SLOTS:
                    t = V_SLOTS.index(slot)
                    act.wait_ge(*ready(f"v{t}", r))
                    nc.scalar.activation(v_parts[:, 0, t], bank(f"v{t}")[:], ACT.Copy).then_inc(s_v1, 1)
                if slot == 20:
                    for t in range(TT):
                        for j, x in enumerate((qT, kT)):
                            copy(x[:, :, t * P:(t + 1) * P], f"{'qk'[j]}T{t}", r, chunks)

            def element(b, has_next):
                for i in range(SELF, CROSS + VALUES):
                    if SELF <= i - TURN < CROSS:
                        high(i - TURN, b)
                    if i < CROSS:
                        exps(i, b)
                    if i == 12:
                        act.wait_ge(*freed("dense0", b))
                        square(h1[:, 0], 4, b)
                expand_high(xk[0], "ck", 0, True, b)
                act.wait_ge(*freed("dense1", b))
                square(h1[:, 1], 5, b)
                act.wait_ge(*ready("cv", b))
                nc.scalar.activation(cv_parts[:, 0], chunks(bank("cv"), TT), ACT.Copy).then_inc(s_c1, 1)
                if has_next:
                    front(b + 1, b, -3)
                    front(b + 1, b, -2)
                act.wait_ge(*ready("ciT1", b))
                expand_high(xk[1], "ck", 1, True, b)
                if has_next:
                    front(b + 1, b, -1)
                for t in range(TT):
                    expand_high(xq[t], f"cq{t}", 0, False, b)
                if has_next:
                    front(b + 1, b, 0)
                for slot in range(SLOTS + 2):
                    if 0 <= slot - TURN < N_CROSS:
                        high(CROSS + slot - TURN, b)
                    if slot < N_CROSS:
                        exps(CROSS + slot, b)
                    if has_next and slot > 0:
                        front(b + 1, b, slot)
                    if slot == SLOTS:
                        copy(ccT.rearrange("p (c m) -> p c m", c=EC), "ccT", b, lambda k: chunks(k, EC))

            for slot in range(-3, SLOTS + 2):
                front(0, None, slot)
            with act.Fori(0, B - 1) as b:
                element(b, True)
            element(B - 1, False)

            def square_b(e, b, buf):
                act.wait_ge(b_h[e], b * 32 + 32)
                for t in range(TT):
                    act.wait_ge(b_ss[e], b * 2 + (t + 1))
                    nc.scalar.activation(sqb[:], h_t[e][:, buf, t], ACT.Square, accum_out=ssb[:, 0, t:t + 1]).then_inc(b_ss[e], 1)

            def turned_high(b, buf):
                for t in range(TT):
                    act.wait_ge(b_tr["l"], b * 2 + (t + 1))
                    nc.scalar.activation(miT_parts[0][:, buf, :, t * P:(t + 1) * P], chunks(TB[t]), ACT.Copy).then_inc(b_mih, 1)

            def weights_high(u):
                cols = slice(u * P, u * P + FW[u])
                for hi, w in ((up_hi[:, :, :, cols], w_up["l"][:, :, :, cols]), (dn_hi[0:FW[u], u], w_dn["l"][0:FW[u], u])):
                    nc.scalar.activation(hi, w, ACT.Copy).then_inc(b_wh, 1)

            act.wait_ge(r_done, 1)
            for e in "vl":
                square_b(e, 0, 0)
                if e == "l":
                    turned_high(0, 0)
                    act.wait_ge(b_w["l"], 64)
                    for u in range(FC):
                        weights_high(u)
                for b, j in tiles_of(act, e):
                    for u in range(FC):
                        if u == MID:
                            square_b(e, b + 1, 1 - j)
                        if u == MID + 3 and e == "l":
                            turned_high(b + 1, 1 - j)
                        act.wait_ge(b_up[e], b * FC + (u + 1))
                        if u >= 2:
                            act.wait_ge(b_hh[e], b * FC + (u - 1))
                        nc.scalar.activation(sg[0:FW[u], u % 2], UP[u % UP_N][0:FW[u], 0:S], ACT.Silu).then_inc(b_sg[e], 1)

        @block.vector
        def _(dve):
            dve.wait_ge(s_pos, 16)
            nc.vector.tensor_copy(posf[:, 0], pos[:]).then_inc(s_mx, 1)
            dve.wait_ge(s_mx, 1)
            nc.vector.tensor_scalar(posf[:, 1], posf[:, 0], 0.0, float(S), ALU.is_lt, ALU.mult).then_inc(s_mx, 1)
            dve.wait_ge(s_mx, 2)
            nc.vector.tensor_tensor(posf[:, 2], posf[:, 0], posf[:, 1], ALU.add).then_inc(s_mx, 1)
            dve.wait_ge(s_mx, 3)
            nc.vector.tensor_scalar(posi[:], posf[:, 2], 0.0, float(S - 1), ALU.max, ALU.min).then_inc(s_pos, 1)
            for c in range(EC):
                dve.wait_ge(bank_ready[f"T{c}"], 1)
                nc.vector.tensor_copy(w_memT[:, c], ps[f"T{c}"][:]).then_inc(bank_free[f"T{c}"], 1)
            for f in range(2 * DC):
                n = f"T{f % 2}"
                dve.wait_ge(bank_ready[n], 2 + f // 2)
                nc.vector.tensor_copy(w_gate[:, f], ps[n][:]).then_inc(bank_free[n], 1)
            MX0 = 3

            steps = [0]

            def step(ins):
                steps[0] += 1
                ins.then_inc(r_dve, 1)
                dve.wait_ge(r_dve, steps[0])

            dve.wait_ge(r_in, 16)
            dve.wait_ge(r_const, 6)
            step(nc.vector.tensor_scalar(vm16[:, 0], tok16, 1.0, None, ALU.is_equal))
            step(nc.vector.memset(vm16[:, 1, S - 1:S], 0.0))
            step(nc.vector.tensor_tensor(vm16[:, 1, 0:S - 1], vm16[:, 0, 0:S - 1], vm16[:, 0, 1:S], ALU.mult))
            step(nc.vector.tensor_tensor_scan(vm16[:, 2], ones16, vm16[:, 1], 0.0, ALU.mult, ALU.add))
            step(nc.vector.tensor_copy(tok_row, tok_row_i))
            assert steps[0] == R_SCAN
            dve.wait_ge(r_pe, 1)
            step(nc.vector.tensor_copy(off16[:, 0:1], ps["O"][0:B, 0:1]))
            step(nc.vector.tensor_copy(cnt_f[:, 0:1], ps["O"][0:1, 1:2]))
            step(nc.vector.tensor_scalar(cnt_f[:, 1:2], cnt_f[:, 0:1], -1.0, float(N), ALU.mult, ALU.add))
            step(nc.vector.tensor_copy(counts[:], cnt_f[:]))
            step(nc.vector.tensor_scalar(vm16[:, 3], vm16[:, 2], off16[:, 0:1], None, ALU.add))
            step(nc.vector.tensor_tensor(tok_row, tok_row, vm16[:, 3], ALU.subtract))
            step(nc.vector.tensor_scalar(tok_row, tok_row, float(N), None, ALU.add))
            step(nc.vector.tensor_scalar(vm16[:, 3], vm16[:, 3], -1.0, None, ALU.add))
            step(nc.vector.tensor_tensor(vm16[:, 3], vm16[:, 3], tok_row, ALU.subtract))
            step(nc.vector.tensor_tensor(vm16[:, 3], vm16[:, 3], vm16[:, 1], ALU.mult))
            step(nc.vector.tensor_tensor(vm16[:, 3], vm16[:, 3], tok_row, ALU.add))
            assert steps[0] == R_POS
            dve.wait_ge(r_pe, 2)
            step(nc.vector.tensor_copy(slot_i, ps["O"][:, 0:TT * B]))
            assert steps[0] == R_SLOTS

            def masks(b):
                eq, mv, ml = mask["l"], mask["v"], mask["l"]
                nc.vector.tensor_scalar(eq[:], tok[:], 1.0, None, ALU.is_equal).then_inc(s_mask, 1)
                nc.vector.memset(mv[:, S - 1:S], 0.0).then_inc(s_mask, 1)
                dve.wait_ge(s_mask, b * 4 + 2)
                nc.vector.tensor_tensor(mv[:, 0:S - 1], eq[:, 0:S - 1], eq[:, 1:S], ALU.mult).then_inc(s_mask, 1)
                dve.wait_ge(s_mask, b * 4 + 3)
                nc.vector.tensor_scalar(ml[:], mv[:], -1.0, 1.0, ALU.mult, ALU.add).then_inc(s_mask, 1)

            def copy(dst, job, b, view=None):
                dve.wait_ge(*ready(job, b))
                src = bank(job)[:] if view is None else view(bank(job))
                nc.vector.tensor_copy(dst, src).then_inc(free_sem(job), 1)

            def maxima(u, b):
                nh, w = len(units[u][1]), units[u][2]
                scale = (HD if u < CROSS else CHD) ** -0.5
                dve.wait_ge(*ready(f"s{u}", b))
                nc.vector.tensor_reduce(mx[:, u, 0:nh], bank(f"s{u}")[:, 0:nh * w].rearrange("p (h k) -> p h k", k=w),
                                        AX_X, ALU.max).then_inc(s_mx, 1)
                s_, v = unit_done(s_mx, u, b)
                dve.wait_ge(s_, v + MX0)
                nc.vector.tensor_scalar(nm[:, u, 0:nh], mx[:, u, 0:nh], -scale, P_LIFT, ALU.mult, ALU.add).then_inc(s_nm, 1)

            def low(u, b):
                dve.wait_ge(*unit_done(s_hi, u, b))
                nc.vector.tensor_tensor(pT_ring[:, u % 2, 1], bank(f"t{u}")[:], pT_ring[:, u % 2, 0], ALU.subtract) \
                    .then_inc(free_sem(f"t{u}"), 1)

            def mean(b, n):
                dve.wait_ge(s_ss, b * 6 + (n + 2))
                nc.vector.tensor_scalar(ms[:, n:n + 1], ss[:, n:n + 1], 1.0 / D, EPS, ALU.mult, ALU.add).then_inc(s_ms, 1)

            def scaled(b, n, dst, src, w, done):
                dve.wait_ge(s_rs, b * 6 + n + 1)
                nc.vector.scalar_tensor_tensor(out=dst, in0=src, scalar=rs[:, n:n + 1], in1=w[:], op0=ALU.mult,
                                               op1=ALU.mult).then_inc(done, 1)

            def split_experts(job, t, b):
                dve.wait_ge(*ready(job, b))
                src = bank(job)[:].rearrange("p (c m) -> p c m", c=DC)
                for buf, e in ((bufA, "v"), (bufB, "l")):
                    m = mask[e][:, t * P:(t + 1) * P].unsqueeze(1).broadcast_to([P, DC, P])
                    o = nc.vector.tensor_tensor(buf[:, :, t * P:(t + 1) * P], src, m, ALU.mult)
                o.then_inc(free_sem(job), 1)

            def rotary(job, j, c, r):
                t = j // 2
                dve.wait_ge(*ready(job, r))
                if j >= 2:
                    dve.wait_ge(s_rot, c * 4 + (j - 1))
                src = bank(job)[:].rearrange("p (h a d) -> p h a d", h=NH, a=2)
                co = cs[:, t, 0:HD].unsqueeze(1).broadcast_to([P, NH, HD])
                si = cs[:, t, HD:2 * HD].rearrange("p (a d) -> p a d", a=2)
                nc.vector.tensor_tensor(rotA[:, j % 2].rearrange("p (h d) -> p h d", h=NH),
                                        bank(job)[:].rearrange("p (h d) -> p h d", h=NH), co, ALU.mult)
                outB = rotB[:, j % 2].rearrange("p (h a d) -> p h a d", h=NH, a=2)
                for k in range(2):
                    o = nc.vector.tensor_tensor(outB[:, :, k], src[:, :, 1 - k],
                                                si[:, k].unsqueeze(1).broadcast_to([P, NH, HD // 2]), ALU.mult)
                o.then_inc(free_sem(job), 1)

            def chunks(k, n=DC):
                return k[:].rearrange("p (c m) -> p c m", c=n)

            def pair(g, b):
                job = f"x{g}"
                dve.wait_ge(*ready(job, b))
                src = bank(job)[:].bitcast(F32R)
                nc.vector.tensor_copy(q_pair[:, g % 2], src[:, 0:S])
                for k in range(2):
                    rows = slice(k * 64, (k + 1) * 64)
                    o = nc.vector.tensor_copy(k_pair[rows, g % 2, k], src[rows, S:2 * S])
                o.then_inc(free_sem(job), 1)

            def attended(b, t):
                last_unit = SELF + (3, N_SELF - 1)[t]
                dve.wait_ge(*probs(last_unit, b))
                nc.vector.reciprocal(rinv[:, 1 + t], sums[:, 1 + t]).then_inc(s_ri, 1)
                dve.wait_ge(s_ri, b * 4 + (t + 1))
                dve.wait_ge(*unit_done(s_pv, last_unit, b))
                nc.vector.tensor_tensor(ao[:, t].rearrange("p (h d) -> p h d", h=NH),
                                        bank(f"o{t}")[:].rearrange("p (h d) -> p h d", h=NH),
                                        rinv[:, 1 + t].unsqueeze(2).broadcast_to([P, NH, HD]), ALU.mult) \
                    .then_inc(free_sem(f"o{t}"), 1)

            def residual(b, t):
                if t == 0:
                    dve.wait_ge(s_st, b * 16 + 16)
                dve.wait_ge(*ready(f"dense{t}", b))
                nc.vector.tensor_tensor(h1[:, t], bank(f"dense{t}")[:], x1[:, t], ALU.add) \
                    .then_inc(free_sem(f"dense{t}"), 1)

            def front(c, r, slot):
                if slot == 0:
                    dve.wait_ge(s_x, c * 48 + 48)
                    masks(c)
                    copy(bufA[:, :, 0:P], "xT0", r, chunks)
                    nc.vector.tensor_reduce(has_v[:], mask["v"][0:1].rearrange("o (t p) -> o t p", p=P), AX_X, ALU.max) \
                        .then_inc(s_has, 1)
                if slot == 1:
                    dve.wait_ge(*ready("l0s", r))
                    for t in range(TT):
                        nc.vector.tensor_reduce(mx[:, t, 0:1], bank("l0s")[:, t * S:(t + 1) * S], AX_X, ALU.max) \
                            .then_inc(s_mx0, 1)
                        dve.wait_ge(s_mx0, c * 2 + (t + 1))
                        nc.vector.tensor_scalar(nm[:, t, 0:1], mx[:, t, 0:1], -D ** -0.5, None, ALU.mult).then_inc(s_nm0, 1)
                if slot == 3:
                    for t in range(TT):
                        dve.wait_ge(*ready(f"pT{t}", r))
                        nc.vector.tensor_copy(p0T[:, t], bank(f"pT{t}")[:, 0:S]).then_inc(free_sem(f"pT{t}"), 1)
                    nc.vector.reciprocal(rinv[:, 0, 0:TT], sums[:, 0, 0:TT]).then_inc(s_ri0, 1)
                if slot == 4:
                    dve.wait_ge(s_ri0, c + 1)
                    for t in range(TT):
                        dve.wait_ge(*ready(f"mc{t}", r))
                        nc.vector.tensor_scalar(mc[:, t], bank(f"mc{t}")[:], rinv[:, 0, t:t + 1], None, ALU.mult) \
                            .then_inc(free_sem(f"mc{t}"), 1)
                if slot in (6, 8):
                    t = slot // 8
                    dve.wait_ge(*ready(f"gate{t}", r))
                    nc.vector.tensor_tensor(gs[:, t], bank(f"gate{t}")[:], bias_bc[:], ALU.add) \
                        .then_inc(free_sem(f"gate{t}"), 1)
                for t in range(TT):
                    if slot == 11 + 2 * t:
                        scaled(c, 2 * t + 1, xf[:, t], x1[:, t], nw_bc["ln_in"], s_xn)
                for t in range(TT):
                    if slot == 9 + 2 * t:
                        scaled(c, 2 * t, x1[:, t], fu[:, t], nw_bc["norm"], s_x1)
                for t in range(TT):
                    if slot == 10 + 2 * t:
                        mean(c, 2 * t + 1)
                for t in range(TT):
                    if slot == 8 + 2 * t:
                        mean(c, 2 * t)
                for t in range(TT):
                    if slot == 7 + 2 * t:
                        dve.wait_ge(s_th, c * 2 + (t + 1))
                        nc.vector.scalar_tensor_tensor(out=gs[:, t], in0=gs[:, t], scalar=1.0, in1=mc[:, t], op0=ALU.add,
                                                       op1=ALU.mult).then_inc(s_f1, 1)
                        dve.wait_ge(s_f1, c * 2 + (t + 1))
                        nc.vector.scalar_tensor_tensor(out=fu[:, t], in0=gs[:, t], scalar=0.5, in1=x_t[:, t], op0=ALU.mult,
                                                       op1=ALU.add).then_inc(s_fu, 1)
                    if slot == 12 + 2 * t:
                        split_experts(f"xnT{t}", t, r)
                if slot in Q_SLOTS:
                    t = Q_SLOTS.index(slot)
                    rotary(f"q{t}", 2 * t, c, r)
                if slot in K_SLOTS:
                    t = K_SLOTS.index(slot)
                    rotary(f"k{t}", 2 * t + 1, c, r)
                if slot in V_SLOTS:
                    t = V_SLOTS.index(slot)
                    dve.wait_ge(s_v1, c * 2 + (t + 1))
                    nc.vector.tensor_tensor(v_rest[:, t], bank(f"v{t}")[:], v_parts[:, 0, t], ALU.subtract) \
                        .then_inc(free_sem(f"v{t}"), 1)
                    dve.wait_ge(*freed(f"v{t}", r))
                    nc.vector.tensor_scalar(v_parts[:, 1, t], v_rest[:, t], 0.0, None, ALU.add).then_inc(s_v2, 1)

            def element(b, has_next):
                for i in range(SELF, CROSS + VALUES):
                    if i < CROSS:
                        maxima(i, b)
                    if SELF <= i - TURN < CROSS:
                        low(i - TURN, b)
                    if i == 8:
                        attended(b, 0)
                    if i == 9:
                        split_experts("aoT0", 0, b)
                    if i == 11:
                        residual(b, 0)
                    if i == 13:
                        mean(b, 4)
                    if i == 14:
                        scaled(b, 4, xn[:, 0], h1[:, 0], nw_bc["cross"], s_ci)
                    if i == 15:
                        copy(ciT[:, :, 0:P], "ciT0", b, chunks)
                attended(b, 1)
                split_experts("aoT1", 1, b)
                residual(b, 1)
                mean(b, 5)
                dve.wait_ge(s_c1, b + 1)
                nc.vector.tensor_tensor(cv_rest, chunks(bank("cv"), TT), cv_parts[:, 0], ALU.subtract).then_inc(free_sem("cv"), 1)
                scaled(b, 5, xn[:, 1], h1[:, 1], nw_bc["cross"], s_ci)
                dve.wait_ge(*freed("cv", b))
                nc.vector.tensor_scalar(cv_parts[:, 1], cv_rest, 0.0, None, ALU.add).then_inc(s_c2, 1)
                copy(ciT[:, :, P:S], "ciT1", b, chunks)
                for n, (dst, job, part) in enumerate(((xk[0], "ck", 0), (xk[1], "ck", 1), (xq[0], "cq0", 0), (xq[1], "cq1", 0))):
                    dve.wait_ge(s_xh, b * 4 + (2 if n < 2 else n + 1))
                    o = nc.vector.tensor_tensor(in_parts(dst, n < 2, 1), twice(bank(job)[:, part * E:(part + 1) * E]),
                                                in_parts(dst, n < 2, 0), ALU.subtract)
                    if n > 0:
                        o.then_inc(free_sem(job), 1)
                if has_next:
                    front(b + 1, b, 0)
                pair(0, b)
                for slot in range(SLOTS + 2):
                    if slot < N_CROSS:
                        maxima(CROSS + slot, b)
                    if 0 <= slot - TURN < N_CROSS:
                        low(CROSS + slot - TURN, b)
                    if CROSS + slot in PAIR_AHEAD:
                        pair(slot // 2 + 1, b)
                    if slot == SLOTS:
                        dve.wait_ge(*probs(END - 1, b))
                        nc.vector.reciprocal(rinv[:, 3:5], sums[:, 3:5]).then_inc(s_ri, 2)
                        dve.wait_ge(s_ri, b * 4 + 4)
                        dve.wait_ge(*unit_done(s_pv, END - 1, b))
                        nc.vector.tensor_tensor(cc.rearrange("p (h d) -> p h d", d=CHD),
                                                bank("o2")[:].rearrange("p (h d) -> p h d", d=CHD),
                                                rinv[:, 3:5].rearrange("p t h -> p (t h)").unsqueeze(2).broadcast_to([P, 2 * NH, CHD]),
                                                ALU.mult).then_inc(free_sem("o2"), 1)
                    if has_next and slot > 0:
                        front(b + 1, b, slot)
                for t in range(TT):
                    dve.wait_ge(*ready(f"cd{t}", b))
                    nc.vector.tensor_tensor(h2[:, t], bank(f"cd{t}")[:], h1[:, t], ALU.add).then_inc(free_sem(f"cd{t}"), 1)

            dve.wait_ge(s_small, 64)
            dve.wait_ge(s_cs, 32)
            dve.wait_ge(s_id, 11)
            for slot in range(-3, SLOTS + 2):
                front(0, None, slot)
            with dve.Fori(0, B - 1) as b:
                element(b, True)
            element(B - 1, False)

            dve.wait_ge(s_st, 16 * B + 16)
            dve.wait_ge(r_back, 16)
            step(nc.vector.tensor_copy(list_f, list_i))
            dve.wait_ge(r_pe, 3)
            nc.vector.tensor_copy(idx[:, 0:2 * CH], ps["O"][:, 0:2 * CH]).then_inc(r_done, 1)
            dve.wait_ge(r_done, 1)
            for e in "vl":
                nc.vector.memset(h_t[e][:], 0.0).then_inc(b_init, 1)
            dve.wait_ge(b_nw, 16)

            def indices(e, b, buf):
                k = b * 2 + CH * "vl".index(e)
                nc.vector.tensor_scalar(idx_cur[e][:, buf], idx[:, bass.ds(k, TT)], 0.0, None, ALU.add).then_inc(b_idx[e], 1)

            def norm_b(e, b, buf):
                for t in range(TT):
                    dve.wait_ge(b_ss[e], b * 2 + (t + 2))
                    nc.vector.tensor_scalar(ssb[:, 1, t:t + 1], ssb[:, 0, t:t + 1], 1.0 / D, EPS, ALU.mult, ALU.add) \
                        .then_inc(b_ms[e], 1)
                for t in range(TT):
                    dve.wait_ge(b_rs[e], b * 2 + (t + 1))
                    nc.vector.scalar_tensor_tensor(out=mi[:, t], in0=h_t[e][:, buf, t], scalar=ssb[:, 2, t:t + 1],
                                                   in1=nw_post[:], op0=ALU.mult, op1=ALU.mult).then_inc(b_mi[e], 1)

            def turned_b(e, b, buf):
                for t in range(TT):
                    if e == "l":
                        dve.wait_ge(b_mih, b * 2 + (t + 1))
                        cols = slice(t * P, (t + 1) * P)
                        nc.vector.tensor_tensor(miT_parts[1][:, buf, :, cols], chunks(TB[t]), miT_parts[0][:, buf, :, cols],
                                                ALU.subtract).then_inc(b_mit[e], 1)
                        continue
                    dve.wait_ge(b_tr[e], b * 2 + (t + 1))
                    nc.vector.tensor_copy(miT[:, buf, :, t * P:(t + 1) * P], TB[t][:].rearrange("p (c m) -> p c m", c=DC)) \
                        .then_inc(b_mit[e], 1)

            def weights_low(u):
                cols = slice(u * P, u * P + FW[u])
                for i, (lo, w, hi) in enumerate(((up_lo[:, :, :, cols], w_up["l"][:, :, :, cols], up_hi[:, :, :, cols]),
                                                 (dn_lo[0:FW[u], u], w_dn["l"][0:FW[u], u], dn_hi[0:FW[u], u]))):
                    dve.wait_ge(b_wh, u * 2 + (i + 1))
                    nc.vector.tensor_tensor(lo, w, hi, ALU.subtract).then_inc(b_wl, 1)

            def hidden_parts(b, u):
                f = hh_sum[0:FW[u], u % 2]
                nc.vector.tensor_tensor(f, UP[u % UP_N][0:FW[u], S:2 * S], sg[0:FW[u], u % 2], ALU.mult).then_inc(b_sum, 1)
                dve.wait_ge(b_sum, b * FC + (u + 1))
                nc.vector.tensor_scalar(hh_parts[0][0:FW[u], u % 4], f, 0.0, None, ALU.add).then_inc(b_hhh, 1)
                dve.wait_ge(b_hhh, b * FC + (u + 1))
                nc.vector.tensor_tensor(hh_parts[1][0:FW[u], u % 4], f, hh_parts[0][0:FW[u], u % 4], ALU.subtract) \
                    .then_inc(b_hh["l"], 1)

            for e in "vl":
                nc.vector.tensor_scalar(idx_cur[e][:, 0], idx[:, CH * "vl".index(e):CH * "vl".index(e) + TT], 0.0, None,
                                        ALU.add).then_inc(b_idx[e], 1)
                norm_b(e, 0, 0)
                turned_b(e, 0, 0)
                if e == "l":
                    for u in range(FC):
                        weights_low(u)
                for b, j in tiles_of(dve, e):
                    dve.wait_ge(b_st[e], b * 32 + 16)
                    indices(e, b + 1, 1 - j)
                    for u in range(FC):
                        if u == MID:
                            norm_b(e, b + 1, 1 - j)
                        if u == MID + 3:
                            turned_b(e, b + 1, 1 - j)
                        dve.wait_ge(b_sg[e], b * FC + (u + 1))
                        if u >= 4:
                            dve.wait_ge(b_dn[e], b * FC + (u - 3))
                        if e == "l":
                            hidden_parts(b, u)
                            continue
                        nc.vector.tensor_tensor(hh[0:FW[u], u % 4], UP[u % UP_N][0:FW[u], S:2 * S], sg[0:FW[u], u % 2], ALU.mult) \
                            .then_inc(b_hh[e], 1)
                    dve.wait_ge(b_dn[e], b * FC + FC)
                    for t in range(TT):
                        nc.vector.tensor_tensor(o_t[e][:, t], DN[t][:], h_t[e][:, j, t], ALU.add).then_inc(b_out[e], 1)

        @block.tensor
        def _(pe):
            pe.wait_ge(s_id, 11)
            pe.wait_ge(s_ws, 16)
            for e in range(EC):
                for d in range(DC):
                    m = nc.tensor.transpose(ps[f"T{e}"][:, d * P:(d + 1) * P], bufA[:, d, e * P:(e + 1) * P], ident[:])
                m.then_inc(bank_ready[f"T{e}"], 1)
            pe.wait_ge(s_wg, 16)
            for f in range(2 * DC):
                n = f"T{f % 2}"
                pe.wait_ge(bank_free[n], 1 + f // 2)
                for d in range(DC):
                    m = nc.tensor.transpose(ps[n][:, d * P:(d + 1) * P], gate_in[:, d, f * P:(f + 1) * P], ident[:])
                m.then_inc(bank_ready[n], 1)

            pe.wait_ge(r_dve, R_SCAN)
            nc.tensor.matmul(ps["O"][0:B, 0:1], below[:], vm16[:, 2, S - 1:S], start=True, stop=True)
            nc.tensor.matmul(ps["O"][0:1, 1:2], vm16[:, 2, S - 1:S], ones16[:, 0:1], start=True, stop=True).then_inc(r_pe, 1)
            pe.wait_ge(r_dve, R_POS)
            for t in range(TT):
                m = nc.tensor.transpose(ps["O"][:, t * B:(t + 1) * B], vm16[:, 3, t * P:(t + 1) * P], ident[0:B, 0:B])
            m.then_inc(r_pe, 1)
            def transposes(job, b, blocks):
                pe.wait_ge(*vacant(job, b))
                for i, src in enumerate(blocks):
                    m = nc.tensor.transpose(bank(job)[:, i * P:(i + 1) * P], src, ident[:])
                m.then_inc(ready_sem(job), 1)

            def gemm(job, b, dst, pairs, last=True):
                for i, (l, r) in enumerate(pairs):
                    m = nc.tensor.matmul(dst, l, r, start=(i == 0), stop=(i == len(pairs) - 1))
                if last:
                    m.then_inc(ready_sem(job), 1)

            def tiles(x, t, n=DC):
                return [x[:, t, c * P:(c + 1) * P] for c in range(n)]

            def scores(u, b):
                before = {SELF: -1, SELF + 1: -1}.get(u, u - SELF - RING["S"])
                pe.wait_ge(s_p, b * N_UNITS + (max(before, -1) + 1 + S_P0))
                t, heads, w = units[u]
                s = bank(f"s{u}")
                if u >= CROSS and t == 0:
                    pe.wait_ge(*freed(f"x{heads[0] // 2}", b))
                if u < CROSS:
                    nc.tensor.matmul(s[:], identb[:], tri[:, t], start=True, stop=True, skip_group_check=True)
                for j, h in enumerate(heads):
                    if u < CROSS:
                        c, r = h // 4, (h % 4) * 32
                        l, k = qT[r:r + 32, c, t * P:(t + 1) * P], kT[r:r + 32, c, 0:w]
                    else:
                        g = h // 2 % 2
                        l, k = q_pair[:, g, t * P:(t + 1) * P], k_pair[:, g, h % 2]
                    m = nc.tensor.matmul(s[:, j * w:(j + 1) * w], l, k, start=(u >= CROSS), stop=True,
                                         skip_group_check=True)
                m.then_inc(ready_sem(f"s{u}"), 1)

            def turn_pair(g, b):
                job = f"x{g}"
                pe.wait_ge(*vacant(job, b))
                for i, src in enumerate(xq + xk):
                    m = nc.tensor.transpose(bank(job)[:, i * P:(i + 1) * P].bitcast(F32R), src[:, g * P:(g + 1) * P],
                                            ident_r[:])
                m.then_inc(ready_sem(job), 1)

            def turn(u, b):
                pe.wait_ge(*probs(u, b))
                transposes(f"t{u}", b, [p_ring[:, u % 3, i * P:(i + 1) * P] for i in range(4)])

            def values(u, b):
                t, heads, w = units[u]
                cross = u >= CROSS
                o = "o2" if cross else f"o{t}"
                if u in (SELF, SELF + 4, CROSS):
                    pe.wait_ge(*vacant(o, b))
                pe.wait_ge(*freed(f"t{u}", b))
                v, d = (cv_parts, CHD) if cross else (v_parts, HD)
                for j, h in enumerate(heads):
                    col = h * d + (t * E if cross else 0)
                    terms = [(k, *parts) for k in range(w // P) for parts in PARTS]
                    for n, (k, pp, vp) in enumerate(terms):
                        i = j * (w // P) + k
                        m = nc.tensor.matmul(bank(o)[:, col:col + d], pT_ring[:, u % 2, pp, i * P:(i + 1) * P],
                                             v[:, vp, k, h * d:(h + 1) * d], start=(n == 0), stop=(n == len(terms) - 1))
                m.then_inc(s_pv, 1)

            def expert_gemms(t, r, inputs, jobs):
                def products(experts):
                    pe.wait_ge(*freed(inputs, r))
                    for job, w, cols in jobs:
                        pe.wait_ge(*vacant(job, r))
                        gemm(job, r, bank(job)[:], [(buf[:, c, t * P:(t + 1) * P], w[e][:, c, cols])
                                                    for buf, e in ((bufB, "l"), (bufA, "v"))[:experts] for c in range(DC)])

                n = pe.value_load(has_v[0:1, t:t + 1], min_val=0, max_val=1)
                with pe.If(n > 0):
                    products(2)
                with pe.Else():
                    products(1)

            def dense(t, b):
                expert_gemms(t, b, f"aoT{t}", [(f"dense{t}", w_dense, slice(0, D))])

            def turn_inputs(t, b):
                pe.wait_ge(s_ci, b * 2 + (t + 1))
                transposes(f"ciT{t}", b, tiles(xn, t))

            def front(c, r, slot):
                if slot == -3:
                    pe.wait_ge(s_x, c * 48 + 48)
                    transposes("ctT", r, [c_t[:, m, e * P:(e + 1) * P] for e in range(EC) for m in range(TT)])
                if slot == 0:
                    for t in range(TT):
                        transposes(f"xT{t}", r, tiles(x_t, t))
                if slot == -2:
                    pe.wait_ge(*freed("ctT", r))
                    for m in range(TT):
                        pe.wait_ge(*vacant(f"mp{m}", r))
                        gemm(f"mp{m}", r, bank(f"mp{m}")[:], [(ctT[:, e, m * P:(m + 1) * P], w_memT[:, e]) for e in range(EC)])
                if slot == -1:
                    pe.wait_ge(*freed("mp0", r))
                    pe.wait_ge(*freed("mp1", r))
                    for k in range(2):
                        transposes(f"mpT{k}", r, [mp[:, m, (2 * k + d) * P:(2 * k + d + 1) * P] for d in range(2) for m in range(TT)])
                if slot == 1:
                    for job in ("xT0", "xT1", "mpT0", "mpT1"):
                        pe.wait_ge(*freed(job, r))
                    pe.wait_ge(*vacant("l0s", r))
                    for t in range(TT):
                        gemm("l0s", r, bank("l0s")[:, t * S:(t + 1) * S],
                             [(bufA[:, d, t * P:(t + 1) * P], mpT[:, d]) for d in range(DC)], last=(t == TT - 1))
                if slot == 3:
                    pe.wait_ge(*freed("l0s", r))
                    for t in range(TT):
                        transposes(f"pT{t}", r, [p0[:, t, m * P:(m + 1) * P] for m in range(TT)])
                if slot == 4:
                    for t in range(TT):
                        pe.wait_ge(*freed(f"pT{t}", r))
                        pe.wait_ge(*vacant(f"mc{t}", r))
                        gemm(f"mc{t}", r, bank(f"mc{t}")[:], [(p0T[:, t, m * P:(m + 1) * P], mp[:, m]) for m in range(TT)])
                if slot == 5:
                    for t in range(TT):
                        pe.wait_ge(*freed(f"mc{t}", r))
                        transposes(f"mcT{t}", r, tiles(mc, t))
                if slot in (6, 8):
                    t = slot // 8
                    pe.wait_ge(*freed(f"mcT{t}", r))
                    pe.wait_ge(*vacant(f"gate{t}", r))
                    gemm(f"gate{t}", r, bank(f"gate{t}")[:],
                         [((bufA, bufB)[d // DC][:, d % DC, t * P:(t + 1) * P], w_gate[:, d]) for d in range(2 * DC)])
                for t in range(TT):
                    for n, (j, slots_) in enumerate((("q", Q_SLOTS), ("k", K_SLOTS), ("v", V_SLOTS))):
                        if slot == slots_[t]:
                            expert_gemms(t, r, f"xnT{t}", [(f"{j}{t}", w_qkv, slice(n * D, (n + 1) * D))])
                for t in range(TT):
                    if slot == 12 + 2 * t:
                        if t == 0:
                            pe.wait_ge(s_has, c + 1)
                        pe.wait_ge(s_xn, c * 2 + (t + 1))
                        transposes(f"xnT{t}", r, tiles(xf, t))
                if slot == 20:
                    for t in range(TT):
                        for j in range(2):
                            pe.wait_ge(s_rot, c * 4 + (2 * t + j + 1))
                            transposes(f"{'qk'[j]}T{t}", r, [qk[:, t, j, d * P:(d + 1) * P] for d in range(DC)])

            def front_done(c, r):
                for t in range(TT):
                    for j in ("qT", "kT"):
                        pe.wait_ge(*freed(f"{j}{t}", r))
                pe.wait_ge(s_v3, c * 2 + 2)

            def element(b, has_next):
                for i in range(SELF, CROSS + VALUES):
                    if i < CROSS:
                        scores(i, b)
                    if SELF <= i - TURN < CROSS:
                        turn(i - TURN, b)
                    if SELF <= i - VALUES < CROSS:
                        values(i - VALUES, b)
                    if i == 9:
                        pe.wait_ge(*freed("o0", b))
                        transposes("aoT0", b, tiles(ao, 0))
                    if i == 10:
                        dense(0, b)
                    if i == 15:
                        turn_inputs(0, b)
                pe.wait_ge(*freed("o1", b))
                transposes("aoT1", b, tiles(ao, 1))
                pe.wait_ge(*vacant("ck", b))
                for m in range(TT):
                    gemm("ck", b, bank("ck")[:, m * E:(m + 1) * E],
                         [(ctT[:, e, m * P:(m + 1) * P], w_ckv[:, e, 0:E]) for e in range(EC)], last=(m == TT - 1))
                dense(1, b)
                pe.wait_ge(*vacant("cv", b))
                for m in range(TT):
                    gemm("cv", b, bank("cv")[:, m * E:(m + 1) * E],
                         [(ctT[:, e, m * P:(m + 1) * P], w_ckv[:, e, E:2 * E]) for e in range(EC)], last=(m == TT - 1))
                if has_next:
                    front(b + 1, b, -3)
                    front(b + 1, b, -2)
                turn_inputs(1, b)
                if has_next:
                    front(b + 1, b, -1)
                for t in range(TT):
                    pe.wait_ge(*freed(f"ciT{t}", b))
                for t in range(TT):
                    pe.wait_ge(*vacant(f"cq{t}", b))
                    gemm(f"cq{t}", b, bank(f"cq{t}")[:, 0:E], [(ciT[:, k, t * P:(t + 1) * P], w_cq[:, k]) for k in range(DC)])
                if has_next:
                    front(b + 1, b, 0)
                for job in ("cq0", "cq1", "ck"):
                    pe.wait_ge(*freed(job, b))
                turn_pair(0, b)
                pe.wait_ge(s_c3, b + 1)
                for slot in range(SLOTS + 2):
                    i = CROSS + slot
                    if slot < N_CROSS:
                        scores(i, b)
                    if 0 <= slot - TURN < N_CROSS:
                        turn(i - TURN, b)
                    if 0 <= slot - VALUES < N_CROSS:
                        values(i - VALUES, b)
                    if i in PAIR_AHEAD:
                        turn_pair(slot // 2 + 1, b)
                    if has_next and slot > 0:
                        front(b + 1, b, slot)
                    if slot == SLOTS:
                        pe.wait_ge(*freed("o2", b))
                        transposes("ccT", b, [cc[:, t * E + c * P:t * E + (c + 1) * P] for c in range(EC) for t in range(TT)])
                pe.wait_ge(*freed("ccT", b))
                for t in range(TT):
                    pe.wait_ge(*vacant(f"cd{t}", b))
                    gemm(f"cd{t}", b, bank(f"cd{t}")[:],
                         [(ccT[:, c * S + t * P:c * S + (t + 1) * P], w_cd[:, c]) for c in range(EC)])

                if has_next:
                    front_done(b + 1, b)

            for slot in range(-3, SLOTS + 2):
                if slot == Q_SLOTS[0]:
                    pe.wait_ge(s_w, 112)
                front(0, None, slot)
            front_done(0, None)
            with pe.Fori(0, B - 1) as b:
                element(b, True)
            element(B - 1, False)

            def turn_b(e, b, buf):
                for t in range(TT):
                    pe.wait_ge(b_mi[e], b * 2 + (t + 1))
                    for c in range(DC):
                        m = nc.tensor.transpose(TB[t][:, c * P:(c + 1) * P], mi[:, t, c * P:(c + 1) * P], ident[:])
                    m.then_inc(b_tr[e], 1)

            def down(e, b, u):
                pe.wait_ge(b_hh[e], b * FC + (u + 1))
                rows = slice(0, FW[u])
                for t in range(TT):
                    cols = slice(t * P, (t + 1) * P)
                    pairs = [(hh[rows, u % 4, cols], w_dn[e][rows, u])] if e == "v" else \
                            [(hh_parts[x][rows, u % 4, cols], dn_parts[w][rows, u]) for x, w in ((0, 0), (0, 1), (1, 0))]
                    for i, (l, r) in enumerate(pairs):
                        m = nc.tensor.matmul(DN[t][:], l, r, start=(u == 0 and i == 0),
                                             stop=(u == FC - 1 and i == len(pairs) - 1))
                m.then_inc(b_dn[e], 1)

            pe.wait_ge(r_dve, R_SLOTS + 1)
            nc.tensor.transpose(ps["O"][:, 0:2 * CH], list_f, ident[0:2 * CH, 0:2 * CH]).then_inc(r_pe, 1)
            for e in "vl":
                turn_b(e, 0, 0)
                if e == "v":
                    pe.wait_ge(b_w[e], 64)
                for b, j in tiles_of(pe, e):
                    pe.wait_ge(b_mit[e], b * 2 + 2)
                    for u in range(FC + 2):
                        if u == MID + 3:
                            turn_b(e, b + 1, 1 - j)
                        if u < FC:
                            if e == "l":
                                pe.wait_ge(b_wl, 2 * (u + 1))
                            if u >= UP_N:
                                pe.wait_ge(b_hh[e], b * FC + (u - UP_N + 1))
                            cols = slice(u * P, u * P + FW[u])
                            for g in range(2):
                                pairs = [(w_up[e][:, c, g, cols], miT[:, j, c]) for c in range(DC)] if e == "v" else \
                                        [(up_parts[w][:, c, g, cols], miT_parts[x][:, j, c])
                                         for c in range(DC) for w, x in ((0, 0), (0, 1), (1, 0))]
                                for i, (l, r) in enumerate(pairs):
                                    m = nc.tensor.matmul(UP[u % UP_N][0:FW[u], g * S:(g + 1) * S], l, r, start=(i == 0),
                                                         stop=(i == len(pairs) - 1))
                            m.then_inc(b_up[e], 1)
                        if u == 2:
                            pe.wait_ge(b_out[e], b * 2 + 1)
                        if u >= 2:
                            down(e, b, u - 2)


def rotary_table(n):
    inv = (1.0 / 10000.0 ** (np.arange(0, HD, 2, dtype=np.float32) / np.float32(HD))).astype(np.float32)
    f = np.outer(np.arange(n, dtype=np.float32), inv).astype(np.float32)
    return np.concatenate([np.cos(f), np.cos(f), -np.sin(f), np.sin(f)], axis=1).astype(np.float32)


_INS = ["x", "ctx_1024", "pos_1xS", "mask_BxS_ik0", "L0_xattn_W_mem", "L0_xattn_W_gate", "L0_xattn_b_gate",
        "L0_xattn_norm_w", "L1_xattn_ln_in_w", "L1_xattn_ln_post_attn_w", "L1_xattn_ln_post_cross_w",
        "L1_xattn_v_qkv", "L1_xattn_l_qkv", "L1_xattn_v_dense", "L1_xattn_l_dense", "L1_xattn_cq_w",
        "L1_xattn_ckv_w", "L1_xattn_cdense_w", "L1_xattn_v_gate", "L1_xattn_v_up", "L1_xattn_v_down",
        "L1_xattn_l_gate", "L1_xattn_l_up", "L1_xattn_l_down"]


def kernel(**inputs):
    import numpy as _np
    import concourse.bacc as _bacc
    from concourse import mybir as _mybir
    from concourse.bass_utils import run_bass_kernel_spmd as _run

    nc = _bacc.Bacc("TRN2", target_bir_lowering=False, num_devices=1)
    arrays, args = {}, {}
    for name in _INS:
        v = _np.ascontiguousarray(inputs[name])
        arrays[f"in_{name}"] = v
        args[name] = nc.dram_tensor(f"in_{name}", v.shape, _mybir.dt.from_np(v.dtype), kind="ExternalInput").ap()
    table = rotary_table(inputs["x"].shape[1])
    arrays["rotary"] = table
    consts = {"rotary": nc.dram_tensor("rotary", table.shape, _mybir.dt.float32, kind="ExternalInput").ap()}
    shape = inputs["x"].shape
    out = nc.dram_tensor("out_0", shape, _mybir.dt.float32, kind="ExternalOutput").ap()
    h_mid = nc.dram_tensor("h_mid", shape, _mybir.dt.float32, kind="Internal").ap()
    slots = nc.dram_tensor("slots", (2 * shape[0] * shape[1], 1), _mybir.dt.int32, kind="Internal").ap()
    program(nc, args, out, h_mid, slots, consts)
    r = _run(nc, [arrays], core_ids=[0])
    return r.results[0]["out_0"]
```
